# Optimizing a Trainium2 kernel written in Bass

```python
import numpy as np
import jax
import jax.numpy as jnp

def _softmax(x, axis=-1):
    return jax.nn.softmax(x, axis=axis)

def _gelu(x):
    return jax.nn.gelu(x, approximate=True)

def _silu(x):
    return jax.nn.silu(x)

def _sigmoid(x):
    return jax.nn.sigmoid(x)

def _layernorm(x, axis=-1, eps=1e-05):
    m = jnp.mean(x, axis=axis, keepdims=True)
    v = jnp.var(x, axis=axis, keepdims=True)
    return (x - m) / jnp.sqrt(v + eps)

def _scatter_add(tgt, idx, src, axis=0):
    return tgt.at[idx].add(src)

def _segment_sum(src, seg, n):
    return jax.ops.segment_sum(src, seg, n)
kernel_name = 'mk_xattn_ffn_d1_seqx_r4_ba7424'

def setup_inputs(seed: int=0):
    np.random.seed(seed)
    _w = jnp.asarray

    def _rec_inputs():
        import jax
        import jax.numpy as jnp
        _rk = jax.random.key(seed)
        x = 7.22e-05 + 1 * jax.random.normal(jax.random.fold_in(_rk, 1), (1, 2048, 256), jnp.float32)
        _lenS = 2048 - jax.random.randint(jax.random.fold_in(_rk, 7), (1,), 0, max(1, 2048 // 4) + 1, jnp.int32)
        _lenS2 = 1601 - jax.random.randint(jax.random.fold_in(_rk, 8), (1,), 0, max(1, 1601 // 4) + 1, jnp.int32)
        _ctx_1024P = jax.random.normal(jax.random.fold_in(_rk, 11), (1, 16, 256), jnp.float32)
        _ctx_1024c = jax.random.dirichlet(jax.random.fold_in(_rk, 511), 0.3 * jnp.ones((16,), jnp.float32), (1, 1601))
        _ctx_1024t = jnp.einsum('bsk,bkd->bsd', _ctx_1024c, _ctx_1024P)
        _ctx_1024t = _ctx_1024t * jax.lax.rsqrt(jnp.mean(jnp.square(_ctx_1024t)) + 1e-12) * 0.953939
        ctx_1024 = 7.22013e-05 + 1.00017 * (_ctx_1024t + 0.3 * jax.random.normal(jax.random.fold_in(_rk, 611), (1, 1601, 256), jnp.float32))
        return (x, ctx_1024, _lenS2)
    x, ctx_1024, _lenS2 = _rec_inputs()

    def _L0_xattn_setup():
        import jax, jax.numpy as jnp
        import numpy as np
        D_MODEL = 256
        N_HEADS = 16
        D_Q = 64
        D_V = 64
        D_OUT = 256
        B, S = (4, 512)

        def _layer_norm(x, g, b, eps=1e-05):
            mu = jnp.mean(x, axis=-1, keepdims=True)
            var = jnp.mean((x - mu) ** 2, axis=-1, keepdims=True)
            return (x - mu) * jax.lax.rsqrt(var + eps) * g + b

        def _rope(x, theta=10000.0):
            D = x.shape[-1]
            inv_freq = 1.0 / theta ** (jnp.arange(0, D, 2, dtype=jnp.float32) / D)
            t = jnp.arange(x.shape[-2], dtype=jnp.float32)
            freqs = t[:, None] * inv_freq[None, :]
            freqs = jnp.repeat(freqs, 2, axis=-1)
            cos, sin = (jnp.cos(freqs), jnp.sin(freqs))
            x1, x2 = (x[..., 0::2], x[..., 1::2])
            rot = jnp.stack([-x2, x1], axis=-1).reshape(x.shape)
            return x * cos + rot * sin
        key = jax.random.key(seed)
        ks = jax.random.split(key, 10)
        x = jax.random.normal(ks[0], (B, S, D_MODEL), dtype=jnp.float32)
        sc = 1.0 / np.sqrt(D_MODEL)
        return {'query_sequences': x, 'key_sequences': x, 'value_sequences': x, 'key_value_sequence_lengths': jax.random.randint(ks[1], (B,), 1, S + 1), 'ln_g': jnp.ones((D_MODEL,), jnp.float32), 'ln_b': jnp.zeros((D_MODEL,), jnp.float32), 'Wq': jax.random.normal(ks[2], (D_MODEL, N_HEADS * D_Q), jnp.float32) * sc, 'bq': jnp.zeros((N_HEADS * D_Q,), jnp.float32), 'Wk': jax.random.normal(ks[3], (D_MODEL, N_HEADS * D_Q), jnp.float32) * sc, 'bk': jnp.zeros((N_HEADS * D_Q,), jnp.float32), 'Wv': jax.random.normal(ks[4], (D_MODEL, N_HEADS * D_V), jnp.float32) * sc, 'bv': jnp.zeros((N_HEADS * D_V,), jnp.float32), 'Wo': jax.random.normal(ks[5], (N_HEADS * D_V, D_OUT), jnp.float32) * (1.0 / np.sqrt(N_HEADS * D_V)), 'bo': jnp.zeros((D_OUT,), jnp.float32)}
    _L0_xattn_all = _L0_xattn_setup()
    _L0_xattn_in = {k: v for k, v in _L0_xattn_all.items() if k in ('ln_g', 'ln_b', 'Wq', 'bq', 'Wk', 'bk', 'Wv', 'bv', 'Wo', 'bo')}
    del _L0_xattn_all

    def _L0_ffn_setup():
        import jax, jax.numpy as jnp
        import numpy as np
        DIM = 256
        N_EXPERTS = 8
        D_FF = 512
        TOP_K = 2
        key = jax.random.key(seed)
        ks = jax.random.split(key, 5)
        s = 0.02
        return {'x': jax.random.normal(ks[0], (2, 512, DIM), dtype=jnp.float32), 'gate_w': jax.random.normal(ks[1], (N_EXPERTS, DIM), dtype=jnp.float32) * s, 'w1': jax.random.normal(ks[2], (N_EXPERTS, D_FF, DIM), dtype=jnp.float32) * s, 'w2': jax.random.normal(ks[3], (N_EXPERTS, DIM, D_FF), dtype=jnp.float32) * s, 'w3': jax.random.normal(ks[4], (N_EXPERTS, D_FF, DIM), dtype=jnp.float32) * s}
    _L0_ffn_all = _L0_ffn_setup()
    _L0_ffn_in = {k: v for k, v in _L0_ffn_all.items() if k in ('gate_w', 'w1', 'w2', 'w3')}
    del _L0_ffn_all
    return {'x': x, 'ctx_1024': ctx_1024, '_lenS2': _lenS2, 'L0_xattn_ln_g': _L0_xattn_in['ln_g'], 'L0_xattn_ln_b': _L0_xattn_in['ln_b'], 'L0_xattn_Wq': _L0_xattn_in['Wq'], 'L0_xattn_bq': _L0_xattn_in['bq'], 'L0_xattn_Wk': _L0_xattn_in['Wk'], 'L0_xattn_bk': _L0_xattn_in['bk'], 'L0_xattn_Wv': _L0_xattn_in['Wv'], 'L0_xattn_bv': _L0_xattn_in['bv'], 'L0_xattn_Wo': _L0_xattn_in['Wo'], 'L0_xattn_bo': _L0_xattn_in['bo'], 'L0_ffn_gate_w': _L0_ffn_in['gate_w'], 'L0_ffn_w1': _L0_ffn_in['w1'], 'L0_ffn_w2': _L0_ffn_in['w2'], 'L0_ffn_w3': _L0_ffn_in['w3']}

def reference(x, ctx_1024, _lenS2, L0_xattn_ln_g, L0_xattn_ln_b, L0_xattn_Wq, L0_xattn_bq, L0_xattn_Wk, L0_xattn_bk, L0_xattn_Wv, L0_xattn_bv, L0_xattn_Wo, L0_xattn_bo, L0_ffn_gate_w, L0_ffn_w1, L0_ffn_w2, L0_ffn_w3):
    import jax
    import jax.numpy as jnp

    def _L0_xattn_ref(query_sequences, key_sequences, value_sequences, key_value_sequence_lengths, ln_g, ln_b, Wq, bq, Wk, bk, Wv, bv, Wo, bo):
        import jax, jax.numpy as jnp
        import numpy as np
        D_MODEL = 256
        N_HEADS = 16
        D_Q = 64
        D_V = 64
        D_OUT = 256
        B, S = (4, 512)

        def _layer_norm(x, g, b, eps=1e-05):
            mu = jnp.mean(x, axis=-1, keepdims=True)
            var = jnp.mean((x - mu) ** 2, axis=-1, keepdims=True)
            return (x - mu) * jax.lax.rsqrt(var + eps) * g + b

        def _rope(x, theta=10000.0):
            D = x.shape[-1]
            inv_freq = 1.0 / theta ** (jnp.arange(0, D, 2, dtype=jnp.float32) / D)
            t = jnp.arange(x.shape[-2], dtype=jnp.float32)
            freqs = t[:, None] * inv_freq[None, :]
            freqs = jnp.repeat(freqs, 2, axis=-1)
            cos, sin = (jnp.cos(freqs), jnp.sin(freqs))
            x1, x2 = (x[..., 0::2], x[..., 1::2])
            rot = jnp.stack([-x2, x1], axis=-1).reshape(x.shape)
            return x * cos + rot * sin
        b, sq, _ = query_sequences.shape
        sk = key_sequences.shape[1]
        q_in = _layer_norm(query_sequences, ln_g, ln_b)
        k_in = _layer_norm(key_sequences, ln_g, ln_b)
        v_in = _layer_norm(value_sequences, ln_g, ln_b)
        q = (q_in @ Wq + bq).reshape(b, sq, N_HEADS, D_Q).transpose(0, 2, 1, 3)
        k = (k_in @ Wk + bk).reshape(b, sk, N_HEADS, D_Q).transpose(0, 2, 1, 3)
        v = (v_in @ Wv + bv).reshape(b, sk, N_HEADS, D_V).transpose(0, 2, 1, 3)
        q = _rope(q)
        k = _rope(k)
        scores = jnp.einsum('bhqd,bhkd->bhqk', q, k) * (1.0 / np.sqrt(D_Q))
        valid = jnp.arange(sk)[None, :] < key_value_sequence_lengths[:, None]
        scores = jnp.where(valid[:, None, None, :], scores, -jnp.inf)
        attn = jax.nn.softmax(scores, axis=-1)
        out = jnp.einsum('bhqk,bhkd->bhqd', attn, v)
        out = out.transpose(0, 2, 1, 3).reshape(b, sq, N_HEADS * D_V)
        return out @ Wo + bo

    def _L0_ffn_ref(x, gate_w, w1, w2, w3):
        import jax, jax.numpy as jnp
        import numpy as np
        DIM = 256
        N_EXPERTS = 8
        D_FF = 512
        TOP_K = 2
        orig_shape = x.shape
        xf = x.reshape(-1, orig_shape[-1])
        scores = jnp.einsum('td,ed->te', xf, gate_w)
        probs = jax.nn.softmax(scores.astype(jnp.float32), axis=-1)
        weights, idx = jax.lax.top_k(probs, TOP_K)
        weights = weights / jnp.sum(weights, axis=-1, keepdims=True)
        weights = weights.astype(x.dtype)
        x1 = jax.nn.silu(jnp.einsum('td,efd->tef', xf, w1))
        x3 = jnp.einsum('td,efd->tef', xf, w3)
        out_all = jnp.einsum('tef,edf->ted', x1 * x3, w2)
        expert_outs = jnp.take_along_axis(out_all, idx[:, :, None], axis=1)
        result = jnp.einsum('tkd,tk->td', expert_outs, weights)
        return result.reshape(orig_shape)
    x = x + _L0_xattn_ref(_layernorm(x, axis=-1), ctx_1024, ctx_1024, _lenS2, L0_xattn_ln_g, L0_xattn_ln_b, L0_xattn_Wq, L0_xattn_bq, L0_xattn_Wk, L0_xattn_bk, L0_xattn_Wv, L0_xattn_bv, L0_xattn_Wo, L0_xattn_bo)
    x = x + _L0_ffn_ref(_layernorm(x, axis=-1), L0_ffn_gate_w, L0_ffn_w1, L0_ffn_w2, L0_ffn_w3)
    return x

_drawn_inputs = setup_inputs


def setup_inputs(seed=0):
    import zlib

    import numpy as np

    out = dict(_drawn_inputs(seed))
    spreads = {'L0_xattn_ln_g': (1.0, 0.2),
     'L0_xattn_ln_b': (0.0, 0.1),
     'L0_xattn_bq': (0.0, 0.797),
     'L0_xattn_bk': (0.0, 0.8),
     'L0_xattn_bv': (0.0, 0.1),
     'L0_xattn_bo': (0.0, 0.1)}
    factors = {'L0_ffn_gate_w': 4.471, 'L0_ffn_w1': 3.906, 'L0_ffn_w2': 3.883, 'L0_ffn_w3': 3.861}
    for name, (base, spread) in spreads.items():
        noise = np.random.default_rng([zlib.crc32(name.encode()), seed]).standard_normal(out[name].shape)
        drawn = base * np.exp(spread * noise) if base else spread * noise
        out[name] = jnp.asarray(drawn.astype(out[name].dtype))
    for name, factor in factors.items():
        out[name] = (out[name] * factor).astype(out[name].dtype)
    return out
```

```python
from contextlib import ExitStack

import concourse.bass as bass
from concourse import mybir

P = 128
F32 = mybir.dt.float32
BF16 = mybir.dt.bfloat16
I32 = mybir.dt.int32
ALU = mybir.AluOpType
ACT = mybir.ActivationFunctionType
AX_X = mybir.AxisListType.X

S, D, H, HD = 2048, 256, 16, 64
L = 1601
E, FF = 8, 512
EPS = 1e-5
DT = D // P
KT = -(-L // P)
LP = KT * P
ST = S // P
PAIRS = H // 2
QC = 512
CH = S // QC
QT = QC // P
KC = LP // 4
HALF = 2 * 401
VW = 2 * HD + 1
BLOCKS = 2 * CH
GROUPS = 7
GSIZE = [2] * 6 + [1]
LAG = 2
POOL_GROUPS = (1, 4)
DVE_GROUPS = tuple(m for m in range(GROUPS) if m not in POOL_GROUPS)
PRING = 4
QK_UNITS, V_UNITS = 8, 4
UNITS = QK_UNITS + V_UNITS
FT = FF // P


def hook_slot(k):
    return GROUPS * (1 + k // 2) + (3, 5)[k % 2]


def need(eng, sem, index, per, count, least=0):
    if isinstance(index, int):
        if per * index + count > 0:
            eng.wait_ge(sem, per * index + count)
    else:
        assert per * least + count > 0
        eng.wait_ge(sem, index * per + count)


def hi_half(ap):
    return ap.bitcast(BF16)


def build(nc, x, ctx_in, length, g, b, w_pairs, b_pairs, bv_pairs, wo, bo, gate, w_exp, rope, keypos, consts, out):
    o_dram = nc.dram_tensor("attention_out", [S, H * HD], F32, kind="Internal").ap()

    with ExitStack() as whole:
        def sem(name):
            return whole.enter_context(nc.semaphore(name))

        def maker(stack):
            def sb(name, shape, dt=F32):
                return stack.enter_context(nc.sbuf_tensor(name, shape, dt))

            def pb(name, shape, dt=F32):
                return stack.enter_context(nc.psum_tensor(name, shape, dt))
            return sb, pb

        sb, _ = maker(whole)
        cst = sb("cst", [P, P + KT + 8])
        ident_b = sb("ident_b", [P, P], BF16)
        eps_col = sb("eps_col", [P, 1])
        ident = cst[:, 0:P]
        rank8 = cst[:, P + KT:P + KT + 8]

        with ExitStack() as upto_attend:
            sb, _ = maker(upto_attend)
            XH = sb("XH", [P, DT, S], BF16)
            XL = sb("XL", [P, DT, S], BF16)
            CHI = sb("CHI", [P, DT, LP], BF16)
            CLO = sb("CLO", [P, DT, LP], BF16)
            ropeq = sb("ropeq", [P, 2, S])
            ropek = sb("ropek", [P, 2, LP])
            invalid = sb("invalid", [P, LP], BF16)
            validc = sb("validc", [P, KT])
            prepare(nc, sem, maker, locals())
            attend(nc, sem, maker, locals())
        experts(nc, sem, maker, locals())


def prepare(nc, sem, maker, have):
    x, ctx_in, length, g, b = (have[k] for k in ("x", "ctx_in", "length", "g", "b"))
    rope, keypos, consts, cst = (have[k] for k in ("rope", "keypos", "consts", "cst"))
    XH, XL, CHI, CLO, ropeq, ropek, invalid, validc, ident_b, eps_col, ident = (have[k] for k in (
        "XH", "XL", "CHI", "CLO", "ropeq", "ropek", "invalid", "validc", "ident_b", "eps_col", "ident"))
    NT = KT + ST
    with ExitStack() as ctx:
        sb, pb = maker(ctx)
        Z = sb("Z", [P, NT, D])
        keyb = sb("keyb", [P, LP])
        valid = sb("valid", [P, LP])
        len_i = sb("len_i", [P, 1], I32)
        len_f = sb("len_f", [P, 1])
        gb = sb("gb", [P, 2, DT])
        stats = sb("stats", [P, NT, 6])
        mv = sb("mv", [P, 2, NT, 2])
        std = sb("std", [P, 2, NT])
        rstd = sb("rstd", [P, 2, NT])
        NB = 4
        T32 = sb("T32", [P, 2, 512])
        tp = [pb(f"tp{i}", [P, 4, P]) for i in range(NB)]

        ctx_loaded = sem("ctx_loaded")
        x_loaded = sem("x_loaded")
        small_loaded = sem("small_loaded")
        rope_loaded = sem("rope_loaded")
        tail_clear = sem("tail_clear")
        consts_made = sem("consts_made")
        stats_made = sem("stats_made")
        moments = sem("moments")
        std_made = sem("std_made")
        rstd_made = sem("rstd_made")
        normed = sem("normed")
        valid_made = sem("valid_made")
        len_made = sem("len_made")
        table_made = sem("table_made")
        turned = sem("turned")
        scaled = sem("scaled")
        hi_made = sem("hi_made")
        lo_made = sem("lo_made")

        turns = [(CHI, CLO, d, t, min(4, KT - t), 0) for t in range(0, KT, 4) for d in range(DT)]
        turns += [(XH, XL, d, t, min(4, ST - t), KT) for t in range(0, ST, 4) for d in range(DT)]

        with nc.Block() as block:
            @block.sync
            def _(sp):
                full = (L // P) * P
                sp.dma_start(Z[:, 0:L // P, :], ctx_in[0, 0:full, :].rearrange("(t p) d -> p t d", p=P)).then_inc(ctx_loaded, 16)
                sp.wait_ge(tail_clear, 1)
                sp.dma_start(Z[0:L - full, KT - 1, :], ctx_in[0, full:L, :]).then_inc(ctx_loaded, 16)
                sp.dma_start(Z[:, KT:NT, :], x[0].rearrange("(t p) d -> p t d", p=P)).then_inc(x_loaded, 16)
                sp.dma_start(ropeq[:], rope.rearrange("c p s -> p c s")).then_inc(rope_loaded, 16)

            @block.scalar
            def _(act):
                act.dma_start(cst[:], consts).then_inc(small_loaded, 16)
                act.dma_start(len_i[:], length.partition_broadcast(P)).then_inc(small_loaded, 16)
                act.dma_start(gb[:, 0, :], g.rearrange("(c p) -> p c", p=P), allow_slow_non_contiguous=True).then_inc(small_loaded, 16)
                act.dma_start(gb[:, 1, :], b.rearrange("(c p) -> p c", p=P), allow_slow_non_contiguous=True).then_inc(small_loaded, 16)
                act.dma_start(keyb[:], keypos.partition_broadcast(P)).then_inc(small_loaded, 16)
                act.wait_ge(consts_made, 1)
                for r, (a, z) in enumerate(((0, NT), (KT, NT))):
                    act.wait_ge(moments, r + 1)
                    act.activation(std[:, r, a:z], mv[:, r, a:z, 1], ACT.Sqrt, bias=eps_col[:]).then_inc(std_made, 1)
                act.wait_ge(small_loaded, 80)
                for n, (hi, lo, d, t, k, at) in enumerate(turns):
                    act.wait_ge(turned, n + 1)
                    if n >= 2:
                        act.wait_ge(lo_made, n - 1)
                    act.activation(T32[:, n % 2, 0:k * P], tp[n % NB][:, 0:k, :], ACT.Identity,
                                   scale=gb[:, 0, d:d + 1], bias=gb[:, 1, d:d + 1]).then_inc(scaled, 1)
                    act.wait_ge(scaled, n + 1)
                    act.activation(hi[:, d, t * P:(t + k) * P], T32[:, n % 2, 0:k * P], ACT.Copy).then_inc(hi_made, 1)

            @block.vector
            def _(dve):
                dve.memset(Z[:, KT - 1, :], 0.0).then_inc(tail_clear, 1)
                dve.memset(eps_col[:], EPS).then_inc(consts_made, 1)
                dve.wait_ge(small_loaded, 80)
                dve.tensor_copy(ident_b[:], ident)
                dve.tensor_copy(len_f[:], len_i[:]).then_inc(len_made, 1)
                dve.wait_ge(len_made, 1)
                dve.tensor_scalar(valid[:], keyb[:], len_f[:, 0:1], None, ALU.is_lt).then_inc(valid_made, 1)
                dve.tensor_scalar(invalid[:], keyb[:], len_f[:, 0:1], None, ALU.is_ge)
                dve.tensor_scalar(validc[:], cst[:, P:P + KT], len_f[:, 0:1], None, ALU.is_lt)
                for r, (a, z) in enumerate(((0, NT), (KT, NT))):
                    if r == 0:
                        dve.wait_ge(ctx_loaded, 32)
                        dve.wait_ge(x_loaded, 16)
                    else:
                        dve.wait_ge(normed, 1)
                    for t in range(a, z):
                        ins = dve.bn_stats(stats[:, t, :], Z[:, t, :])
                    ins.then_inc(stats_made, 1)
                    dve.wait_ge(stats_made, r + 1)
                    for t in range(a, z):
                        ins = dve.bn_aggr(mv[:, r, t, :], stats[:, t, :])
                    ins.then_inc(moments, 1)
                    dve.wait_ge(std_made, r + 1)
                    dve.reciprocal(rstd[:, r, a:z], std[:, r, a:z]).then_inc(rstd_made, 1)
                    dve.wait_ge(rstd_made, r + 1)
                    for t in range(a, z):
                        ins = dve.tensor_scalar(Z[:, t, :], Z[:, t, :], mv[:, r, t, 0:1], rstd[:, r, t:t + 1],
                                                ALU.subtract, ALU.mult)
                    ins.then_inc(normed, 1)
                for n, (hi, lo, d, t, k, at) in enumerate(turns):
                    dve.wait_ge(hi_made, n + 1)
                    dve.tensor_tensor(lo[:, d, t * P:(t + k) * P], T32[:, n % 2, 0:k * P],
                                      hi[:, d, t * P:(t + k) * P], ALU.subtract).then_inc(lo_made, 1)

            @block.gpsimd
            def _(pool):
                pool.wait_ge(valid_made, 1)
                pool.wait_ge(rope_loaded, 16)
                for c in range(2):
                    pool.tensor_tensor(ropek[:, c, :], ropeq[:, c, 0:LP], valid[:], ALU.mult)

            @block.tensor
            def _(pe):
                pe.wait_ge(small_loaded, 80)
                pe.wait_ge(normed, 1)
                for n, (hi, lo, d, t, k, at) in enumerate(turns):
                    if at and turns[n - 1][5] == 0:
                        pe.wait_ge(normed, 2)
                    if n >= NB:
                        pe.wait_ge(scaled, n - NB + 1)
                    for j in range(k):
                        ins = pe.transpose(tp[n % NB][:, j, :], Z[:, at + t + j, d * P:(d + 1) * P], ident)
                    ins.then_inc(turned, 1)


def attend(nc, sem, maker, have):
    XH, XL, CHI, CLO, ropeq, ropek, invalid, validc, ident_b = (have[k] for k in (
        "XH", "XL", "CHI", "CLO", "ropeq", "ropek", "invalid", "validc", "ident_b"))
    w_pairs, b_pairs, bv_pairs, o_dram = (have[k] for k in ("w_pairs", "b_pairs", "bv_pairs", "o_dram"))
    with ExitStack() as ctx:
        sb, pb = maker(ctx)
        Q1 = [sb(f"Q1_{a}", [P, S], BF16) for a in range(2)]
        Q2 = [sb(f"Q2_{a}", [HD + 1, S], BF16) for a in range(2)]
        K1 = [sb(f"K1_{a}", [P, LP], BF16) for a in range(2)]
        K2 = [sb(f"K2_{a}", [HD + 1, LP], BF16) for a in range(2)]
        VV = [sb(f"VV_{a}", [P, KT, VW], BF16) for a in range(2)]
        next_hi = [sb("next_q_hi", [P, S], BF16), sb("next_k_hi", [P, LP], BF16)]
        next_lo = [sb("next_q_lo", [P, S], BF16), sb("next_k_lo", [P, LP], BF16)]
        next_v = sb("next_v", [P, 2, KT, VW], BF16)
        w32 = sb("w32", [P, 3, DT, P])
        w_hi = sb("w_hi", [P, 3, DT, P], BF16)
        w_lo = sb("w_lo", [P, 3, DT, P], BF16)
        bqk = sb("bqk", [P, 2])
        bvb = sb("bvb", [P, P])
        q32 = sb("q32", [P, 2, QC])
        q32s = sb("q32s", [P, 2, QC])
        by_cos = sb("by_cos", [P, QC])
        by_sin = sb("by_sin", [P, QC])
        turned_raw = sb("turned_raw", [P, QC])
        turned = sb("turned", [P, 2, QC])
        key0 = sb("key0", [P, 1])
        v32 = sb("v32", [P, 4, P])
        v32m = sb("v32m", [P, 4, P])
        prob = sb("prob", [P, PRING, 2, QC])
        prob_lo = sb("prob_lo", [P, PRING, 2, QC], BF16)
        half_max = sb("half_max", [P, 2, QT, 2])
        max_col = sb("max_col", [P, QT], BF16)
        o_raw = sb("o_raw", [P, 2, QT, VW])
        rden = sb("rden", [P, 2, QT])
        o_sum = sb("o_sum", [P, QT, HD])
        o_out = sb("o_out", [P, 2, QT, HD])

        sc = [pb(f"sc{i}", [P, QC]) for i in range(2)]
        pv = pb("pv", [P, 2, 512])
        mx = pb("mx", [P, 2, 512])
        mt = pb("mt", [P, 512])
        pj = pb("pj", [P, 512])

        w_loaded = sem("w_loaded")
        w_hi_made, w_lo_made = sem("w_hi_made"), sem("w_lo_made")
        pj_ready = sem("pj_ready")
        pj_read_act, pj_read_dve = sem("pj_read_act"), sem("pj_read_dve")
        swapped = [sem("swapped0"), sem("swapped1")]
        cos_done, sin_done, raw_done, turn_done = sem("cos_done"), sem("sin_done"), sem("raw_done"), sem("turn_done")
        key0_made = sem("key0_made")
        qk_hi_made, qk_lo_made = sem("qk_hi_made"), sem("qk_lo_made")
        v_biased, v_masked, v_hi_made, v_lo_made = sem("v_biased"), sem("v_masked"), sem("v_hi_made"), sem("v_lo_made")
        q_loaded = [sem("q_loaded0"), sem("q_loaded1")]
        k_loaded = [sem("k_loaded0"), sem("k_loaded1")]
        v_loaded = [sem("v_loaded0"), sem("v_loaded1")]
        ones_made = sem("ones_made")
        scores_ready = sem("scores_ready")
        exp_done = sem("exp_done")
        lo_dve, lo_pool = sem("lo_dve"), sem("lo_pool")
        pv_done = sem("pv_done")
        half_ready = sem("half_ready")
        half_read = sem("half_read")
        max_made, col_made, row_ready, row_made = sem("max_made"), sem("col_made"), sem("row_ready"), sem("row_made")
        o_copied = sem("o_copied")
        rden_made = sem("rden_made")
        o_summed = sem("o_summed")
        o_made = sem("o_made")
        o_stored = [sem("o_stored0"), sem("o_stored1")]

        per_dve, per_pool = len(DVE_GROUPS), len(POOL_GROUPS)

        def tiles_of(s):
            i, m = divmod(s, GROUPS)
            return [(KT * i + 2 * m + j, 2 * m + j) for j in range(GSIZE[m])]

        def halves_of(s):
            i, m = divmod(s, GROUPS)
            block_, hs = (i + 1, [3 + m]) if m < 5 else (i + 2, [[0], [1, 2]][m - 5])
            return [(block_, h // 2, h % 2) for h in hs]

        def set_of(block_):
            return block_ // CH % 2, block_ % CH

        def v_tiles(v):
            return range(4 * v, min(4 * v + 4, KT))

        def body(program, loop_engine):
            with loop_engine.Fori(0, PAIRS - 1) as p:
                program(p, False)
            program(PAIRS - 1, True)

        def unit_block(u):
            kind, c = divmod(u, 4)
            n = (QC, KC)[kind]
            return kind, slice(c * n, (c + 1) * n), n

        with nc.Block() as block:
            @block.tensor
            def _(pe):
                def project(pair, u, least=0):
                    if u == 0:
                        need(pe, w_hi_made, pair, 1, 1, least)
                        need(pe, w_lo_made, pair, 1, 1, least)
                        need(pe, pj_read_dve, pair, V_UNITS, 0, least)
                    elif u <= QK_UNITS:
                        need(pe, pj_read_act, pair, QK_UNITS, u, least)
                    else:
                        need(pe, pj_read_dve, pair, V_UNITS, u - QK_UNITS, least)
                    if u < QK_UNITS:
                        kind, cols, n = unit_block(u)
                        hi, lo = ((XH, XL), (CHI, CLO))[kind]
                        steps = [(w, z, d) for d in range(DT) for w, z in ((w_hi, hi), (w_hi, lo), (w_lo, hi))]
                        for j, (w, z, d) in enumerate(steps):
                            ins = pe.matmul(pj[:, 0:n], w[:, kind, d, :], z[:, d, cols], start=j == 0, stop=j == len(steps) - 1)
                    else:
                        for k, t in enumerate(v_tiles(u - QK_UNITS)):
                            steps = [(z, w, d) for d in range(DT) for z, w in ((CHI, w_hi), (CHI, w_lo), (CLO, w_hi))]
                            for j, (z, w, d) in enumerate(steps):
                                ins = pe.matmul(pj[:, k * P:(k + 1) * P], z[:, d, t * P:(t + 1) * P], w[:, 2, d, :],
                                                start=j == 0, stop=j == len(steps) - 1)
                    ins.then_inc(pj_ready, 1)

                def scores(p, s):
                    i, m = divmod(s, GROUPS)
                    a, c = set_of(i)
                    q = slice(c * QC, (c + 1) * QC)
                    if m == 0:
                        need(pe, row_made, p, BLOCKS, i + 1)
                    for n, t in tiles_of(s):
                        k = slice(t * P, (t + 1) * P)
                        need(pe, exp_done, p, BLOCKS * KT, n + 1)
                        pe.matmul(sc[n % 2][:], K1[a][:, k], Q1[a][:, q], start=True, stop=False)
                        pe.matmul(sc[n % 2][:], K2[a][:, k], Q2[a][:, q], start=False, stop=True).then_inc(scores_ready, 1)

                def half(p, b_, qt, h):
                    a, c = set_of(b_)
                    if c == 0 and qt == 0 and h == 0:
                        need(pe, q_loaded[a], p, 48, 48 * (1 + b_ // BLOCKS))
                        need(pe, k_loaded[a], p, 48, 48 * (1 + b_ // BLOCKS))
                    need(pe, half_read, p, BLOCKS * 2 * QT, 2 * QT * b_ + 2 * qt + h + 1)
                    for j in range(2):
                        k0 = h * HALF + j * HALF // 2
                        ins = pe.matmul(mx[:, j, 0:HALF // 2], Q1[a][:, c * QC + qt * P:c * QC + (qt + 1) * P],
                                        K1[a][:, k0:k0 + HALF // 2], start=True, stop=True)
                    ins.then_inc(half_ready, 1)

                def max_row(p, b_):
                    need(pe, col_made, p, BLOCKS, b_ + 1)
                    need(pe, row_made, p, BLOCKS, b_)
                    for qt in range(QT):
                        ins = pe.matmul(mt[0:1, qt * P:(qt + 1) * P], max_col[:, qt:qt + 1], ident_b[:], start=True, stop=True)
                    ins.then_inc(row_ready, 1)

                def times_v(p, s):
                    i, m = divmod(s, GROUPS)
                    a, _ = set_of(i)
                    if s in (0, GROUPS * CH):
                        need(pe, v_loaded[a], p, 16, 16)
                    if m == 0:
                        need(pe, o_copied, p, BLOCKS, i + 1)
                    if m in DVE_GROUPS:
                        need(pe, lo_dve, p, BLOCKS * per_dve, i * per_dve + DVE_GROUPS.index(m) + 1)
                    else:
                        need(pe, lo_pool, p, BLOCKS * per_pool, i * per_pool + POOL_GROUPS.index(m) + 1)
                    for j, (n, t) in enumerate(tiles_of(s)):
                        hi = hi_half(prob[:, s % PRING, j, :])
                        for qt in range(QT):
                            at = (qt % 2) * VW
                            pe.matmul(pv[:, qt // 2, at:at + VW], hi[:, 2 * qt * P + 1:2 * (qt + 1) * P:2], VV[a][:, t, :],
                                      start=t == 0 and qt % 2 == 0, stop=False, skip_group_check=True)
                            ins = pe.matmul(pv[:, qt // 2, at + HD:at + VW], prob_lo[:, s % PRING, j, qt * P:(qt + 1) * P],
                                            VV[a][:, t, HD:VW], start=False, stop=t == KT - 1, skip_group_check=True)
                    ins.then_inc(pv_done, 1)

                def slot(p, s, last):
                    if not (last and s >= BLOCKS * GROUPS):
                        scores(p, s)
                    if s >= LAG:
                        times_v(p, s - LAG)
                    for b_, qt, h in halves_of(s):
                        if not (last and b_ >= BLOCKS):
                            half(p, b_, qt, h)
                    if s % GROUPS == 5 and not (last and s // GROUPS + 1 >= BLOCKS):
                        max_row(p, s // GROUPS + 1)

                def pair(p, last):
                    for s in range(LAG, BLOCKS * GROUPS + LAG):
                        slot(p, s, last)
                        for u in range(UNITS):
                            if not last and s == hook_slot(u):
                                project(p + 1, u, 1)

                pe.sem_inc(pv_done, PRING)
                for u in range(UNITS):
                    project(0, u)
                pe.wait_ge(ones_made, 2)
                for qt in range(QT):
                    for h in range(2):
                        half(0, 0, qt, h)
                max_row(0, 0)
                for h in range(3):
                    half(0, 1, h // 2, h % 2)
                for s in range(LAG):
                    slot(0, s, False)
                body(pair, pe)

            @block.scalar
            def _(act):
                def split_weights(pair, least=0):
                    need(act, w_loaded, pair, 48, 48, least)
                    need(act, pj_ready, pair, UNITS, 0, least)
                    act.activation(w_hi[:], w32[:], ACT.Copy).then_inc(w_hi_made, 1)

                def evacuate(pair, u, least=0):
                    kind, cols, n = unit_block(u)
                    need(act, pj_ready, pair, UNITS, u + 1, least)
                    need(act, swapped[u % 2], pair, 64 * 4, 64 * (u // 2), least)
                    need(act, turn_done, pair, QK_UNITS, u - 1, least)
                    act.activation(q32[:, u % 2, 0:n], pj[:, 0:n], ACT.Identity,
                                   bias=bqk[:, kind:kind + 1]).then_inc(pj_read_act, 1)

                def qk_hi(pair, u, least=0):
                    kind, cols, n = unit_block(u)
                    need(act, turn_done, pair, QK_UNITS, u + 1, least)
                    if u in (0, 4):
                        for a in range(2):
                            need(act, (q_loaded, k_loaded)[kind][a], pair, 48, 0, least)
                    act.activation(next_hi[kind][:, cols], turned[:, u % 2, 0:n], ACT.Copy).then_inc(qk_hi_made, 1)

                def v_hi(pair, v, least=0):
                    ts = v_tiles(v)
                    need(act, v_masked, pair, V_UNITS, v + 1, least)
                    if v == 0:
                        for a in range(2):
                            need(act, v_loaded[a], pair, 16, 0, least)
                    for a in range(2):
                        ins = act.activation(next_v[:, a, ts[0]:ts[-1] + 1, HD:2 * HD], v32m[:, 0:len(ts), a * HD:(a + 1) * HD], ACT.Copy)
                    ins.then_inc(v_hi_made, 1)

                def hooks(pair, k, least=0):
                    if 0 <= k - 2 < QK_UNITS:
                        qk_hi(pair, k - 2, least)
                    if 0 <= k - 1 - QK_UNITS < V_UNITS:
                        v_hi(pair, k - 1 - QK_UNITS, least)
                    if k < QK_UNITS:
                        evacuate(pair, k, least)

                def exps(p, s):
                    need(act, pv_done, p, BLOCKS * GROUPS, s + 1)
                    for j, (n, t) in enumerate(tiles_of(s)):
                        need(act, scores_ready, p, BLOCKS * KT, n + 1)
                        act.activation(prob[:, s % PRING, j, :], sc[n % 2][:], ACT.Exp, scale=HD ** -0.5).then_inc(exp_done, 1)

                def copy_out(p, i):
                    need(act, pv_done, p, BLOCKS * GROUPS, GROUPS * (i + 1) + PRING)
                    need(act, o_made, p, BLOCKS, i + 1)
                    act.activation(o_raw[:, i % 2, :, :].rearrange("p (b t) v -> p b t v", b=2),
                                   pv[:, :, 0:2 * VW].rearrange("p b (t v) -> p b t v", t=2), ACT.Copy).then_inc(o_copied, 1)

                def max_row(p, b_):
                    a, c = set_of(b_)
                    need(act, row_ready, p, BLOCKS, b_ + 1)
                    act.activation(Q2[a][HD:HD + 1, c * QC:(c + 1) * QC], mt[0:1, :], ACT.Copy, scale=-1.0).then_inc(row_made, 1)

                def slot(p, s, last):
                    i, m = divmod(s, GROUPS)
                    if not (last and s >= BLOCKS * GROUPS):
                        exps(p, s)
                    if m == 1 and s > GROUPS:
                        copy_out(p, i - 1)
                    if m == 5 and not (last and i + 1 >= BLOCKS):
                        max_row(p, i + 1)

                def pair(p, last):
                    for s in range(LAG, BLOCKS * GROUPS + LAG):
                        slot(p, s, last)
                        if not last:
                            if s == 4:
                                split_weights(p + 1, 1)
                            for k in range(UNITS + 2):
                                if s == hook_slot(k):
                                    hooks(p + 1, k, 1)

                act.sem_inc(exp_done, 2)
                act.sem_inc(o_copied, 1)
                split_weights(0)
                for k in range(UNITS + 2):
                    hooks(0, k)
                max_row(0, 0)
                for s in range(LAG):
                    slot(0, s, False)
                body(pair, act)

            @block.vector
            def _(dve):
                def cosines(pair, u, least=0):
                    kind, cols, n = unit_block(u)
                    need(dve, pj_read_act, pair, QK_UNITS, u + 1, least)
                    dve.tensor_tensor(by_cos[:, 0:n], q32[:, u % 2, 0:n], (ropeq, ropek)[kind][:, 0, cols], ALU.mult).then_inc(cos_done, 1)

                def turn(pair, u, least=0):
                    kind, cols, n = unit_block(u)
                    need(dve, cos_done, pair, QK_UNITS, u + 1, least)
                    need(dve, sin_done, pair, QK_UNITS, u + 1, least)
                    need(dve, qk_lo_made, pair, QK_UNITS, u - 1, least)
                    if kind == 0:
                        dve.tensor_tensor(turned[:, u % 2, 0:n], by_cos[:, 0:n], by_sin[:, 0:n], ALU.add).then_inc(turn_done, 1)
                        return
                    dve.tensor_tensor(turned_raw[:, 0:n], by_cos[:, 0:n], by_sin[:, 0:n], ALU.add).then_inc(raw_done, 1)
                    need(dve, raw_done, pair, 4, u - 4 + 1, least)
                    if u == 4:
                        dve.tensor_copy(key0[:], turned_raw[:, 0:1]).then_inc(key0_made, 1)
                        need(dve, key0_made, pair, 1, 1, least)
                    dve.scalar_tensor_tensor(out=turned[:, u % 2, 0:n], in0=invalid[:, cols], scalar=key0[:, 0:1],
                                             in1=turned_raw[:, 0:n], op0=ALU.mult, op1=ALU.add).then_inc(turn_done, 1)

                def qk_lo(pair, u, least=0):
                    kind, cols, n = unit_block(u)
                    need(dve, qk_hi_made, pair, QK_UNITS, u + 1, least)
                    dve.tensor_tensor(next_lo[kind][:, cols], turned[:, u % 2, 0:n], next_hi[kind][:, cols],
                                      ALU.subtract).then_inc(qk_lo_made, 1)

                def v_mask(pair, v, least=0):
                    ts = v_tiles(v)
                    n = len(ts)
                    need(dve, pj_ready, pair, UNITS, QK_UNITS + v + 1, least)
                    need(dve, v_lo_made, pair, V_UNITS, v, least)
                    dve.tensor_tensor(v32[:, 0:n, :], pj[:, 0:n * P].rearrange("p (t c) -> p t c", t=n),
                                      bvb[:].unsqueeze(1).to_broadcast([P, n, P]), ALU.add).then_inc(pj_read_dve, 1)
                    need(dve, pj_read_dve, pair, V_UNITS, v + 1, least)
                    dve.tensor_tensor(v32m[:, 0:n, :], v32[:, 0:n, :],
                                      validc[:, ts[0]:ts[-1] + 1].unsqueeze(2).to_broadcast([P, n, P]), ALU.mult).then_inc(v_masked, 1)

                def v_lo(pair, v, least=0):
                    ts = v_tiles(v)
                    need(dve, v_hi_made, pair, V_UNITS, v + 1, least)
                    for a in range(2):
                        ins = dve.tensor_tensor(next_v[:, a, ts[0]:ts[-1] + 1, 0:HD], v32m[:, 0:len(ts), a * HD:(a + 1) * HD],
                                                next_v[:, a, ts[0]:ts[-1] + 1, HD:2 * HD], ALU.subtract)
                    ins.then_inc(v_lo_made, 1)

                def hooks(pair, k, least=0):
                    if 0 <= k - 2 < QK_UNITS:
                        qk_lo(pair, k - 2, least)
                    if 0 <= k - 1 - QK_UNITS < V_UNITS:
                        v_lo(pair, k - 1 - QK_UNITS, least)
                    if 0 <= k - 1 < QK_UNITS:
                        cosines(pair, k - 1, least)
                    if 0 <= k - QK_UNITS < V_UNITS:
                        v_mask(pair, k - QK_UNITS, least)

                def half(p, b_, qt, h):
                    at = 2 * QT * b_ + 2 * qt + h
                    need(dve, half_ready, p, BLOCKS * 2 * QT, at + 1)
                    dve.tensor_reduce(half_max[:, b_ % 2, qt, h:h + 1], mx[:, :, 0:HALF // 2], mybir.AxisListType.XY, ALU.max).then_inc(half_read, 1)

                def max_column(p, b_):
                    need(dve, half_read, p, BLOCKS * 2 * QT, 2 * QT * (b_ + 1) + 1)
                    need(dve, row_ready, p, BLOCKS, b_)
                    dve.tensor_reduce(max_col[:], half_max[:, b_ % 2], AX_X, ALU.max).then_inc(col_made, 1)

                def low(p, s):
                    g = GSIZE[s % GROUPS]
                    need(dve, exp_done, p, BLOCKS * KT, tiles_of(s)[-1][0] + 1 + 2)
                    dve.tensor_tensor(prob_lo[:, s % PRING, 0:g, :], prob[:, s % PRING, 0:g, :],
                                      hi_half(prob[:, s % PRING, 0:g, :])[:, :, 1::2], ALU.subtract).then_inc(lo_dve, 1)

                def inverse(p, i):
                    need(dve, o_copied, p, BLOCKS, i + 1 + 1)
                    dve.reciprocal(rden[:, i % 2, :], o_raw[:, i % 2, :, 2 * HD]).then_inc(rden_made, 1)

                def slot(p, s, last):
                    i, m = divmod(s, GROUPS)
                    if m in DVE_GROUPS and not (last and s >= BLOCKS * GROUPS):
                        low(p, s)
                    if m == 1 and s > GROUPS:
                        inverse(p, i - 1)
                    for b_, qt, h in halves_of(s):
                        if not (last and b_ >= BLOCKS):
                            half(p, b_, qt, h)
                    if m == 4 and not (last and i + 1 >= BLOCKS):
                        max_column(p, i + 1)

                def pair(p, last):
                    for s in range(LAG, BLOCKS * GROUPS + LAG):
                        slot(p, s, last)
                        if not last:
                            for k in range(UNITS + 2):
                                if s == hook_slot(k):
                                    hooks(p + 1, k, 1)
                                if s == hook_slot(k) + 1 and 0 <= k - 1 < QK_UNITS:
                                    turn(p + 1, k - 1, 1)

                dve.sem_inc(half_read, 1)
                for a in range(2):
                    dve.memset(K2[a][HD:HD + 1, :], 1.0).then_inc(ones_made, 1)
                    dve.tensor_copy(next_v[:, a, :, 2 * HD], validc[:])
                for k in range(UNITS + 2):
                    hooks(0, k)
                    if 0 <= k - 1 < QK_UNITS:
                        turn(0, k - 1)
                for qt in range(QT):
                    for h in range(2):
                        half(0, 0, qt, h)
                max_column(0, 0)
                for h in range(3):
                    half(0, 1, h // 2, h % 2)
                for s in range(LAG):
                    slot(0, s, False)
                body(pair, dve)

            @block.gpsimd
            def _(pool):
                def split_weights(pair, least=0):
                    need(pool, w_hi_made, pair, 1, 1, least)
                    pool.tensor_tensor(w_lo[:], w32[:], w_hi[:], ALU.subtract).then_inc(w_lo_made, 1)

                def sines(pair, u, least=0):
                    kind, cols, n = unit_block(u)
                    need(pool, swapped[u % 2], pair, 64 * 4, 64 * (u // 2 + 1), least)
                    need(pool, turn_done, pair, QK_UNITS, u, least)
                    pool.tensor_tensor(by_sin[:, 0:n], q32s[:, u % 2, 0:n], (ropeq, ropek)[kind][:, 1, cols], ALU.mult).then_inc(sin_done, 1)

                def low(p, s):
                    g = GSIZE[s % GROUPS]
                    need(pool, exp_done, p, BLOCKS * KT, tiles_of(s)[-1][0] + 1 + 2)
                    pool.tensor_tensor(prob_lo[:, s % PRING, 0:g, :], prob[:, s % PRING, 0:g, :],
                                       hi_half(prob[:, s % PRING, 0:g, :])[:, :, 1::2], ALU.subtract).then_inc(lo_pool, 1)

                def output(p, i):
                    need(pool, rden_made, p, BLOCKS, i + 1)
                    pool.tensor_tensor(o_sum[:], o_raw[:, i % 2, :, 0:HD], o_raw[:, i % 2, :, HD:2 * HD], ALU.add).then_inc(o_summed, 1)
                    need(pool, o_summed, p, BLOCKS, i + 1)
                    need(pool, o_stored[i % 2], p, 16 * BLOCKS // 2, 16 * (i // 2 + 1))
                    pool.tensor_tensor(o_out[:, i % 2, :, :], o_sum[:], rden[:, i % 2, :].unsqueeze(2).to_broadcast([P, QT, HD]),
                                       ALU.mult).then_inc(o_made, 1)

                def slot(p, s, last):
                    i, m = divmod(s, GROUPS)
                    if m in POOL_GROUPS and not (last and s >= BLOCKS * GROUPS):
                        low(p, s)
                    if m == 1 and s > GROUPS:
                        output(p, i - 1)

                def pair(p, last):
                    for s in range(LAG, BLOCKS * GROUPS + LAG):
                        slot(p, s, last)
                        if not last:
                            if s == 4:
                                split_weights(p + 1, 1)
                            for k in range(UNITS + 2):
                                if s == hook_slot(k) and 0 <= k - 1 < QK_UNITS:
                                    sines(p + 1, k - 1, 1)

                pool.sem_inc(o_made, 2)
                split_weights(0)
                for u in range(QK_UNITS):
                    sines(0, u)
                for s in range(LAG):
                    slot(0, s, False)
                body(pair, pool)

            @block.sync
            def _(sp):
                def load_weights(pair, least=0):
                    need(sp, w_lo_made, pair, 1, 0, least)
                    sp.dma_start(w32[:], w_pairs[bass.ds(pair, 1)].rearrange("a p k c n -> p (a k) c n")).then_inc(w_loaded, 16)
                    need(sp, pj_read_act, pair, QK_UNITS, 0, least)
                    sp.dma_start(bqk[:], b_pairs[bass.ds(pair, 1)].rearrange("a p k -> p (a k)")).then_inc(w_loaded, 16)
                    need(sp, v_masked, pair, V_UNITS, 0, least)
                    sp.dma_start(bvb[:], bv_pairs[bass.ds(pair, 1)].rearrange("a c -> (a c)").partition_broadcast(P)).then_inc(w_loaded, 16)

                def swap(pair, u, least=0):
                    kind, cols, n = unit_block(u)
                    need(sp, pj_read_act, pair, QK_UNITS, u + 1, least)
                    for h in range(2):
                        for k in range(2):
                            a, z = HD * h + 32 * k, HD * h + 32 * (1 - k)
                            sp.dma_start(q32s[a:a + 32, u % 2, 0:n], q32[z:z + 32, u % 2, 0:n]).then_inc(swapped[u % 2], 16)

                def load_q(pair, a):
                    need(sp, qk_lo_made, pair, QK_UNITS, 4, 0 if isinstance(pair, int) else 1)
                    r = slice(a * HD, (a + 1) * HD)
                    sp.dma_start(Q1[a][0:HD, :], next_hi[0][r, :]).then_inc(q_loaded[a], 16)
                    sp.dma_start(Q1[a][HD:P, :], next_hi[0][r, :]).then_inc(q_loaded[a], 16)
                    sp.dma_start(Q2[a][0:HD, :], next_lo[0][r, :]).then_inc(q_loaded[a], 16)

                def load_k(pair, a):
                    need(sp, qk_lo_made, pair, QK_UNITS, 8, 0 if isinstance(pair, int) else 1)
                    r = slice(a * HD, (a + 1) * HD)
                    sp.dma_start(K1[a][0:HD, :], next_hi[1][r, :]).then_inc(k_loaded[a], 16)
                    sp.dma_start(K1[a][HD:P, :], next_lo[1][r, :]).then_inc(k_loaded[a], 16)
                    sp.dma_start(K2[a][0:HD, :], next_hi[1][r, :]).then_inc(k_loaded[a], 16)

                def load_v(pair, a):
                    need(sp, v_lo_made, pair, V_UNITS, 4, 0 if isinstance(pair, int) else 1)
                    sp.dma_start(VV[a][:], next_v[:, a, :, :]).then_inc(v_loaded[a], 16)

                def store(p, i):
                    a, c = set_of(i)
                    need(sp, o_made, p, BLOCKS, i + 1 + 2)
                    rows = o_dram[c * QC:(c + 1) * QC, :].rearrange("(t p) d -> p t d", p=P)
                    sp.dma_start(rows[:, :, bass.ds(p * P + a * HD, HD)], o_out[:, i % 2, :, :]).then_inc(o_stored[i % 2], 16)

                def pair(p, last):
                    if not last:
                        load_weights(p + 1, 1)
                    for s in range(LAG, BLOCKS * GROUPS + LAG):
                        if s % GROUPS == 1 and s > GROUPS:
                            store(p, s // GROUPS - 1)
                        if last:
                            continue
                        for u in range(QK_UNITS):
                            if s == hook_slot(u):
                                swap(p + 1, u, 1)
                        if s == hook_slot(6) + 1:
                            load_q(p + 1, 0)
                        if s == hook_slot(9) + 1:
                            load_k(p + 1, 0)
                        if s == hook_slot(12) + 1:
                            load_v(p + 1, 0)
                    if not last:
                        load_q(p + 1, 1)
                        load_k(p + 1, 1)
                        load_v(p + 1, 1)

                for i in range(2):
                    sp.sem_inc(o_stored[i], 16)
                load_weights(0)
                for u in range(QK_UNITS):
                    swap(0, u)
                for a in range(2):
                    load_q(0, a)
                    load_k(0, a)
                for a in range(2):
                    load_v(0, a)
                body(pair, sp)
                for i in range(2):
                    sp.wait_ge(o_stored[i], 16 + 16 * PAIRS * BLOCKS // 2)

def experts(nc, sem, maker, have):
    x, wo, bo, gate, w_exp, o_dram, out = (have[k] for k in ("x", "wo", "bo", "gate", "w_exp", "o_dram", "out"))
    ident, ident_b, eps_col, rank8 = (have[k] for k in ("ident", "ident_b", "eps_col", "rank8"))
    with ExitStack() as both:
        sb, _ = maker(both)
        x1 = sb("x1", [P, ST, D])
        YH = sb("YH", [P, DT, S], BF16)
        YL = sb("YL", [P, DT, S], BF16)
        logits = sb("logits", [P, ST, E])
        project_out(nc, sem, maker, locals())
        mixture(nc, sem, maker, locals())


def project_out(nc, sem, maker, have):
    x, wo, bo, gate, o_dram, ident, eps_col, x1, YH, YL, logits = (have[k] for k in (
        "x", "wo", "bo", "gate", "o_dram", "ident", "eps_col", "x1", "YH", "YL", "logits"))
    J = H * HD // P
    with ExitStack() as ctx:
        sb, pb = maker(ctx)
        o_in = sb("o_in", [P, 2, J * P])
        OH = sb("OH", [P, 2, J, P], BF16)
        OL = sb("OL", [P, 2, J, P], BF16)
        wo32 = sb("wo32", [P, J, D])
        wo_hi = sb("wo_hi", [P, J, D], BF16)
        wo_lo = sb("wo_lo", [P, J, D], BF16)
        bob = sb("bob", [P, D])
        gate_sb = sb("gate_sb", [P, DT, E])
        stats = sb("stats2", [P, 2, 6])
        mv = sb("mv2", [P, 2, 2])
        std = sb("std2", [P, 2])
        rstd = sb("rstd2", [P, 2])
        normed = sb("normed2", [P, 2, D])
        YF = sb("YF", [P, 2, DT, P])
        ot = [pb(f"ot{i}", [P, 2, 4, P]) for i in range(2)]
        wp = [pb(f"wp{i}", [P, 512]) for i in range(2)]
        yt = pb("yt", [P, 4, P])
        gp = pb("gp", [P, 512])

        o_loaded = [sem("o_loaded0"), sem("o_loaded1")]
        in_loaded, wo_loaded = sem("in_loaded"), sem("wo_loaded")
        wo_hi_made, wo_lo_made = sem("wo_hi_made"), sem("wo_lo_made")
        bias_added = sem("bias_added")
        ot_ready, oh_made, ol_made = sem("ot_ready"), sem("oh_made"), sem("ol_made")
        wp_ready, x1_made, st_made, mv_made, sd_made, rs_made, nm_made = (sem(n) for n in (
            "wp_ready", "x1_made", "st_made", "mv_made", "sd_made", "rs_made", "nm_made"))
        yt_ready, yh_made, yl_made, gp_ready, gp_read = (sem(n) for n in ("yt_ready", "yh_made", "yl_made", "gp_ready", "gp_read"))

        STEPS = ST + 4

        with nc.Block() as block:
            @block.sync
            def _(sp):
                sp.dma_start(wo32[:], wo.rearrange("(j p) d -> p j d", p=P)).then_inc(wo_loaded, 16)
                for t in range(ST):
                    if t >= 2:
                        sp.wait_ge(ot_ready, t - 1)
                    sp.dma_start(o_in[:, t % 2, :], o_dram[t * P:(t + 1) * P, :]).then_inc(o_loaded[t % 2], 16)

            @block.scalar
            def _(act):
                act.dma_start(x1[:], x[0].rearrange("(t p) d -> p t d", p=P)).then_inc(in_loaded, 16)
                act.dma_start(bob[:], bo.partition_broadcast(P)).then_inc(in_loaded, 16)
                act.dma_start(gate_sb[:], gate).then_inc(in_loaded, 16)
                act.wait_ge(wo_loaded, 16)
                act.activation(wo_hi[:], wo32[:], ACT.Copy).then_inc(wo_hi_made, 1)
                for step in range(STEPS):
                    t = step
                    if t < ST:
                        act.wait_ge(ot_ready, t + 1)
                        if t >= 2:
                            act.wait_ge(wp_ready, t - 1)
                        act.activation(OH[:, t % 2, :, :], ot[t % 2][:].rearrange("p b k c -> p (b k) c"), ACT.Copy).then_inc(oh_made, 1)
                    t = step - 1
                    if 0 <= t < ST:
                        act.wait_ge(mv_made, t + 1)
                        act.activation(std[:, t % 2:t % 2 + 1], mv[:, t % 2, 1:2], ACT.Sqrt, bias=eps_col[:]).then_inc(sd_made, 1)
                    t = step - 3
                    if 0 <= t < ST:
                        act.wait_ge(yt_ready, t + 1)
                        if t >= 2:
                            act.wait_ge(gp_ready, t - 1)
                        act.activation(YF[:, t % 2, :, :], yt[:, 0:DT, :], ACT.Copy)
                        act.activation(YH[:, :, t * P:(t + 1) * P], yt[:, 0:DT, :], ACT.Copy).then_inc(yh_made, 1)

            @block.gpsimd
            def _(pool):
                pool.wait_ge(wo_hi_made, 1)
                pool.tensor_tensor(wo_lo[:], wo32[:], wo_hi[:], ALU.subtract).then_inc(wo_lo_made, 1)
                pool.wait_ge(in_loaded, 48)
                pool.tensor_tensor(x1[:], x1[:], bob[:].unsqueeze(1).to_broadcast([P, ST, D]), ALU.add).then_inc(bias_added, 1)

            @block.vector
            def _(dve):
                for step in range(STEPS):
                    t = step
                    if t < ST:
                        dve.wait_ge(oh_made, t + 1)
                        dve.tensor_tensor(OL[:, t % 2, :, :], ot[t % 2][:].rearrange("p b k c -> p (b k) c"), OH[:, t % 2, :, :],
                                          ALU.subtract).then_inc(ol_made, 1)
                    t = step - 1
                    if 0 <= t < ST:
                        if t == 0:
                            dve.wait_ge(bias_added, 1)
                        dve.wait_ge(wp_ready, t + 1)
                        dve.tensor_tensor(x1[:, t, :], wp[t % 2][:, 0:D], x1[:, t, :], ALU.add).then_inc(x1_made, 1)
                        dve.wait_ge(x1_made, t + 1)
                        dve.bn_stats(stats[:, t % 2, :], x1[:, t, :]).then_inc(st_made, 1)
                        dve.wait_ge(st_made, t + 1)
                        dve.bn_aggr(mv[:, t % 2, :], stats[:, t % 2, :]).then_inc(mv_made, 1)
                    t = step - 2
                    if 0 <= t < ST:
                        dve.wait_ge(sd_made, t + 1)
                        dve.reciprocal(rstd[:, t % 2:t % 2 + 1], std[:, t % 2:t % 2 + 1]).then_inc(rs_made, 1)
                        dve.wait_ge(rs_made, t + 1)
                        if t >= 2:
                            dve.wait_ge(yt_ready, t - 1)
                        dve.tensor_scalar(normed[:, t % 2, :], x1[:, t, :], mv[:, t % 2, 0:1], rstd[:, t % 2:t % 2 + 1],
                                          ALU.subtract, ALU.mult).then_inc(nm_made, 1)
                    t = step - 3
                    if 0 <= t < ST:
                        dve.wait_ge(yh_made, t + 1)
                        dve.tensor_tensor(YL[:, :, t * P:(t + 1) * P], yt[:, 0:DT, :], YH[:, :, t * P:(t + 1) * P],
                                          ALU.subtract).then_inc(yl_made, 1)
                    t = step - 4
                    if 0 <= t < ST:
                        dve.wait_ge(gp_ready, t + 1)
                        dve.tensor_copy(logits[:, t, :], gp[:, 0:E]).then_inc(gp_read, 1)

            @block.tensor
            def _(pe):
                for step in range(STEPS):
                    t = step
                    if t < ST:
                        pe.wait_ge(o_loaded[t % 2], 16 * (t // 2 + 1))
                        if t >= 2:
                            pe.wait_ge(ol_made, t - 1)
                        for j in range(J):
                            ins = pe.transpose(ot[t % 2][:, j // 4, j % 4, :], o_in[:, t % 2, j * P:(j + 1) * P], ident)
                        ins.then_inc(ot_ready, 1)
                    t = step - 1
                    if 0 <= t < ST:
                        if t == 0:
                            pe.wait_ge(wo_lo_made, 1)
                        pe.wait_ge(ol_made, t + 1)
                        if t >= 2:
                            pe.wait_ge(x1_made, t - 1)
                        steps = [(z, w, j) for j in range(J) for z, w in ((OH, wo_hi), (OH, wo_lo), (OL, wo_hi))]
                        for n, (z, w, j) in enumerate(steps):
                            ins = pe.matmul(wp[t % 2][:, 0:D], z[:, t % 2, j, :], w[:, j, :], start=n == 0, stop=n == len(steps) - 1)
                        ins.then_inc(wp_ready, 1)
                    t = step - 3
                    if 0 <= t < ST:
                        pe.wait_ge(nm_made, t + 1)
                        if t >= 1:
                            pe.wait_ge(yl_made, t)
                        for d in range(DT):
                            ins = pe.transpose(yt[:, d, :], normed[:, t % 2, d * P:(d + 1) * P], ident)
                        ins.then_inc(yt_ready, 1)
                    t = step - 4
                    if 0 <= t < ST:
                        pe.wait_ge(yh_made, t + 1)
                        if t >= 1:
                            pe.wait_ge(gp_read, t)
                        for d in range(DT):
                            ins = pe.matmul(gp[:, 0:E], YF[:, t % 2, d, :], gate_sb[:, d, :], start=d == 0, stop=d == DT - 1)
                        ins.then_inc(gp_ready, 1)


def mixture(nc, sem, maker, have):
    w_exp, out, x1, YH, YL, logits, rank8 = (have[k] for k in ("w_exp", "out", "x1", "YH", "YL", "logits", "rank8"))
    WC = 2 * DT * FF + FT * D
    ITS = 2 * CH
    TT = QC // P
    Q = FT
    with ExitStack() as ctx:
        sb, pb = maker(ctx)
        w32 = sb("we32", [P, WC])
        w_hi = sb("we_hi", [P, 2, WC], BF16)
        w_lo = sb("we_lo", [P, 2, WC], BF16)
        gates = sb("gates", [P, ST, E])
        gcur = sb("gcur", [P, ST, 2])
        g8 = [sb(f"g8_{i}", [P, ST, E]) for i in range(3)]
        pick = [sb(f"pick{i}", [P, ST, E]) for i in range(2)]
        top = sb("top", [P, 4, ST])
        ew = sb("ew", [P, 4, ST])
        act_s = sb("act_s", [P, 2, QC])
        hid = sb("hid", [P, 2, FT, QC])
        hid_lo = sb("hid_lo", [P, 2, FT, QC], BF16)
        pa = [pb(f"pa{i}", [P, QC]) for i in range(2)]
        pg = [pb(f"pg{i}", [P, QC]) for i in range(2)]
        py = [pb(f"py{i}", [P, 2, D]) for i in range(4)]

        we_loaded, we_hi_made, we_lo_made = sem("we_loaded"), sem("we_hi_made"), sem("we_lo_made")
        up_ready = sem("up_ready")
        silu_made = sem("silu_made")
        hid_made = sem("hid_made")
        lo_made = sem("hid_lo_made")
        down_ready = sem("down_ready")
        added = sem("added")
        routed, picked, exp_made, gates_made, gcur_made = (sem(n) for n in ("routed", "picked", "exp_made", "gates_made", "gcur_made"))
        stored = sem("stored")

        def w13(which, e, d, f):
            at = (which * DT + d) * FF + f * P
            return slice(at, at + P)

        def w2(f):
            at = 2 * DT * FF + f * D
            return slice(at, at + D)

        def body(program, engine):
            with engine.Fori(0, E // 2 - 1) as q:
                program(q, False)
            program(E // 2 - 1, True)

        SLOTS = range(Q, Q * (ITS + 1))

        def downs_of(z):
            for i in range(ITS):
                for k in range(2):
                    if z == Q * i + 5 + 2 * k:
                        return i, k

        with nc.Block() as block:
            @block.sync
            def _(sp):
                def load(e, least=0):
                    need(sp, we_lo_made, e, 1, 0, least)
                    sp.dma_start(w32[:], w_exp[bass.ds(e, 1)].rearrange("a p c -> p (a c)")).then_inc(we_loaded, 16)

                def two(q, last):
                    load(2 * q + 1, 1)
                    if not last:
                        load(2 * q + 2, 1)

                load(0)
                body(two, sp)
                for c in range(CH):
                    sp.wait_ge(added, 4 + (E - 1) * 2 * CH + 2 * (c + 1))
                    sp.dma_start(out[0, c * QC:(c + 1) * QC, :].rearrange("(t p) d -> p t d", p=P),
                                 x1[:, c * TT:(c + 1) * TT, :]).then_inc(stored, 16)
                sp.wait_ge(stored, 16 * CH)

            @block.scalar
            def _(act):
                def silu(q, z):
                    need(act, up_ready, q, ITS * Q, z + 1)
                    need(act, hid_made, q, ITS * Q, z + 1)
                    act.activation(act_s[:, z % 2, :], pa[z % 2][:], ACT.Silu).then_inc(silu_made, 1)

                def two(q, last):
                    for z in SLOTS:
                        if z == Q + 2:
                            need(act, we_loaded, q, 32, 32)
                            need(act, down_ready, q, ITS * 2, 4)
                            act.activation(w_hi[:, 1, :], w32[:], ACT.Copy).then_inc(we_hi_made, 1)
                        if z == Q * (CH + 1) + 2 and not last:
                            need(act, we_loaded, q, 32, 48)
                            need(act, down_ready, q, ITS * 2, 4 + 2 * CH)
                            act.activation(w_hi[:, 0, :], w32[:], ACT.Copy).then_inc(we_hi_made, 1)
                        if not (last and z >= Q * ITS):
                            silu(q, z)

                act.wait_ge(routed, 1)
                act.activation(ew[:, 0, :], top[:, 2, :], ACT.Exp).then_inc(exp_made, 1)
                act.wait_ge(we_loaded, 16)
                act.activation(w_hi[:, 0, :], w32[:], ACT.Copy).then_inc(we_hi_made, 1)
                for z in range(Q):
                    silu(0, z)
                body(two, act)

            @block.gpsimd
            def _(pool):
                def split(q, slot, count):
                    need(pool, we_hi_made, q, 2, count)
                    pool.tensor_tensor(w_lo[:, slot, :], w32[:], w_hi[:, slot, :], ALU.subtract).then_inc(we_lo_made, 1)

                def low(q, z):
                    i, f = divmod(z, Q)
                    need(pool, hid_made, q, ITS * Q, z + 1 + 2)
                    pool.tensor_tensor(hid_lo[:, i % 2, f, :], hid[:, i % 2, f, :], hi_half(hid[:, i % 2, f, :])[:, 1::2],
                                       ALU.subtract).then_inc(lo_made, 1)

                def two(q, last):
                    for z in SLOTS:
                        if z == Q + 2:
                            split(q, 1, 2)
                        if z == Q * (CH + 1) + 2 and not last:
                            split(q, 0, 3)
                        if not (last and z >= Q * ITS):
                            low(q, z)

                split(0, 0, 1)
                for z in range(Q):
                    low(0, z)
                body(two, pool)

            @block.vector
            def _(dve):
                def route():
                    chain = [0]

                    def then(ins):
                        chain[0] += 1
                        ins.then_inc(picked, 1)
                        dve.wait_ge(picked, chain[0])

                    ranks = rank8.unsqueeze(1).to_broadcast([P, ST, E])
                    left = logits
                    for k in range(2):
                        def wide(row):
                            return top[:, row, :].unsqueeze(2).to_broadcast([P, ST, E])
                        then(dve.tensor_reduce(top[:, k, :], left[:], AX_X, ALU.max))
                        then(dve.tensor_tensor(g8[0][:], left[:], wide(k), ALU.is_ge))
                        then(dve.tensor_tensor(g8[1][:], g8[0][:], ranks, ALU.mult))
                        then(dve.tensor_reduce(top[:, 3, :], g8[1][:], AX_X, ALU.max))
                        then(dve.tensor_tensor(pick[k][:], g8[1][:], wide(3), ALU.is_equal))
                        if k == 0:
                            then(dve.scalar_tensor_tensor(out=g8[2][:], in0=pick[0][:], scalar=-3e38, in1=logits[:],
                                                          op0=ALU.mult, op1=ALU.add))
                            left = g8[2]
                    dve.tensor_tensor(top[:, 2, :], top[:, 1, :], top[:, 0, :], ALU.subtract).then_inc(routed, 1)
                    dve.wait_ge(exp_made, 1)
                    then(dve.tensor_scalar(ew[:, 1, :], ew[:, 0, :], 1.0, None, ALU.add))
                    then(dve.reciprocal(ew[:, 2, :], ew[:, 1, :]))
                    then(dve.tensor_tensor(ew[:, 3, :], ew[:, 0, :], ew[:, 2, :], ALU.mult))
                    for k in range(2):
                        then(dve.tensor_tensor(g8[k][:], pick[k][:], ew[:, 2 + k, :].unsqueeze(2).to_broadcast([P, ST, E]), ALU.mult))
                    dve.tensor_tensor(gates[:], g8[0][:], g8[1][:], ALU.add).then_inc(gates_made, 1)
                    dve.wait_ge(gates_made, 1)

                def hidden(q, z):
                    i, f = divmod(z, Q)
                    need(dve, silu_made, q, ITS * Q, z + 1)
                    need(dve, down_ready, q, ITS * 2, 2 * (i - 1) + 4)
                    dve.tensor_tensor(hid[:, i % 2, f, :], act_s[:, z % 2, :], pg[z % 2][:], ALU.mult).then_inc(hid_made, 1)

                def add(q, i, k):
                    c = i % CH
                    need(dve, down_ready, q, ITS * 2, 2 * i + k + 1 + 4)
                    for j in range(2):
                        t = c * TT + 2 * k + j
                        ins = dve.scalar_tensor_tensor(out=x1[:, t, :], in0=py[(2 * i + k) % 4][:, j, :], scalar=gcur[:, t, i // CH:i // CH + 1],
                                                       in1=x1[:, t, :], op0=ALU.mult, op1=ALU.add)
                    ins.then_inc(added, 1)

                def two(q, last):
                    need(dve, added, q, ITS * 2, 4)
                    dve.tensor_copy(gcur[:], gates[:, :, bass.ds(2 * q, 2)]).then_inc(gcur_made, 1)
                    need(dve, gcur_made, q, 1, 1)
                    for z in SLOTS:
                        if not (last and z >= Q * ITS):
                            hidden(q, z)
                        if downs_of(z - 1):
                            add(q, *downs_of(z - 1))
                    add(q, *downs_of(SLOTS[-1]))

                dve.sem_inc(hid_made, 2)
                dve.sem_inc(added, 4)
                route()
                for z in range(Q):
                    hidden(0, z)
                body(two, dve)

            @block.tensor
            def _(pe):
                def up(q, z):
                    i, f = divmod(z, Q)
                    slot, c = i // CH % 2, i % CH
                    if f == 0 and c == 0:
                        need(pe, we_lo_made, q, 2, i // CH + 1)
                    need(pe, hid_made, q, ITS * Q, z + 1)
                    for which, bank in ((0, pa), (1, pg)):
                        steps = [(w, y, d) for d in range(DT) for w, y in ((w_hi, YH), (w_hi, YL), (w_lo, YH))]
                        for n, (w, y, d) in enumerate(steps):
                            ins = pe.matmul(bank[z % 2][:], w[:, slot, w13(which, i, d, f)], y[:, d, c * QC:(c + 1) * QC],
                                            start=n == 0, stop=n == len(steps) - 1)
                    ins.then_inc(up_ready, 1)

                def down(q, i, k):
                    slot = i // CH % 2
                    bank = (2 * i + k) % 4
                    need(pe, added, q, ITS * 2, 2 * i + k + 1)
                    need(pe, lo_made, q, ITS * Q, Q * (i + 1))
                    for j in range(2):
                        tok = slice((2 * k + j) * P, (2 * k + j + 1) * P)
                        for f in range(FT):
                            hi = hi_half(hid[:, i % 2, f, :])[:, 2 * tok.start + 1:2 * tok.stop:2]
                            for n, (z, w) in enumerate(((hi, w_hi), (hi, w_lo), (hid_lo[:, i % 2, f, tok], w_hi))):
                                ins = pe.matmul(py[bank][:, j, :], z, w[:, slot, w2(f)], start=f == 0 and n == 0,
                                                stop=f == FT - 1 and n == 2)
                    ins.then_inc(down_ready, 1)

                def two(q, last):
                    for z in SLOTS:
                        if not (last and z >= Q * ITS):
                            up(q, z)
                        if downs_of(z):
                            down(q, *downs_of(z))

                pe.sem_inc(down_ready, 4)
                for z in range(Q):
                    up(0, z)
                body(two, pe)


_INS = ["x", "ctx_1024", "_lenS2", "L0_xattn_ln_g", "L0_xattn_ln_b", "w_pairs", "b_pairs", "bv_pairs", "L0_xattn_Wo",
        "L0_xattn_bo", "gate", "w_exp", "rope", "keypos", "consts"]


def kernel(**inputs):
    import numpy as np
    import concourse.bacc as bacc
    from concourse.bass_utils import run_bass_kernel_spmd

    a = {k: np.asarray(v) for k, v in inputs.items()}
    order = np.concatenate([np.arange(0, HD, 2), np.arange(1, HD, 2)])
    cols = (np.arange(H)[:, None] * HD + order[None, :]).reshape(-1)

    def by_pair(w):
        return w.reshape(DT, P, PAIRS, P).transpose(2, 1, 0, 3)

    a["w_pairs"] = np.stack([by_pair(a["L0_xattn_Wq"][:, cols]), by_pair(a["L0_xattn_Wk"][:, cols]),
                             by_pair(a["L0_xattn_Wv"])], axis=2)
    a["b_pairs"] = np.stack([a["L0_xattn_bq"][cols].reshape(PAIRS, P), a["L0_xattn_bk"][cols].reshape(PAIRS, P)], axis=2)
    a["bv_pairs"] = a["L0_xattn_bv"].reshape(PAIRS, P)
    a["gate"] = a["L0_ffn_gate_w"].T.reshape(DT, P, E).transpose(1, 0, 2)

    def by_rows(w):
        return w.reshape(E, -1, P, w.shape[2]).transpose(0, 2, 1, 3).reshape(E, P, -1)

    a["w_exp"] = np.concatenate([by_rows(a["L0_ffn_w1"].transpose(0, 2, 1)), by_rows(a["L0_ffn_w3"].transpose(0, 2, 1)),
                                 by_rows(a["L0_ffn_w2"].transpose(0, 2, 1))], axis=2)
    inv = (np.float32(1) / np.power(10000.0, np.arange(0, HD, 2) / HD)).astype(np.float32)
    angle = (np.arange(S, dtype=np.float32)[None, :] * inv[:, None]).astype(np.float64)
    a["rope"] = np.stack([np.tile(np.cos(angle), (4, 1)),
                          np.tile(np.concatenate([-np.sin(angle), np.sin(angle)]), (2, 1))]).astype(np.float32)
    key = np.arange(LP, dtype=np.float32)
    key[L:] = 1e9
    a["keypos"] = key
    a["consts"] = np.concatenate([np.eye(P, dtype=np.float32), key.reshape(KT, P).T,
                                  np.tile(np.arange(E, 0, -1, dtype=np.float32), (P, 1))], axis=1)

    nc = bacc.Bacc("TRN2", target_bir_lowering=False, num_devices=1)
    arrays, args = {}, []
    for name in _INS:
        v = np.ascontiguousarray(a[name])
        arrays[f"in_{name}"] = v
        args.append(nc.dram_tensor(f"in_{name}", v.shape, mybir.dt.from_np(v.dtype), kind="ExternalInput").ap())
    out = nc.dram_tensor("out", [1, S, D], F32, kind="ExternalOutput").ap()
    build(nc, *args, out)
    r = run_bass_kernel_spmd(nc, [arrays], core_ids=[0])
    return r.results[0]["out"]
```

```python
from contextlib import ExitStack

import concourse.bass as bass
from concourse import mybir

P = 128
F32 = mybir.dt.float32
BF16 = mybir.dt.bfloat16
I32 = mybir.dt.int32
ALU = mybir.AluOpType
ACT = mybir.ActivationFunctionType
AX_X = mybir.AxisListType.X

S, D, H, HD = 2048, 256, 16, 64
L = 1601
E, FF = 8, 512
EPS = 1e-5
DT = D // P
KT = -(-L // P)
LP = KT * P
ST = S // P
PAIRS = H // 2
QC = 512
CH = S // QC
QT = QC // P
VW = 2 * HD + 1
BLOCKS = 2 * CH
LAG = 2
PRING = 4
QK_UNITS = 8
FT = FF // P
KEY_TILES = (10, 11, 12, 13)


class Plan:

    def __init__(self, kt):
        self.kt = kt
        self.gsize = [2] * (kt // 2) + [1] * (kt % 2)
        self.groups = len(self.gsize)
        self.pool_groups = (1, self.groups // 2 + 1)
        self.dve_groups = tuple(m for m in range(self.groups) if m not in self.pool_groups)
        self.kc = kt * P // 4
        self.v_units = -(-kt // 4)
        self.units = QK_UNITS + self.v_units
        if kt * P <= 3 * 512:
            self.width = -(-kt * P // 3)
            self.parts = [[min(j * self.width, kt * P - self.width) for j in range(3)]]
        else:
            self.width = -(-L // 4)
            self.parts = [[2 * h * self.width, (2 * h + 1) * self.width] for h in range(2)]
        self.block_parts = QT * len(self.parts)
        slots = self.groups - 1
        each = [self.block_parts // slots + (j < self.block_parts % slots) for j in range(slots)]
        self.parts_at = [list(range(sum(each[:j]), sum(each[:j + 1]))) for j in range(slots)]

    def tiles_of(self, s):
        i, m = divmod(s, self.groups)
        return [(self.kt * i + 2 * m + j, 2 * m + j) for j in range(self.gsize[m])]

    def parts_of(self, s):
        i, m = divmod(s, self.groups)
        if m == self.groups - 2:
            return []
        ahead, at = (2, 0) if m == self.groups - 1 else (1, m + 1)
        return [(i + ahead, n // len(self.parts), n % len(self.parts)) for n in self.parts_at[at]]

    def column_block(self, s):
        i, m = divmod(s, self.groups)
        return i + 1 if m == self.groups - 3 else None

    def row_block(self, s):
        i, m = divmod(s, self.groups)
        return i + 1 if m == self.groups - 2 else None

    def hook_slot(self, k):
        return self.groups * (1 + k // 2) + (0, 2)[k % 2]

    def v_tiles(self, v):
        return range(4 * v, min(4 * v + 4, self.kt))

    def unit_block(self, u):
        kind, c = divmod(u, 4)
        n = (QC, self.kc)[kind]
        return kind, slice(c * n, (c + 1) * n), n


def for_key_count(engine, length, program):
    count = engine.value_load(length)

    def choose(plans):
        if len(plans) == 1:
            program(Plan(plans[0]))
            return
        with engine.If(count <= plans[0] * P):
            program(Plan(plans[0]))
        with engine.Else():
            choose(plans[1:])

    choose(KEY_TILES)


def need(eng, sem, index, per, count, least=0):
    if isinstance(index, int):
        if per * index + count > 0:
            eng.wait_ge(sem, per * index + count)
    else:
        assert per * least + count > 0
        eng.wait_ge(sem, index * per + count)


def hi_half(ap):
    return ap.bitcast(BF16)


def build(nc, x, ctx_in, length, g, b, w_pairs, b_pairs, bv_pairs, wo, bo, gate, w_exp, rope, keypos, consts, out):
    o_dram = nc.dram_tensor("attention_out", [S, H * HD], F32, kind="Internal").ap()

    with ExitStack() as whole:
        def sem(name):
            return whole.enter_context(nc.semaphore(name))

        def maker(stack):
            def sb(name, shape, dt=F32):
                return stack.enter_context(nc.sbuf_tensor(name, shape, dt))

            def pb(name, shape, dt=F32):
                return stack.enter_context(nc.psum_tensor(name, shape, dt))
            return sb, pb

        sb, _ = maker(whole)
        cst = sb("cst", [P, P + KT + 8])
        ident_b = sb("ident_b", [P, P], BF16)
        eps_col = sb("eps_col", [P, 1])
        ident = cst[:, 0:P]
        rank8 = cst[:, P + KT:P + KT + 8]

        with ExitStack() as upto_attend:
            sb, _ = maker(upto_attend)
            XH = sb("XH", [P, DT, S], BF16)
            XL = sb("XL", [P, DT, S], BF16)
            CHI = sb("CHI", [P, DT, LP], BF16)
            CLO = sb("CLO", [P, DT, LP], BF16)
            ropeq = sb("ropeq", [P, 2, S])
            ropek = sb("ropek", [P, 2, LP])
            invalid = sb("invalid", [P, LP], BF16)
            validc = sb("validc", [P, KT])
            prepare(nc, sem, maker, locals())
            attend(nc, sem, maker, locals())
        experts(nc, sem, maker, locals())


def prepare(nc, sem, maker, have):
    x, ctx_in, length, g, b = (have[k] for k in ("x", "ctx_in", "length", "g", "b"))
    rope, keypos, consts, cst = (have[k] for k in ("rope", "keypos", "consts", "cst"))
    XH, XL, CHI, CLO, ropeq, ropek, invalid, validc, ident_b, eps_col, ident = (have[k] for k in (
        "XH", "XL", "CHI", "CLO", "ropeq", "ropek", "invalid", "validc", "ident_b", "eps_col", "ident"))
    NT = KT + ST
    with ExitStack() as ctx:
        sb, pb = maker(ctx)
        Z = sb("Z", [P, NT, D])
        keyb = sb("keyb", [P, LP])
        valid = sb("valid", [P, LP])
        len_i = sb("len_i", [P, 1], I32)
        len_f = sb("len_f", [P, 1])
        gb = sb("gb", [P, 2, DT])
        stats = sb("stats", [P, NT, 6])
        mv = sb("mv", [P, 2, NT, 2])
        std = sb("std", [P, 2, NT])
        rstd = sb("rstd", [P, 2, NT])
        NB = 4
        T32 = sb("T32", [P, 2, 512])
        tp = [pb(f"tp{i}", [P, 4, P]) for i in range(NB)]

        ctx_loaded = sem("ctx_loaded")
        x_loaded = sem("x_loaded")
        small_loaded = sem("small_loaded")
        rope_loaded = sem("rope_loaded")
        tail_clear = sem("tail_clear")
        consts_made = sem("consts_made")
        stats_made = sem("stats_made")
        moments = sem("moments")
        std_made = sem("std_made")
        rstd_made = sem("rstd_made")
        normed = sem("normed")
        valid_made = sem("valid_made")
        len_made = sem("len_made")
        table_made = sem("table_made")
        turned = sem("turned")
        scaled = sem("scaled")
        hi_made = sem("hi_made")
        lo_made = sem("lo_made")

        turns = [(CHI, CLO, d, t, min(4, KT - t), 0) for t in range(0, KT, 4) for d in range(DT)]
        turns += [(XH, XL, d, t, min(4, ST - t), KT) for t in range(0, ST, 4) for d in range(DT)]

        with nc.Block() as block:
            @block.sync
            def _(sp):
                full = (L // P) * P
                sp.dma_start(Z[:, 0:L // P, :], ctx_in[0, 0:full, :].rearrange("(t p) d -> p t d", p=P)).then_inc(ctx_loaded, 16)
                sp.wait_ge(tail_clear, 1)
                sp.dma_start(Z[0:L - full, KT - 1, :], ctx_in[0, full:L, :]).then_inc(ctx_loaded, 16)
                sp.dma_start(Z[:, KT:NT, :], x[0].rearrange("(t p) d -> p t d", p=P)).then_inc(x_loaded, 16)
                sp.dma_start(ropeq[:], rope.rearrange("c p s -> p c s")).then_inc(rope_loaded, 16)

            @block.scalar
            def _(act):
                act.dma_start(cst[:], consts).then_inc(small_loaded, 16)
                act.dma_start(len_i[:], length.partition_broadcast(P)).then_inc(small_loaded, 16)
                act.dma_start(gb[:, 0, :], g.rearrange("(c p) -> p c", p=P), allow_slow_non_contiguous=True).then_inc(small_loaded, 16)
                act.dma_start(gb[:, 1, :], b.rearrange("(c p) -> p c", p=P), allow_slow_non_contiguous=True).then_inc(small_loaded, 16)
                act.dma_start(keyb[:], keypos.partition_broadcast(P)).then_inc(small_loaded, 16)
                act.wait_ge(consts_made, 1)
                for r, (a, z) in enumerate(((0, NT), (KT, NT))):
                    act.wait_ge(moments, r + 1)
                    act.activation(std[:, r, a:z], mv[:, r, a:z, 1], ACT.Sqrt, bias=eps_col[:]).then_inc(std_made, 1)
                act.wait_ge(small_loaded, 80)
                for n, (hi, lo, d, t, k, at) in enumerate(turns):
                    act.wait_ge(turned, n + 1)
                    if n >= 2:
                        act.wait_ge(lo_made, n - 1)
                    act.activation(T32[:, n % 2, 0:k * P], tp[n % NB][:, 0:k, :], ACT.Identity,
                                   scale=gb[:, 0, d:d + 1], bias=gb[:, 1, d:d + 1]).then_inc(scaled, 1)
                    act.wait_ge(scaled, n + 1)
                    act.activation(hi[:, d, t * P:(t + k) * P], T32[:, n % 2, 0:k * P], ACT.Copy).then_inc(hi_made, 1)

            @block.vector
            def _(dve):
                dve.memset(Z[:, KT - 1, :], 0.0).then_inc(tail_clear, 1)
                dve.memset(eps_col[:], EPS).then_inc(consts_made, 1)
                dve.wait_ge(small_loaded, 80)
                dve.tensor_copy(ident_b[:], ident)
                dve.tensor_copy(len_f[:], len_i[:]).then_inc(len_made, 1)
                dve.wait_ge(len_made, 1)
                dve.tensor_scalar(valid[:], keyb[:], len_f[:, 0:1], None, ALU.is_lt).then_inc(valid_made, 1)
                dve.tensor_scalar(invalid[:], keyb[:], len_f[:, 0:1], None, ALU.is_ge)
                dve.tensor_scalar(validc[:], cst[:, P:P + KT], len_f[:, 0:1], None, ALU.is_lt)
                for r, (a, z) in enumerate(((0, NT), (KT, NT))):
                    if r == 0:
                        dve.wait_ge(ctx_loaded, 32)
                        dve.wait_ge(x_loaded, 16)
                    else:
                        dve.wait_ge(normed, 1)
                    for t in range(a, z):
                        ins = dve.bn_stats(stats[:, t, :], Z[:, t, :])
                    ins.then_inc(stats_made, 1)
                    dve.wait_ge(stats_made, r + 1)
                    for t in range(a, z):
                        ins = dve.bn_aggr(mv[:, r, t, :], stats[:, t, :])
                    ins.then_inc(moments, 1)
                    dve.wait_ge(std_made, r + 1)
                    dve.reciprocal(rstd[:, r, a:z], std[:, r, a:z]).then_inc(rstd_made, 1)
                    dve.wait_ge(rstd_made, r + 1)
                    for t in range(a, z):
                        ins = dve.tensor_scalar(Z[:, t, :], Z[:, t, :], mv[:, r, t, 0:1], rstd[:, r, t:t + 1],
                                                ALU.subtract, ALU.mult)
                    ins.then_inc(normed, 1)
                for n, (hi, lo, d, t, k, at) in enumerate(turns):
                    dve.wait_ge(hi_made, n + 1)
                    dve.tensor_tensor(lo[:, d, t * P:(t + k) * P], T32[:, n % 2, 0:k * P],
                                      hi[:, d, t * P:(t + k) * P], ALU.subtract).then_inc(lo_made, 1)

            @block.gpsimd
            def _(pool):
                pool.wait_ge(valid_made, 1)
                pool.wait_ge(rope_loaded, 16)
                for c in range(2):
                    pool.tensor_tensor(ropek[:, c, :], ropeq[:, c, 0:LP], valid[:], ALU.mult)

            @block.tensor
            def _(pe):
                pe.wait_ge(small_loaded, 80)
                pe.wait_ge(normed, 1)
                for n, (hi, lo, d, t, k, at) in enumerate(turns):
                    if at and turns[n - 1][5] == 0:
                        pe.wait_ge(normed, 2)
                    if n >= NB:
                        pe.wait_ge(scaled, n - NB + 1)
                    for j in range(k):
                        ins = pe.transpose(tp[n % NB][:, j, :], Z[:, at + t + j, d * P:(d + 1) * P], ident)
                    ins.then_inc(turned, 1)


def attend(nc, sem, maker, have):
    XH, XL, CHI, CLO, ropeq, ropek, invalid, validc, ident_b = (have[k] for k in (
        "XH", "XL", "CHI", "CLO", "ropeq", "ropek", "invalid", "validc", "ident_b"))
    w_pairs, b_pairs, bv_pairs, o_dram = (have[k] for k in ("w_pairs", "b_pairs", "bv_pairs", "o_dram"))
    length = have["length"].unsqueeze(0)
    with ExitStack() as ctx:
        sb, pb = maker(ctx)
        Q1 = [sb(f"Q1_{a}", [P, S], BF16) for a in range(2)]
        Q2 = [sb(f"Q2_{a}", [HD + 1, S], BF16) for a in range(2)]
        K1 = [sb(f"K1_{a}", [P, LP], BF16) for a in range(2)]
        K2 = [sb(f"K2_{a}", [HD + 1, LP], BF16) for a in range(2)]
        VV = [sb(f"VV_{a}", [P, KT, VW], BF16) for a in range(2)]
        next_hi = [sb("next_q_hi", [P, S], BF16), sb("next_k_hi", [P, LP], BF16)]
        next_lo = [sb("next_q_lo", [P, S], BF16), sb("next_k_lo", [P, LP], BF16)]
        next_v = sb("next_v", [P, 2, KT, VW], BF16)
        w32 = sb("w32", [P, 3, DT, P])
        w_hi = sb("w_hi", [P, 3, DT, P], BF16)
        w_lo = sb("w_lo", [P, 3, DT, P], BF16)
        bqk = sb("bqk", [P, 2])
        bvb = sb("bvb", [P, P])
        q32 = sb("q32", [P, 2, QC])
        q32s = sb("q32s", [P, 2, QC])
        by_cos = sb("by_cos", [P, QC])
        by_sin = sb("by_sin", [P, QC])
        turned_raw = sb("turned_raw", [P, QC])
        turned = sb("turned", [P, 2, QC])
        key0 = sb("key0", [P, 1])
        v32 = sb("v32", [P, 4, P])
        v32m = sb("v32m", [P, 4, P])
        prob = sb("prob", [P, PRING, 2, QC])
        prob_lo = sb("prob_lo", [P, PRING, 2, QC], BF16)
        part_max = sb("part_max", [P, 2, QT, 2])
        max_col = sb("max_col", [P, QT], BF16)
        o_raw = sb("o_raw", [P, 2, QT, VW])
        rden = sb("rden", [P, 2, QT])
        o_sum = sb("o_sum", [P, QT, HD])
        o_out = sb("o_out", [P, 2, QT, HD])

        sc = [pb(f"sc{i}", [P, QC]) for i in range(2)]
        pv = pb("pv", [P, 2, 512])
        mx = pb("mx", [P, 3, 512])
        pj = pb("pj", [P, 512])

        w_loaded = sem("w_loaded")
        w_hi_made, w_lo_made = sem("w_hi_made"), sem("w_lo_made")
        pj_ready = sem("pj_ready")
        pj_read_act, pj_read_dve = sem("pj_read_act"), sem("pj_read_dve")
        swapped = [sem("swapped0"), sem("swapped1")]
        cos_done, sin_done, raw_done, turn_done = sem("cos_done"), sem("sin_done"), sem("raw_done"), sem("turn_done")
        key0_made = sem("key0_made")
        qk_hi_made, qk_lo_made = sem("qk_hi_made"), sem("qk_lo_made")
        v_biased, v_masked, v_hi_made, v_lo_made = sem("v_biased"), sem("v_masked"), sem("v_hi_made"), sem("v_lo_made")
        q_loaded = [sem("q_loaded0"), sem("q_loaded1")]
        k_loaded = [sem("k_loaded0"), sem("k_loaded1")]
        v_loaded = [sem("v_loaded0"), sem("v_loaded1")]
        ones_made = sem("ones_made")
        scores_ready = sem("scores_ready")
        exp_done = sem("exp_done")
        lo_dve, lo_pool = sem("lo_dve"), sem("lo_pool")
        pv_done = sem("pv_done")
        part_ready = sem("part_ready")
        part_read = sem("part_read")
        max_made, col_made, row_ready, row_made = sem("max_made"), sem("col_made"), sem("row_ready"), sem("row_made")
        o_copied = sem("o_copied")
        rden_made = sem("rden_made")
        o_summed = sem("o_summed")
        o_made = sem("o_made")
        o_stored = [sem("o_stored0"), sem("o_stored1")]

        def set_of(block_):
            return block_ // CH % 2, block_ % CH

        def body(program, loop_engine):
            with loop_engine.Fori(0, PAIRS - 1) as p:
                program(p, False)
            program(PAIRS - 1, True)

        with nc.Block() as block:
            @block.tensor
            def _(pe):
                def program(pl):
                    def project(pair, u, least=0):
                        if u == 0:
                            need(pe, w_hi_made, pair, 1, 1, least)
                            need(pe, w_lo_made, pair, 1, 1, least)
                            need(pe, pj_read_dve, pair, pl.v_units, 0, least)
                        elif u <= QK_UNITS:
                            need(pe, pj_read_act, pair, QK_UNITS, u, least)
                        else:
                            need(pe, pj_read_dve, pair, pl.v_units, u - QK_UNITS, least)
                        if u < QK_UNITS:
                            kind, cols, n = pl.unit_block(u)
                            hi, lo = ((XH, XL), (CHI, CLO))[kind]
                            steps = [(w, z, d) for d in range(DT) for w, z in ((w_hi, hi), (w_hi, lo), (w_lo, hi))]
                            for j, (w, z, d) in enumerate(steps):
                                ins = pe.matmul(pj[:, 0:n], w[:, kind, d, :], z[:, d, cols], start=j == 0, stop=j == len(steps) - 1)
                        else:
                            for k, t in enumerate(pl.v_tiles(u - QK_UNITS)):
                                steps = [(z, w, d) for d in range(DT) for z, w in ((CHI, w_hi), (CHI, w_lo), (CLO, w_hi))]
                                for j, (z, w, d) in enumerate(steps):
                                    ins = pe.matmul(pj[:, k * P:(k + 1) * P], z[:, d, t * P:(t + 1) * P], w[:, 2, d, :],
                                                    start=j == 0, stop=j == len(steps) - 1)
                        ins.then_inc(pj_ready, 1)

                    def scores(p, s):
                        i, m = divmod(s, pl.groups)
                        a, c = set_of(i)
                        q = slice(c * QC, (c + 1) * QC)
                        if m == 0:
                            need(pe, row_made, p, BLOCKS, i + 1)
                        for n, t in pl.tiles_of(s):
                            k = slice(t * P, (t + 1) * P)
                            need(pe, exp_done, p, BLOCKS * pl.kt, n + 1)
                            pe.matmul(sc[n % 2][:], K1[a][:, k], Q1[a][:, q], start=True, stop=False)
                            pe.matmul(sc[n % 2][:], K2[a][:, k], Q2[a][:, q], start=False, stop=True).then_inc(scores_ready, 1)

                    def part(p, b_, qt, h):
                        a, c = set_of(b_)
                        if c == 0 and qt == 0 and h == 0:
                            need(pe, q_loaded[a], p, 48, 48 * (1 + b_ // BLOCKS))
                            need(pe, k_loaded[a], p, 48, 48 * (1 + b_ // BLOCKS))
                        if qt == 0 and h == 0:
                            need(pe, row_made, p, BLOCKS, b_)
                        need(pe, part_read, p, BLOCKS * pl.block_parts, pl.block_parts * b_ + len(pl.parts) * qt + h + 1)
                        for j, k0 in enumerate(pl.parts[h]):
                            ins = pe.matmul(mx[:, j, 0:pl.width], Q1[a][:, c * QC + qt * P:c * QC + (qt + 1) * P],
                                            K1[a][:, k0:k0 + pl.width], start=True, stop=True)
                        ins.then_inc(part_ready, 1)

                    def max_row(p, b_):
                        need(pe, col_made, p, BLOCKS, b_ + 1)
                        for qt in range(QT):
                            ins = pe.matmul(mx[0:1, 0, qt * P:(qt + 1) * P], max_col[:, qt:qt + 1], ident_b[:], start=True, stop=True)
                        ins.then_inc(row_ready, 1)

                    def times_v(p, s):
                        i, m = divmod(s, pl.groups)
                        a, _ = set_of(i)
                        if s in (0, pl.groups * CH):
                            need(pe, v_loaded[a], p, 16, 16)
                        if m == 0:
                            need(pe, o_copied, p, BLOCKS, i + 1)
                        if m in pl.dve_groups:
                            need(pe, lo_dve, p, BLOCKS * len(pl.dve_groups), i * len(pl.dve_groups) + pl.dve_groups.index(m) + 1)
                        else:
                            need(pe, lo_pool, p, BLOCKS * len(pl.pool_groups), i * len(pl.pool_groups) + pl.pool_groups.index(m) + 1)
                        for j, (n, t) in enumerate(pl.tiles_of(s)):
                            hi = hi_half(prob[:, s % PRING, j, :])
                            for qt in range(QT):
                                at = (qt % 2) * VW
                                pe.matmul(pv[:, qt // 2, at:at + VW], hi[:, 2 * qt * P + 1:2 * (qt + 1) * P:2], VV[a][:, t, :],
                                          start=t == 0 and qt % 2 == 0, stop=False, skip_group_check=True)
                                ins = pe.matmul(pv[:, qt // 2, at + HD:at + VW], prob_lo[:, s % PRING, j, qt * P:(qt + 1) * P],
                                                VV[a][:, t, HD:VW], start=False, stop=t == pl.kt - 1, skip_group_check=True)
                        ins.then_inc(pv_done, 1)

                    def slot_scores(p, s, last):
                        if not (last and s >= BLOCKS * pl.groups):
                            scores(p, s)

                    def slot(p, s, last):
                        if pl.row_block(s) is not None and not (last and pl.row_block(s) >= BLOCKS):
                            max_row(p, pl.row_block(s))
                        for n, (b_, qt, h) in enumerate(pl.parts_of(s)):
                            if not (last and b_ >= BLOCKS):
                                part(p, b_, qt, h)
                            if n == 0:
                                slot_scores(p, s, last)
                        if not pl.parts_of(s):
                            slot_scores(p, s, last)
                        if s >= LAG:
                            times_v(p, s - LAG)

                    def pair(p, last):
                        for s in range(LAG, BLOCKS * pl.groups + LAG):
                            slot(p, s, last)
                            for u in range(pl.units):
                                if not last and s == pl.hook_slot(u):
                                    project(p + 1, u, 1)

                    pe.sem_inc(pv_done, PRING)
                    for u in range(pl.units):
                        project(0, u)
                    pe.wait_ge(ones_made, 2)
                    for n in range(pl.block_parts):
                        part(0, 0, n // len(pl.parts), n % len(pl.parts))
                    max_row(0, 0)
                    for b_, qt, h in pl.parts_of(-1):
                        part(0, b_, qt, h)
                    for s in range(LAG):
                        slot(0, s, False)
                    body(pair, pe)

                for_key_count(pe, length, program)

            @block.scalar
            def _(act):
                def program(pl):
                    def load_weights(pair, least=0):
                        need(act, w_lo_made, pair, 1, 0, least)
                        act.dma_start(w32[:], w_pairs[bass.ds(pair, 1)].rearrange("a p k c n -> p (a k) c n")).then_inc(w_loaded, 16)
                        need(act, pj_read_act, pair, QK_UNITS, 0, least)
                        act.dma_start(bqk[:], b_pairs[bass.ds(pair, 1)].rearrange("a p k -> p (a k)")).then_inc(w_loaded, 16)
                        need(act, v_masked, pair, pl.v_units, 0, least)
                        act.dma_start(bvb[:], bv_pairs[bass.ds(pair, 1)].rearrange("a c -> (a c)").partition_broadcast(P)).then_inc(w_loaded, 16)

                    def split_weights(pair, least=0):
                        need(act, w_loaded, pair, 48, 48, least)
                        need(act, pj_ready, pair, pl.units, 0, least)
                        act.activation(w_hi[:], w32[:], ACT.Copy).then_inc(w_hi_made, 1)

                    def evacuate(pair, u, least=0):
                        kind, cols, n = pl.unit_block(u)
                        need(act, pj_ready, pair, pl.units, u + 1, least)
                        need(act, swapped[u % 2], pair, 64 * 4, 64 * (u // 2), least)
                        need(act, turn_done, pair, QK_UNITS, u - 1, least)
                        act.activation(q32[:, u % 2, 0:n], pj[:, 0:n], ACT.Identity,
                                       bias=bqk[:, kind:kind + 1]).then_inc(pj_read_act, 1)

                    def qk_hi(pair, u, least=0):
                        kind, cols, n = pl.unit_block(u)
                        need(act, turn_done, pair, QK_UNITS, u + 1, least)
                        if u in (0, 4):
                            for a in range(2):
                                need(act, (q_loaded, k_loaded)[kind][a], pair, 48, 0, least)
                        act.activation(next_hi[kind][:, cols], turned[:, u % 2, 0:n], ACT.Copy).then_inc(qk_hi_made, 1)

                    def v_hi(pair, v, least=0):
                        ts = pl.v_tiles(v)
                        need(act, v_masked, pair, pl.v_units, v + 1, least)
                        if v == 0:
                            for a in range(2):
                                need(act, v_loaded[a], pair, 16, 0, least)
                        for a in range(2):
                            ins = act.activation(next_v[:, a, ts[0]:ts[-1] + 1, HD:2 * HD], v32m[:, 0:len(ts), a * HD:(a + 1) * HD], ACT.Copy)
                        ins.then_inc(v_hi_made, 1)

                    def hooks(pair, k, least=0):
                        if 0 <= k - 2 < QK_UNITS:
                            qk_hi(pair, k - 2, least)
                        if 0 <= k - 1 - QK_UNITS < pl.v_units:
                            v_hi(pair, k - 1 - QK_UNITS, least)
                        if k < QK_UNITS:
                            evacuate(pair, k, least)

                    def exps(p, s):
                        need(act, pv_done, p, BLOCKS * pl.groups, s + 1)
                        for j, (n, t) in enumerate(pl.tiles_of(s)):
                            need(act, scores_ready, p, BLOCKS * pl.kt, n + 1)
                            act.activation(prob[:, s % PRING, j, :], sc[n % 2][:], ACT.Exp, scale=HD ** -0.5).then_inc(exp_done, 1)

                    def copy_out(p, i):
                        need(act, pv_done, p, BLOCKS * pl.groups, pl.groups * (i + 1) + PRING)
                        need(act, o_made, p, BLOCKS, i + 1)
                        act.activation(o_raw[:, i % 2, :, :].rearrange("p (b t) v -> p b t v", b=2),
                                       pv[:, :, 0:2 * VW].rearrange("p b (t v) -> p b t v", t=2), ACT.Copy).then_inc(o_copied, 1)

                    def max_row(p, b_):
                        a, c = set_of(b_)
                        need(act, row_ready, p, BLOCKS, b_ + 1)
                        act.activation(Q2[a][HD:HD + 1, c * QC:(c + 1) * QC], mx[0:1, 0, :], ACT.Copy, scale=-1.0).then_inc(row_made, 1)

                    def slot(p, s, last):
                        i, m = divmod(s, pl.groups)
                        if pl.row_block(s) is not None and not (last and pl.row_block(s) >= BLOCKS):
                            max_row(p, pl.row_block(s))
                        if not (last and s >= BLOCKS * pl.groups):
                            exps(p, s)
                        if m == 1 and s > pl.groups:
                            copy_out(p, i - 1)

                    def pair(p, last):
                        for s in range(LAG, BLOCKS * pl.groups + LAG):
                            slot(p, s, last)
                            if not last:
                                if s == LAG:
                                    load_weights(p + 1, 1)
                                if s == pl.groups - 1:
                                    split_weights(p + 1, 1)
                                for k in range(pl.units + 2):
                                    if s == pl.hook_slot(k):
                                        hooks(p + 1, k, 1)

                    act.sem_inc(exp_done, 2)
                    act.sem_inc(o_copied, 1)
                    load_weights(0)
                    split_weights(0)
                    for k in range(pl.units + 2):
                        hooks(0, k)
                    max_row(0, 0)
                    for s in range(LAG):
                        slot(0, s, False)
                    body(pair, act)

                for_key_count(act, length, program)

            @block.vector
            def _(dve):
                def program(pl):
                    def cosines(pair, u, least=0):
                        kind, cols, n = pl.unit_block(u)
                        need(dve, pj_read_act, pair, QK_UNITS, u + 1, least)
                        need(dve, turn_done, pair, QK_UNITS, u, least)
                        dve.tensor_tensor(by_cos[:, 0:n], q32[:, u % 2, 0:n], (ropeq, ropek)[kind][:, 0, cols], ALU.mult).then_inc(cos_done, 1)

                    def turn(pair, u, least=0):
                        kind, cols, n = pl.unit_block(u)
                        need(dve, cos_done, pair, QK_UNITS, u + 1, least)
                        need(dve, sin_done, pair, QK_UNITS, u + 1, least)
                        need(dve, qk_lo_made, pair, QK_UNITS, u - 1, least)
                        if kind == 0:
                            dve.tensor_tensor(turned[:, u % 2, 0:n], by_cos[:, 0:n], by_sin[:, 0:n], ALU.add).then_inc(turn_done, 1)
                            return
                        dve.tensor_tensor(turned_raw[:, 0:n], by_cos[:, 0:n], by_sin[:, 0:n], ALU.add).then_inc(raw_done, 1)
                        need(dve, raw_done, pair, 4, u - 4 + 1, least)
                        if u == 4:
                            dve.tensor_copy(key0[:], turned_raw[:, 0:1]).then_inc(key0_made, 1)
                            need(dve, key0_made, pair, 1, 1, least)
                        dve.scalar_tensor_tensor(out=turned[:, u % 2, 0:n], in0=invalid[:, cols], scalar=key0[:, 0:1],
                                                 in1=turned_raw[:, 0:n], op0=ALU.mult, op1=ALU.add).then_inc(turn_done, 1)

                    def v_mask(pair, v, least=0):
                        ts = pl.v_tiles(v)
                        n = len(ts)
                        need(dve, pj_ready, pair, pl.units, QK_UNITS + v + 1, least)
                        need(dve, v_lo_made, pair, pl.v_units, v, least)
                        dve.tensor_tensor(v32[:, 0:n, :], pj[:, 0:n * P].rearrange("p (t c) -> p t c", t=n),
                                          bvb[:].unsqueeze(1).to_broadcast([P, n, P]), ALU.add).then_inc(pj_read_dve, 1)
                        need(dve, pj_read_dve, pair, pl.v_units, v + 1, least)
                        dve.tensor_tensor(v32m[:, 0:n, :], v32[:, 0:n, :],
                                          validc[:, ts[0]:ts[-1] + 1].unsqueeze(2).to_broadcast([P, n, P]), ALU.mult).then_inc(v_masked, 1)

                    def v_lo(pair, v, least=0):
                        ts = pl.v_tiles(v)
                        need(dve, v_hi_made, pair, pl.v_units, v + 1, least)
                        for a in range(2):
                            ins = dve.tensor_tensor(next_v[:, a, ts[0]:ts[-1] + 1, 0:HD], v32m[:, 0:len(ts), a * HD:(a + 1) * HD],
                                                    next_v[:, a, ts[0]:ts[-1] + 1, HD:2 * HD], ALU.subtract)
                        ins.then_inc(v_lo_made, 1)

                    def hooks(pair, k, least=0):
                        if 0 <= k - 1 - QK_UNITS < pl.v_units:
                            v_lo(pair, k - 1 - QK_UNITS, least)
                        if 0 <= k - 1 < QK_UNITS:
                            cosines(pair, k - 1, least)
                        if 0 <= k - QK_UNITS < pl.v_units:
                            v_mask(pair, k - QK_UNITS, least)

                    def part(p, b_, qt, h):
                        need(dve, part_ready, p, BLOCKS * pl.block_parts, pl.block_parts * b_ + len(pl.parts) * qt + h + 1)
                        dve.tensor_reduce(part_max[:, b_ % 2, qt, h:h + 1], mx[:, 0:len(pl.parts[h]), 0:pl.width],
                                          mybir.AxisListType.XY, ALU.max).then_inc(part_read, 1)

                    def max_column(p, b_):
                        need(dve, part_read, p, BLOCKS * pl.block_parts, pl.block_parts * (b_ + 1) + 1)
                        need(dve, row_ready, p, BLOCKS, b_)
                        dve.tensor_reduce(max_col[:], part_max[:, b_ % 2, :, 0:len(pl.parts)], AX_X, ALU.max).then_inc(col_made, 1)

                    def low(p, s):
                        g = pl.gsize[s % pl.groups]
                        need(dve, exp_done, p, BLOCKS * pl.kt, pl.tiles_of(s)[-1][0] + 1 + 2)
                        dve.tensor_tensor(prob_lo[:, s % PRING, 0:g, :], prob[:, s % PRING, 0:g, :],
                                          hi_half(prob[:, s % PRING, 0:g, :])[:, :, 1::2], ALU.subtract).then_inc(lo_dve, 1)

                    def inverse(p, i):
                        need(dve, o_copied, p, BLOCKS, i + 1 + 1)
                        dve.reciprocal(rden[:, i % 2, :], o_raw[:, i % 2, :, 2 * HD]).then_inc(rden_made, 1)

                    def slot(p, s, last):
                        i, m = divmod(s, pl.groups)
                        for b_, qt, h in pl.parts_of(s):
                            if not (last and b_ >= BLOCKS):
                                part(p, b_, qt, h)
                        if pl.column_block(s) is not None and not (last and pl.column_block(s) >= BLOCKS):
                            max_column(p, pl.column_block(s))
                        if m in pl.dve_groups and not (last and s >= BLOCKS * pl.groups):
                            low(p, s)
                        if m == 1 and s > pl.groups:
                            inverse(p, i - 1)

                    def pair(p, last):
                        for s in range(LAG, BLOCKS * pl.groups + LAG):
                            slot(p, s, last)
                            if not last:
                                for k in range(pl.units + 2):
                                    if s == pl.hook_slot(k):
                                        hooks(p + 1, k, 1)
                                    if s == pl.hook_slot(k) + 1 and 0 <= k - 1 < QK_UNITS:
                                        turn(p + 1, k - 1, 1)

                    dve.sem_inc(part_read, 1)
                    for a in range(2):
                        dve.memset(K2[a][HD:HD + 1, :], 1.0).then_inc(ones_made, 1)
                        dve.tensor_copy(next_v[:, a, :, 2 * HD], validc[:])
                    for k in range(pl.units + 2):
                        hooks(0, k)
                        if 0 <= k - 1 < QK_UNITS:
                            turn(0, k - 1)
                    for n in range(pl.block_parts):
                        part(0, 0, n // len(pl.parts), n % len(pl.parts))
                    max_column(0, 0)
                    for b_, qt, h in pl.parts_of(-1):
                        part(0, b_, qt, h)
                    for s in range(LAG):
                        slot(0, s, False)
                    body(pair, dve)

                for_key_count(dve, length, program)

            @block.gpsimd
            def _(pool):
                def program(pl):
                    def split_weights(pair, least=0):
                        need(pool, w_hi_made, pair, 1, 1, least)
                        pool.tensor_tensor(w_lo[:], w32[:], w_hi[:], ALU.subtract).then_inc(w_lo_made, 1)

                    def sines(pair, u, least=0):
                        kind, cols, n = pl.unit_block(u)
                        need(pool, swapped[u % 2], pair, 64 * 4, 64 * (u // 2 + 1), least)
                        need(pool, turn_done, pair, QK_UNITS, u, least)
                        pool.tensor_tensor(by_sin[:, 0:n], q32s[:, u % 2, 0:n], (ropeq, ropek)[kind][:, 1, cols], ALU.mult).then_inc(sin_done, 1)

                    def qk_lo(pair, u, least=0):
                        kind, cols, n = pl.unit_block(u)
                        need(pool, qk_hi_made, pair, QK_UNITS, u + 1, least)
                        pool.tensor_tensor(next_lo[kind][:, cols], turned[:, u % 2, 0:n], next_hi[kind][:, cols],
                                          ALU.subtract).then_inc(qk_lo_made, 1)

                    def low(p, s):
                        g = pl.gsize[s % pl.groups]
                        need(pool, exp_done, p, BLOCKS * pl.kt, pl.tiles_of(s)[-1][0] + 1 + 2)
                        pool.tensor_tensor(prob_lo[:, s % PRING, 0:g, :], prob[:, s % PRING, 0:g, :],
                                           hi_half(prob[:, s % PRING, 0:g, :])[:, :, 1::2], ALU.subtract).then_inc(lo_pool, 1)

                    def hooks(pair, k, least=0):
                        if 0 <= k - 2 < QK_UNITS:
                            qk_lo(pair, k - 2, least)
                        if 0 <= k - 1 < QK_UNITS:
                            sines(pair, k - 1, least)

                    def output(p, i):
                        need(pool, rden_made, p, BLOCKS, i + 1)
                        pool.tensor_tensor(o_sum[:], o_raw[:, i % 2, :, 0:HD], o_raw[:, i % 2, :, HD:2 * HD], ALU.add).then_inc(o_summed, 1)
                        need(pool, o_summed, p, BLOCKS, i + 1)
                        need(pool, o_stored[i % 2], p, 16 * BLOCKS // 2, 16 * (i // 2 + 1))
                        pool.tensor_tensor(o_out[:, i % 2, :, :], o_sum[:], rden[:, i % 2, :].unsqueeze(2).to_broadcast([P, QT, HD]),
                                           ALU.mult).then_inc(o_made, 1)

                    def slot(p, s, last):
                        i, m = divmod(s, pl.groups)
                        if m in pl.pool_groups and not (last and s >= BLOCKS * pl.groups):
                            low(p, s)
                        if m == 1 and s > pl.groups:
                            output(p, i - 1)

                    def pair(p, last):
                        for s in range(LAG, BLOCKS * pl.groups + LAG):
                            slot(p, s, last)
                            if not last:
                                if s == pl.groups - 1:
                                    split_weights(p + 1, 1)
                                for k in range(pl.units + 2):
                                    if s == pl.hook_slot(k):
                                        hooks(p + 1, k, 1)

                    pool.sem_inc(o_made, 2)
                    split_weights(0)
                    for k in range(pl.units + 2):
                        hooks(0, k)
                    for s in range(LAG):
                        slot(0, s, False)
                    body(pair, pool)

                for_key_count(pool, length, program)

            @block.sync
            def _(sp):
                def program(pl):
                    def swap(pair, u, least=0):
                        kind, cols, n = pl.unit_block(u)
                        need(sp, pj_read_act, pair, QK_UNITS, u + 1, least)
                        for h in range(2):
                            for k in range(2):
                                a, z = HD * h + 32 * k, HD * h + 32 * (1 - k)
                                sp.dma_start(q32s[a:a + 32, u % 2, 0:n], q32[z:z + 32, u % 2, 0:n]).then_inc(swapped[u % 2], 16)

                    def load_q(pair, a):
                        need(sp, qk_lo_made, pair, QK_UNITS, 4, 0 if isinstance(pair, int) else 1)
                        r = slice(a * HD, (a + 1) * HD)
                        sp.dma_start(Q1[a][0:HD, :], next_hi[0][r, :]).then_inc(q_loaded[a], 16)
                        sp.dma_start(Q1[a][HD:P, :], next_hi[0][r, :]).then_inc(q_loaded[a], 16)
                        sp.dma_start(Q2[a][0:HD, :], next_lo[0][r, :]).then_inc(q_loaded[a], 16)

                    def load_k(pair, a):
                        need(sp, qk_lo_made, pair, QK_UNITS, 8, 0 if isinstance(pair, int) else 1)
                        n = pl.kt * P
                        r = slice(a * HD, (a + 1) * HD)
                        sp.dma_start(K1[a][0:HD, 0:n], next_hi[1][r, 0:n]).then_inc(k_loaded[a], 16)
                        sp.dma_start(K1[a][HD:P, 0:n], next_lo[1][r, 0:n]).then_inc(k_loaded[a], 16)
                        sp.dma_start(K2[a][0:HD, 0:n], next_hi[1][r, 0:n]).then_inc(k_loaded[a], 16)

                    def load_v(pair, a):
                        need(sp, v_lo_made, pair, pl.v_units, pl.v_units, 0 if isinstance(pair, int) else 1)
                        sp.dma_start(VV[a][:, 0:pl.kt, :], next_v[:, a, 0:pl.kt, :]).then_inc(v_loaded[a], 16)

                    def store(p, i):
                        a, c = set_of(i)
                        need(sp, o_made, p, BLOCKS, i + 1 + 2)
                        rows = o_dram[c * QC:(c + 1) * QC, :].rearrange("(t p) d -> p t d", p=P)
                        sp.dma_start(rows[:, :, bass.ds(p * P + a * HD, HD)], o_out[:, i % 2, :, :]).then_inc(o_stored[i % 2], 16)

                    def pair(p, last):
                        for s in range(LAG, BLOCKS * pl.groups + LAG):
                            if s % pl.groups == 1 and s > pl.groups:
                                store(p, s // pl.groups - 1)
                            if last:
                                continue
                            for u in range(QK_UNITS):
                                if s == pl.hook_slot(u):
                                    swap(p + 1, u, 1)
                            if s == pl.hook_slot(6) + 1:
                                load_q(p + 1, 0)
                            if s == pl.hook_slot(9) + 1:
                                load_k(p + 1, 0)
                            if s == pl.hook_slot(12) + 1:
                                load_v(p + 1, 0)
                        if not last:
                            load_q(p + 1, 1)
                            load_k(p + 1, 1)
                            load_v(p + 1, 1)

                    for i in range(2):
                        sp.sem_inc(o_stored[i], 16)
                    for u in range(QK_UNITS):
                        swap(0, u)
                    for a in range(2):
                        load_q(0, a)
                        load_k(0, a)
                    for a in range(2):
                        load_v(0, a)
                    body(pair, sp)
                    for i in range(2):
                        sp.wait_ge(o_stored[i], 16 + 16 * PAIRS * BLOCKS // 2)

                for_key_count(sp, length, program)


def experts(nc, sem, maker, have):
    x, wo, bo, gate, w_exp, o_dram, out = (have[k] for k in ("x", "wo", "bo", "gate", "w_exp", "o_dram", "out"))
    ident, ident_b, eps_col, rank8 = (have[k] for k in ("ident", "ident_b", "eps_col", "rank8"))
    with ExitStack() as both:
        sb, _ = maker(both)
        x1 = sb("x1", [P, ST, D])
        YH = sb("YH", [P, DT, S], BF16)
        YL = sb("YL", [P, DT, S], BF16)
        logits = sb("logits", [P, ST, E])
        project_out(nc, sem, maker, locals())
        mixture(nc, sem, maker, locals())


def project_out(nc, sem, maker, have):
    x, wo, bo, gate, o_dram, ident, eps_col, x1, YH, YL, logits = (have[k] for k in (
        "x", "wo", "bo", "gate", "o_dram", "ident", "eps_col", "x1", "YH", "YL", "logits"))
    J = H * HD // P
    with ExitStack() as ctx:
        sb, pb = maker(ctx)
        o_in = sb("o_in", [P, 2, J * P])
        OH = sb("OH", [P, 2, J, P], BF16)
        OL = sb("OL", [P, 2, J, P], BF16)
        wo32 = sb("wo32", [P, J, D])
        wo_hi = sb("wo_hi", [P, J, D], BF16)
        wo_lo = sb("wo_lo", [P, J, D], BF16)
        bob = sb("bob", [P, D])
        gate_sb = sb("gate_sb", [P, DT, E])
        stats = sb("stats2", [P, 2, 6])
        mv = sb("mv2", [P, 2, 2])
        std = sb("std2", [P, 2])
        rstd = sb("rstd2", [P, 2])
        normed = sb("normed2", [P, 2, D])
        YF = sb("YF", [P, 2, DT, P])
        ot = [pb(f"ot{i}", [P, 2, 4, P]) for i in range(2)]
        wp = [pb(f"wp{i}", [P, 512]) for i in range(2)]
        yt = pb("yt", [P, 4, P])
        gp = pb("gp", [P, 512])

        o_loaded = [sem("o_loaded0"), sem("o_loaded1")]
        in_loaded, wo_loaded = sem("in_loaded"), sem("wo_loaded")
        wo_hi_made, wo_lo_made = sem("wo_hi_made"), sem("wo_lo_made")
        bias_added = sem("bias_added")
        ot_ready, oh_made, ol_made = sem("ot_ready"), sem("oh_made"), sem("ol_made")
        wp_ready, x1_made, st_made, mv_made, sd_made, rs_made, nm_made = (sem(n) for n in (
            "wp_ready", "x1_made", "st_made", "mv_made", "sd_made", "rs_made", "nm_made"))
        yt_ready, yh_made, yl_made, gp_ready, gp_read = (sem(n) for n in ("yt_ready", "yh_made", "yl_made", "gp_ready", "gp_read"))

        STEPS = ST + 4

        with nc.Block() as block:
            @block.sync
            def _(sp):
                sp.dma_start(wo32[:], wo.rearrange("(j p) d -> p j d", p=P)).then_inc(wo_loaded, 16)
                for t in range(ST):
                    if t >= 2:
                        sp.wait_ge(ot_ready, t - 1)
                    sp.dma_start(o_in[:, t % 2, :], o_dram[t * P:(t + 1) * P, :]).then_inc(o_loaded[t % 2], 16)

            @block.scalar
            def _(act):
                act.dma_start(x1[:], x[0].rearrange("(t p) d -> p t d", p=P)).then_inc(in_loaded, 16)
                act.dma_start(bob[:], bo.partition_broadcast(P)).then_inc(in_loaded, 16)
                act.dma_start(gate_sb[:], gate).then_inc(in_loaded, 16)
                act.wait_ge(wo_loaded, 16)
                act.activation(wo_hi[:], wo32[:], ACT.Copy).then_inc(wo_hi_made, 1)
                for step in range(STEPS):
                    t = step
                    if t < ST:
                        act.wait_ge(ot_ready, t + 1)
                        if t >= 2:
                            act.wait_ge(wp_ready, t - 1)
                        act.activation(OH[:, t % 2, :, :], ot[t % 2][:].rearrange("p b k c -> p (b k) c"), ACT.Copy).then_inc(oh_made, 1)
                    t = step - 1
                    if 0 <= t < ST:
                        act.wait_ge(mv_made, t + 1)
                        act.activation(std[:, t % 2:t % 2 + 1], mv[:, t % 2, 1:2], ACT.Sqrt, bias=eps_col[:]).then_inc(sd_made, 1)
                    t = step - 3
                    if 0 <= t < ST:
                        act.wait_ge(yt_ready, t + 1)
                        if t >= 2:
                            act.wait_ge(gp_ready, t - 1)
                        act.activation(YF[:, t % 2, :, :], yt[:, 0:DT, :], ACT.Copy)
                        act.activation(YH[:, :, t * P:(t + 1) * P], yt[:, 0:DT, :], ACT.Copy).then_inc(yh_made, 1)

            @block.gpsimd
            def _(pool):
                pool.wait_ge(wo_hi_made, 1)
                pool.tensor_tensor(wo_lo[:], wo32[:], wo_hi[:], ALU.subtract).then_inc(wo_lo_made, 1)
                pool.wait_ge(in_loaded, 48)
                pool.tensor_tensor(x1[:], x1[:], bob[:].unsqueeze(1).to_broadcast([P, ST, D]), ALU.add).then_inc(bias_added, 1)

            @block.vector
            def _(dve):
                for step in range(STEPS):
                    t = step
                    if t < ST:
                        dve.wait_ge(oh_made, t + 1)
                        dve.tensor_tensor(OL[:, t % 2, :, :], ot[t % 2][:].rearrange("p b k c -> p (b k) c"), OH[:, t % 2, :, :],
                                          ALU.subtract).then_inc(ol_made, 1)
                    t = step - 1
                    if 0 <= t < ST:
                        if t == 0:
                            dve.wait_ge(bias_added, 1)
                        dve.wait_ge(wp_ready, t + 1)
                        dve.tensor_tensor(x1[:, t, :], wp[t % 2][:, 0:D], x1[:, t, :], ALU.add).then_inc(x1_made, 1)
                        dve.wait_ge(x1_made, t + 1)
                        dve.bn_stats(stats[:, t % 2, :], x1[:, t, :]).then_inc(st_made, 1)
                        dve.wait_ge(st_made, t + 1)
                        dve.bn_aggr(mv[:, t % 2, :], stats[:, t % 2, :]).then_inc(mv_made, 1)
                    t = step - 2
                    if 0 <= t < ST:
                        dve.wait_ge(sd_made, t + 1)
                        dve.reciprocal(rstd[:, t % 2:t % 2 + 1], std[:, t % 2:t % 2 + 1]).then_inc(rs_made, 1)
                        dve.wait_ge(rs_made, t + 1)
                        if t >= 2:
                            dve.wait_ge(yt_ready, t - 1)
                        dve.tensor_scalar(normed[:, t % 2, :], x1[:, t, :], mv[:, t % 2, 0:1], rstd[:, t % 2:t % 2 + 1],
                                          ALU.subtract, ALU.mult).then_inc(nm_made, 1)
                    t = step - 3
                    if 0 <= t < ST:
                        dve.wait_ge(yh_made, t + 1)
                        dve.tensor_tensor(YL[:, :, t * P:(t + 1) * P], yt[:, 0:DT, :], YH[:, :, t * P:(t + 1) * P],
                                          ALU.subtract).then_inc(yl_made, 1)
                    t = step - 4
                    if 0 <= t < ST:
                        dve.wait_ge(gp_ready, t + 1)
                        dve.tensor_copy(logits[:, t, :], gp[:, 0:E]).then_inc(gp_read, 1)

            @block.tensor
            def _(pe):
                for step in range(STEPS):
                    t = step
                    if t < ST:
                        pe.wait_ge(o_loaded[t % 2], 16 * (t // 2 + 1))
                        if t >= 2:
                            pe.wait_ge(ol_made, t - 1)
                        for j in range(J):
                            ins = pe.transpose(ot[t % 2][:, j // 4, j % 4, :], o_in[:, t % 2, j * P:(j + 1) * P], ident)
                        ins.then_inc(ot_ready, 1)
                    t = step - 1
                    if 0 <= t < ST:
                        if t == 0:
                            pe.wait_ge(wo_lo_made, 1)
                        pe.wait_ge(ol_made, t + 1)
                        if t >= 2:
                            pe.wait_ge(x1_made, t - 1)
                        steps = [(z, w, j) for j in range(J) for z, w in ((OH, wo_hi), (OH, wo_lo), (OL, wo_hi))]
                        for n, (z, w, j) in enumerate(steps):
                            ins = pe.matmul(wp[t % 2][:, 0:D], z[:, t % 2, j, :], w[:, j, :], start=n == 0, stop=n == len(steps) - 1)
                        ins.then_inc(wp_ready, 1)
                    t = step - 3
                    if 0 <= t < ST:
                        pe.wait_ge(nm_made, t + 1)
                        if t >= 1:
                            pe.wait_ge(yl_made, t)
                        for d in range(DT):
                            ins = pe.transpose(yt[:, d, :], normed[:, t % 2, d * P:(d + 1) * P], ident)
                        ins.then_inc(yt_ready, 1)
                    t = step - 4
                    if 0 <= t < ST:
                        pe.wait_ge(yh_made, t + 1)
                        if t >= 1:
                            pe.wait_ge(gp_read, t)
                        for d in range(DT):
                            ins = pe.matmul(gp[:, 0:E], YF[:, t % 2, d, :], gate_sb[:, d, :], start=d == 0, stop=d == DT - 1)
                        ins.then_inc(gp_ready, 1)


def mixture(nc, sem, maker, have):
    w_exp, out, x1, YH, YL, logits, rank8 = (have[k] for k in ("w_exp", "out", "x1", "YH", "YL", "logits", "rank8"))
    WC = 2 * DT * FF + FT * D
    ITS = 2 * CH
    TT = QC // P
    Q = FT
    with ExitStack() as ctx:
        sb, pb = maker(ctx)
        w32 = sb("we32", [P, WC])
        w_hi = sb("we_hi", [P, 2, WC], BF16)
        w_lo = sb("we_lo", [P, 2, WC], BF16)
        gates = sb("gates", [P, ST, E])
        gcur = sb("gcur", [P, ST, 2])
        g8 = [sb(f"g8_{i}", [P, ST, E]) for i in range(3)]
        pick = [sb(f"pick{i}", [P, ST, E]) for i in range(2)]
        top = sb("top", [P, 4, ST])
        ew = sb("ew", [P, 4, ST])
        act_s = sb("act_s", [P, 2, QC])
        hid = sb("hid", [P, 2, FT, QC])
        hid_lo = sb("hid_lo", [P, 2, FT, QC], BF16)
        pa = [pb(f"pa{i}", [P, QC]) for i in range(2)]
        pg = [pb(f"pg{i}", [P, QC]) for i in range(2)]
        py = [pb(f"py{i}", [P, 2, D]) for i in range(4)]

        we_loaded, we_hi_made, we_lo_made = sem("we_loaded"), sem("we_hi_made"), sem("we_lo_made")
        up_ready = sem("up_ready")
        silu_made = sem("silu_made")
        hid_made = sem("hid_made")
        lo_made = sem("hid_lo_made")
        down_ready = sem("down_ready")
        added = sem("added")
        routed, picked, exp_made, gates_made, gcur_made = (sem(n) for n in ("routed", "picked", "exp_made", "gates_made", "gcur_made"))
        stored = sem("stored")

        def w13(which, e, d, f):
            at = (which * DT + d) * FF + f * P
            return slice(at, at + P)

        def w2(f):
            at = 2 * DT * FF + f * D
            return slice(at, at + D)

        def body(program, engine):
            with engine.Fori(0, E // 2 - 1) as q:
                program(q, False)
            program(E // 2 - 1, True)

        SLOTS = range(Q, Q * (ITS + 1))

        def downs_of(z):
            for i in range(ITS):
                for k in range(2):
                    if z == Q * i + 5 + 2 * k:
                        return i, k

        with nc.Block() as block:
            @block.sync
            def _(sp):
                def load(e, least=0):
                    need(sp, we_lo_made, e, 1, 0, least)
                    sp.dma_start(w32[:], w_exp[bass.ds(e, 1)].rearrange("a p c -> p (a c)")).then_inc(we_loaded, 16)

                def two(q, last):
                    load(2 * q + 1, 1)
                    if not last:
                        load(2 * q + 2, 1)

                load(0)
                body(two, sp)
                for c in range(CH):
                    sp.wait_ge(added, 4 + (E - 1) * 2 * CH + 2 * (c + 1))
                    sp.dma_start(out[0, c * QC:(c + 1) * QC, :].rearrange("(t p) d -> p t d", p=P),
                                 x1[:, c * TT:(c + 1) * TT, :]).then_inc(stored, 16)
                sp.wait_ge(stored, 16 * CH)

            @block.scalar
            def _(act):
                def silu(q, z):
                    need(act, up_ready, q, ITS * Q, z + 1)
                    need(act, hid_made, q, ITS * Q, z + 1)
                    act.activation(act_s[:, z % 2, :], pa[z % 2][:], ACT.Silu).then_inc(silu_made, 1)

                def two(q, last):
                    for z in SLOTS:
                        if z == Q + 2:
                            need(act, we_loaded, q, 32, 32)
                            need(act, down_ready, q, ITS * 2, 4)
                            act.activation(w_hi[:, 1, :], w32[:], ACT.Copy).then_inc(we_hi_made, 1)
                        if z == Q * (CH + 1) + 2 and not last:
                            need(act, we_loaded, q, 32, 48)
                            need(act, down_ready, q, ITS * 2, 4 + 2 * CH)
                            act.activation(w_hi[:, 0, :], w32[:], ACT.Copy).then_inc(we_hi_made, 1)
                        if not (last and z >= Q * ITS):
                            silu(q, z)

                act.wait_ge(routed, 1)
                act.activation(ew[:, 0, :], top[:, 2, :], ACT.Exp).then_inc(exp_made, 1)
                act.wait_ge(we_loaded, 16)
                act.activation(w_hi[:, 0, :], w32[:], ACT.Copy).then_inc(we_hi_made, 1)
                for z in range(Q):
                    silu(0, z)
                body(two, act)

            @block.gpsimd
            def _(pool):
                def split(q, slot, count):
                    need(pool, we_hi_made, q, 2, count)
                    pool.tensor_tensor(w_lo[:, slot, :], w32[:], w_hi[:, slot, :], ALU.subtract).then_inc(we_lo_made, 1)

                def low(q, z):
                    i, f = divmod(z, Q)
                    need(pool, hid_made, q, ITS * Q, z + 1 + 2)
                    pool.tensor_tensor(hid_lo[:, i % 2, f, :], hid[:, i % 2, f, :], hi_half(hid[:, i % 2, f, :])[:, 1::2],
                                       ALU.subtract).then_inc(lo_made, 1)

                def two(q, last):
                    for z in SLOTS:
                        if z == Q + 2:
                            split(q, 1, 2)
                        if z == Q * (CH + 1) + 2 and not last:
                            split(q, 0, 3)
                        if not (last and z >= Q * ITS):
                            low(q, z)

                split(0, 0, 1)
                for z in range(Q):
                    low(0, z)
                body(two, pool)

            @block.vector
            def _(dve):
                def route():
                    chain = [0]

                    def then(ins):
                        chain[0] += 1
                        ins.then_inc(picked, 1)
                        dve.wait_ge(picked, chain[0])

                    ranks = rank8.unsqueeze(1).to_broadcast([P, ST, E])
                    left = logits
                    for k in range(2):
                        def wide(row):
                            return top[:, row, :].unsqueeze(2).to_broadcast([P, ST, E])
                        then(dve.tensor_reduce(top[:, k, :], left[:], AX_X, ALU.max))
                        then(dve.tensor_tensor(g8[0][:], left[:], wide(k), ALU.is_ge))
                        then(dve.tensor_tensor(g8[1][:], g8[0][:], ranks, ALU.mult))
                        then(dve.tensor_reduce(top[:, 3, :], g8[1][:], AX_X, ALU.max))
                        then(dve.tensor_tensor(pick[k][:], g8[1][:], wide(3), ALU.is_equal))
                        if k == 0:
                            then(dve.scalar_tensor_tensor(out=g8[2][:], in0=pick[0][:], scalar=-3e38, in1=logits[:],
                                                          op0=ALU.mult, op1=ALU.add))
                            left = g8[2]
                    dve.tensor_tensor(top[:, 2, :], top[:, 1, :], top[:, 0, :], ALU.subtract).then_inc(routed, 1)
                    dve.wait_ge(exp_made, 1)
                    then(dve.tensor_scalar(ew[:, 1, :], ew[:, 0, :], 1.0, None, ALU.add))
                    then(dve.reciprocal(ew[:, 2, :], ew[:, 1, :]))
                    then(dve.tensor_tensor(ew[:, 3, :], ew[:, 0, :], ew[:, 2, :], ALU.mult))
                    for k in range(2):
                        then(dve.tensor_tensor(g8[k][:], pick[k][:], ew[:, 2 + k, :].unsqueeze(2).to_broadcast([P, ST, E]), ALU.mult))
                    dve.tensor_tensor(gates[:], g8[0][:], g8[1][:], ALU.add).then_inc(gates_made, 1)
                    dve.wait_ge(gates_made, 1)

                def hidden(q, z):
                    i, f = divmod(z, Q)
                    need(dve, silu_made, q, ITS * Q, z + 1)
                    need(dve, down_ready, q, ITS * 2, 2 * (i - 1) + 4)
                    dve.tensor_tensor(hid[:, i % 2, f, :], act_s[:, z % 2, :], pg[z % 2][:], ALU.mult).then_inc(hid_made, 1)

                def add(q, i, k):
                    c = i % CH
                    need(dve, down_ready, q, ITS * 2, 2 * i + k + 1 + 4)
                    for j in range(2):
                        t = c * TT + 2 * k + j
                        ins = dve.scalar_tensor_tensor(out=x1[:, t, :], in0=py[(2 * i + k) % 4][:, j, :], scalar=gcur[:, t, i // CH:i // CH + 1],
                                                       in1=x1[:, t, :], op0=ALU.mult, op1=ALU.add)
                    ins.then_inc(added, 1)

                def two(q, last):
                    need(dve, added, q, ITS * 2, 4)
                    dve.tensor_copy(gcur[:], gates[:, :, bass.ds(2 * q, 2)]).then_inc(gcur_made, 1)
                    need(dve, gcur_made, q, 1, 1)
                    for z in SLOTS:
                        if not (last and z >= Q * ITS):
                            hidden(q, z)
                        if downs_of(z - 1):
                            add(q, *downs_of(z - 1))
                    add(q, *downs_of(SLOTS[-1]))

                dve.sem_inc(hid_made, 2)
                dve.sem_inc(added, 4)
                route()
                for z in range(Q):
                    hidden(0, z)
                body(two, dve)

            @block.tensor
            def _(pe):
                def up(q, z):
                    i, f = divmod(z, Q)
                    slot, c = i // CH % 2, i % CH
                    if f == 0 and c == 0:
                        need(pe, we_lo_made, q, 2, i // CH + 1)
                    need(pe, hid_made, q, ITS * Q, z + 1)
                    for which, bank in ((0, pa), (1, pg)):
                        steps = [(w, y, d) for d in range(DT) for w, y in ((w_hi, YH), (w_hi, YL), (w_lo, YH))]
                        for n, (w, y, d) in enumerate(steps):
                            ins = pe.matmul(bank[z % 2][:], w[:, slot, w13(which, i, d, f)], y[:, d, c * QC:(c + 1) * QC],
                                            start=n == 0, stop=n == len(steps) - 1)
                    ins.then_inc(up_ready, 1)

                def down(q, i, k):
                    slot = i // CH % 2
                    bank = (2 * i + k) % 4
                    need(pe, added, q, ITS * 2, 2 * i + k + 1)
                    need(pe, lo_made, q, ITS * Q, Q * (i + 1))
                    for j in range(2):
                        tok = slice((2 * k + j) * P, (2 * k + j + 1) * P)
                        for f in range(FT):
                            hi = hi_half(hid[:, i % 2, f, :])[:, 2 * tok.start + 1:2 * tok.stop:2]
                            for n, (z, w) in enumerate(((hi, w_hi), (hi, w_lo), (hid_lo[:, i % 2, f, tok], w_hi))):
                                ins = pe.matmul(py[bank][:, j, :], z, w[:, slot, w2(f)], start=f == 0 and n == 0,
                                                stop=f == FT - 1 and n == 2)
                    ins.then_inc(down_ready, 1)

                def two(q, last):
                    for z in SLOTS:
                        if not (last and z >= Q * ITS):
                            up(q, z)
                        if downs_of(z):
                            down(q, *downs_of(z))

                pe.sem_inc(down_ready, 4)
                for z in range(Q):
                    up(0, z)
                body(two, pe)


_INS = ["x", "ctx_1024", "_lenS2", "L0_xattn_ln_g", "L0_xattn_ln_b", "w_pairs", "b_pairs", "bv_pairs", "L0_xattn_Wo",
        "L0_xattn_bo", "gate", "w_exp", "rope", "keypos", "consts"]


def kernel(**inputs):
    import numpy as np
    import concourse.bacc as bacc
    from concourse.bass_utils import run_bass_kernel_spmd

    a = {k: np.asarray(v) for k, v in inputs.items()}
    order = np.concatenate([np.arange(0, HD, 2), np.arange(1, HD, 2)])
    cols = (np.arange(H)[:, None] * HD + order[None, :]).reshape(-1)

    def by_pair(w):
        return w.reshape(DT, P, PAIRS, P).transpose(2, 1, 0, 3)

    a["w_pairs"] = np.stack([by_pair(a["L0_xattn_Wq"][:, cols]), by_pair(a["L0_xattn_Wk"][:, cols]),
                             by_pair(a["L0_xattn_Wv"])], axis=2)
    a["b_pairs"] = np.stack([a["L0_xattn_bq"][cols].reshape(PAIRS, P), a["L0_xattn_bk"][cols].reshape(PAIRS, P)], axis=2)
    a["bv_pairs"] = a["L0_xattn_bv"].reshape(PAIRS, P)
    a["gate"] = a["L0_ffn_gate_w"].T.reshape(DT, P, E).transpose(1, 0, 2)

    def by_rows(w):
        return w.reshape(E, -1, P, w.shape[2]).transpose(0, 2, 1, 3).reshape(E, P, -1)

    a["w_exp"] = np.concatenate([by_rows(a["L0_ffn_w1"].transpose(0, 2, 1)), by_rows(a["L0_ffn_w3"].transpose(0, 2, 1)),
                                 by_rows(a["L0_ffn_w2"].transpose(0, 2, 1))], axis=2)
    inv = (np.float32(1) / np.power(10000.0, np.arange(0, HD, 2) / HD)).astype(np.float32)
    angle = (np.arange(S, dtype=np.float32)[None, :] * inv[:, None]).astype(np.float64)
    a["rope"] = np.stack([np.tile(np.cos(angle), (4, 1)),
                          np.tile(np.concatenate([-np.sin(angle), np.sin(angle)]), (2, 1))]).astype(np.float32)
    key = np.arange(LP, dtype=np.float32)
    key[L:] = 1e9
    a["keypos"] = key
    a["consts"] = np.concatenate([np.eye(P, dtype=np.float32), key.reshape(KT, P).T,
                                  np.tile(np.arange(E, 0, -1, dtype=np.float32), (P, 1))], axis=1)

    nc = bacc.Bacc("TRN2", target_bir_lowering=False, num_devices=1)
    arrays, args = {}, []
    for name in _INS:
        v = np.ascontiguousarray(a[name])
        arrays[f"in_{name}"] = v
        args.append(nc.dram_tensor(f"in_{name}", v.shape, mybir.dt.from_np(v.dtype), kind="ExternalInput").ap())
    out = nc.dram_tensor("out", [1, S, D], F32, kind="ExternalOutput").ap()
    build(nc, *args, out)
    r = run_bass_kernel_spmd(nc, [arrays], core_ids=[0])
    return r.results[0]["out"]
```

```python
from contextlib import ExitStack

import concourse.bass as bass
from concourse import mybir

P = 128
F32 = mybir.dt.float32
BF16 = mybir.dt.bfloat16
I32 = mybir.dt.int32
U32 = mybir.dt.uint32
ALU = mybir.AluOpType
ACT = mybir.ActivationFunctionType
AX_X = mybir.AxisListType.X

S, D, H, HD = 2048, 256, 16, 64
L = 1601
E, FF = 8, 512
EPS = 1e-5
DT = D // P
KT = -(-L // P)
LP = KT * P
ST = S // P
PAIRS = H // 2
QC = 512
CH = S // QC
QT = QC // P
VW = 2 * HD + 1
BLOCKS = 2 * CH
LAG = 2
PRING = 4
QK_UNITS = 8
FT = FF // P
WC = 2 * DT * FF + FT * D
MT = (2 * S + E * (P - 1)) // P
KEY_TILES = (10, 11, 12, 13)


class Plan:

    def __init__(self, kt):
        self.kt = kt
        self.gsize = [2] * (kt // 2) + [1] * (kt % 2)
        self.groups = len(self.gsize)
        self.pool_groups = (1, self.groups // 2 + 1)
        self.dve_groups = tuple(m for m in range(self.groups) if m not in self.pool_groups)
        self.kc = kt * P // 4
        self.v_units = -(-kt // 4)
        self.units = QK_UNITS + self.v_units
        if kt * P <= 3 * 512:
            self.width = -(-kt * P // 3)
            self.parts = [[min(j * self.width, kt * P - self.width)] for j in range(3)]
            self.part_slots = 3
        else:
            self.width = -(-L // 4)
            self.parts = [[2 * h * self.width, (2 * h + 1) * self.width] for h in range(2)]
            self.part_slots = 1
        self.block_parts = QT * len(self.parts)
        order = [m % self.groups for m in range(-2, self.groups - 2)]
        each = [self.block_parts // self.groups] * self.groups
        for j in sorted(range(self.groups), key=lambda j: order[j] not in self.pool_groups)[:self.block_parts % self.groups]:
            each[j] += 1
        self.parts_at = [list(range(sum(each[:j]), sum(each[:j + 1]))) for j in range(self.groups)]

    def tiles_of(self, s):
        i, m = divmod(s, self.groups)
        return [(self.kt * i + 2 * m + j, 2 * m + j) for j in range(self.gsize[m])]

    def parts_of(self, s):
        i, m = divmod(s, self.groups)
        ahead, at = (2, m - self.groups + 2) if m >= self.groups - 2 else (1, m + 2)
        return [(i + ahead, n // len(self.parts), n % len(self.parts)) for n in self.parts_at[at]]

    def part_banks(self, qt, h):
        n = len(self.parts[h])
        first = (len(self.parts) * qt + h) % self.part_slots * n
        return range(first, first + n)

    def column_block(self, s):
        i, m = divmod(s, self.groups)
        return i + 1 if m == self.groups - 3 else None

    def row_block(self, s):
        i, m = divmod(s, self.groups)
        return i + 1 if m == self.groups - 2 else None

    def hook_slot(self, k):
        return self.groups * (1 + k // 2) + (0, 2)[k % 2]

    def v_tiles(self, v):
        return range(4 * v, min(4 * v + 4, self.kt))

    def unit_block(self, u):
        kind, c = divmod(u, 4)
        n = (QC, self.kc)[kind]
        return kind, slice(c * n, (c + 1) * n), n


def for_key_count(engine, length, program):
    count = engine.value_load(length)

    def choose(plans):
        if len(plans) == 1:
            program(Plan(plans[0]))
            return
        with engine.If(count <= plans[0] * P):
            program(Plan(plans[0]))
        with engine.Else():
            choose(plans[1:])

    choose(KEY_TILES)


def need(eng, sem, index, per, count, least=0):
    if isinstance(index, int):
        if per * index + count > 0:
            eng.wait_ge(sem, per * index + count)
    else:
        assert per * least + count > 0
        eng.wait_ge(sem, index * per + count)


def hi_half(ap):
    return ap.bitcast(BF16)


def build(nc, x, ctx_in, length, g, b, w_pairs, b_pairs, bv_cols, wo, bo, gate, w_exp, rope, keypos, consts, out):
    o_dram = nc.dram_tensor("attention_out", [S, H * HD], F32, kind="Internal").ap()
    x_slots = nc.dram_tensor("expert_inputs", [MT * P, 2 * D], BF16, kind="Internal").ap()
    y_slots = nc.dram_tensor("expert_outputs", [MT * P, D], F32, kind="Internal").ap()

    with ExitStack() as whole:
        def sem(name):
            return whole.enter_context(nc.semaphore(name))

        def maker(stack):
            def sb(name, shape, dt=F32):
                return stack.enter_context(nc.sbuf_tensor(name, shape, dt))

            def pb(name, shape, dt=F32):
                return stack.enter_context(nc.psum_tensor(name, shape, dt))
            return sb, pb

        sb, _ = maker(whole)
        cst = sb("cst", [P, 2 * P + KT + E + E * E + ST + MT])
        zeroed = sem("slots_zeroed")
        zeros = sb("zeros", [P, 2 * D], BF16)
        ident_b = sb("ident_b", [P, P], BF16)
        eps_col = sb("eps_col", [P, 1])
        wo_hi = sb("wo_hi", [P, H * HD // P, D], BF16)
        wo_lo = sb("wo_lo", [P, H * HD // P, D], BF16)
        bob = sb("bob", [P, D])
        ident = cst[:, 0:P]
        rank8 = cst[:, P + KT:P + KT + 8]

        with ExitStack() as upto_attend:
            sb, _ = maker(upto_attend)
            XH = sb("XH", [P, DT, S], BF16)
            XL = sb("XL", [P, DT, S], BF16)
            CHI = sb("CHI", [P, DT, LP], BF16)
            CLO = sb("CLO", [P, DT, LP], BF16)
            ropeq = sb("ropeq", [P, 2, S])
            ropek = sb("ropek", [P, 2, LP])
            invalid = sb("invalid", [P, LP], BF16)
            validc = sb("validc", [P, KT])
            w32 = sb("w32", [P, 3, DT, P])
            w_hi = sb("w_hi", [P, 3, DT, P], BF16)
            w_lo = sb("w_lo", [P, 3, DT, P], BF16)
            bqk = sb("bqk", [P, 2])
            w_loaded, w_hi_made, w_lo_made = sem("w_loaded"), sem("w_hi_made"), sem("w_lo_made")
            prepare(nc, sem, maker, locals())
            attend(nc, sem, maker, locals())
        experts(nc, sem, maker, locals())


def prepare(nc, sem, maker, have):
    x, ctx_in, length, g, b = (have[k] for k in ("x", "ctx_in", "length", "g", "b"))
    rope, keypos, consts, cst = (have[k] for k in ("rope", "keypos", "consts", "cst"))
    x_slots, y_slots, zeros, zeroed = (have[k] for k in ("x_slots", "y_slots", "zeros", "zeroed"))
    wo, bo, w_pairs, b_pairs, bv_cols, wo_hi, wo_lo, bob = (have[k] for k in (
        "wo", "bo", "w_pairs", "b_pairs", "bv_cols", "wo_hi", "wo_lo", "bob"))
    w32, w_hi, w_lo, bqk, w_loaded, w_hi_made, w_lo_made = (have[k] for k in (
        "w32", "w_hi", "w_lo", "bqk", "w_loaded", "w_hi_made", "w_lo_made"))
    XH, XL, CHI, CLO, ropeq, ropek, invalid, validc, ident_b, eps_col, ident = (have[k] for k in (
        "XH", "XL", "CHI", "CLO", "ropeq", "ropek", "invalid", "validc", "ident_b", "eps_col", "ident"))
    NT = KT + ST
    with ExitStack() as ctx:
        sb, pb = maker(ctx)
        Z = sb("Z", [P, NT, D])
        keyb = sb("keyb", [P, LP])
        valid = sb("valid", [P, LP])
        len_i = sb("len_i", [P, 1], I32)
        len_f = sb("len_f", [P, 1])
        gb = sb("gb", [P, 2, DT])
        rounds = [(0, KT), (KT, NT), (KT, NT)]
        GN = 4
        groups = [(r, t, min(t + GN, z)) for r, (a, z) in enumerate(rounds) for t in range(a, z, GN)]
        NG = len(groups)
        C_GROUPS = sum(r == 0 for r, _, _ in groups)
        stats = sb("stats", [P, NG, GN, 6])
        mv = sb("mv", [P, NG, GN, 2])
        std = sb("std", [P, NG, GN])
        rstd = sb("rstd", [P, NG, GN])
        shift = sb("shift", [P, C_GROUPS, GN])
        NB = 4
        NS = 4
        T32 = sb("T32", [P, NS, 512])
        wo32 = sb("wo32", [P, H * HD // P, D])
        bo_b = sb("bo_b", [P, D])
        bv = sb("bv", [P, H * HD // P])
        bias_bank = pb("bias_bank", [P, 512])
        tp = [pb(f"tp{i}", [P, 4, P]) for i in range(NB)]

        ctx_loaded = sem("ctx_loaded")
        x_loaded = sem("x_loaded")
        small_loaded = sem("small_loaded")
        gb_loaded = sem("gb_loaded")
        keys_loaded = sem("keys_loaded")
        rope_loaded = sem("rope_loaded")
        wo_loaded, wo_hi_made, bias_ready = sem("wo_loaded"), sem("wo_hi_made"), sem("bias_ready")
        masked = sem("masked")
        tail_clear = sem("tail_clear")
        consts_made = sem("consts_made")
        stats_made = sem("stats_made")
        moments = sem("moments")
        std_made = sem("std_made")
        rstd_made = sem("rstd_made")
        shift_made = sem("shift_made")
        ctx_normed = sem("ctx_normed")
        x_normed = sem("x_normed")
        valid_made = sem("valid_made")
        len_made = sem("len_made")
        zeros_made = sem("zeros_made")
        turned = sem("turned")
        scaled = sem("scaled")
        hi_made = sem("hi_made")
        lo_made = sem("lo_made")

        turns = [(CHI, CLO, d, t, min(4, KT - t), 0) for t in range(0, KT, 4) for d in range(DT)]
        turns += [(XH, XL, d, t, min(4, ST - t), KT) for t in range(0, ST, 4) for d in range(DT)]
        C_TURNS = sum(at == 0 for *_, at in turns)

        with nc.Block() as block:
            @block.sync
            def _(sp):
                full = (L // P) * P
                sp.dma_start(Z[:, 0:L // P, :], ctx_in[0, 0:full, :].rearrange("(t p) d -> p t d", p=P)).then_inc(ctx_loaded, 16)
                sp.wait_ge(tail_clear, 1)
                sp.dma_start(Z[0:L - full, KT - 1, :], ctx_in[0, full:L, :]).then_inc(ctx_loaded, 16)
                sp.dma_start(Z[:, KT:NT, :], x[0].rearrange("(t p) d -> p t d", p=P)).then_inc(x_loaded, 16)
                sp.dma_start(w32[:], w_pairs[0].rearrange("p k c n -> p k c n")).then_inc(w_loaded, 16)
                sp.dma_start(bqk[:], b_pairs[0]).then_inc(w_loaded, 16)
                sp.dma_start(keyb[:], keypos.partition_broadcast(P)).then_inc(keys_loaded, 16)
                sp.dma_start(ropeq[:], rope.rearrange("c p s -> p c s")).then_inc(rope_loaded, 16)
                sp.dma_start(wo32[:], wo.rearrange("(j p) d -> p j d", p=P)).then_inc(wo_loaded, 16)
                sp.dma_start(bo_b[:], bo.partition_broadcast(P)).then_inc(wo_loaded, 16)
                sp.dma_start(bv[:], bv_cols).then_inc(wo_loaded, 16)
                sp.wait_ge(zeros_made, 1)
                sp.dma_start(x_slots.rearrange("(t p) c -> p t c", p=P),
                             zeros[:].unsqueeze(1).to_broadcast([P, MT, 2 * D])).then_inc(zeroed, 16)
                sp.dma_start(y_slots.rearrange("(t p) c -> p t c", p=P),
                             zeros[:].bitcast(F32).unsqueeze(1).to_broadcast([P, MT, D])).then_inc(zeroed, 16)

            @block.scalar
            def _(act):
                act.dma_start(cst[:], consts).then_inc(small_loaded, 16)
                act.dma_start(len_i[:], length.partition_broadcast(P)).then_inc(small_loaded, 16)
                act.dma_start(gb[:, 0, :], g.rearrange("(c p) -> p c", p=P), allow_slow_non_contiguous=True).then_inc(gb_loaded, 16)
                act.dma_start(gb[:, 1, :], b.rearrange("(c p) -> p c", p=P), allow_slow_non_contiguous=True).then_inc(gb_loaded, 16)
                act.wait_ge(consts_made, 1)

                def root(r):
                    act.wait_ge(moments, r + 1)
                    gs = [n for n, group in enumerate(groups) if group[0] == r]
                    act.activation(std[:, gs[0]:gs[-1] + 1, :], mv[:, gs[0]:gs[-1] + 1, :, 1], ACT.Sqrt, bias=eps_col[:]).then_inc(std_made, 1)

                def scale(n):
                    hi, lo, d, t, k, at = turns[n]
                    act.wait_ge(turned, n + 1)
                    if n >= NS:
                        act.wait_ge(lo_made, n - NS + 1)
                    act.activation(T32[:, n % NS, 0:k * P], tp[n % NB][:, 0:k, :], ACT.Identity,
                                   scale=gb[:, 0, d:d + 1], bias=gb[:, 1, d:d + 1]).then_inc(scaled, 1)

                def high(n):
                    hi, lo, d, t, k, at = turns[n]
                    if n < C_TURNS:
                        act.wait_ge(masked, n + 1)
                    else:
                        act.wait_ge(scaled, n + 1)
                    act.activation(hi[:, d, t * P:(t + k) * P], T32[:, n % NS, 0:k * P], ACT.Copy).then_inc(hi_made, 1)

                root(0)
                act.wait_ge(shift_made, 1)
                for n, (r, t, z) in enumerate(groups[:C_GROUPS]):
                    for j in range(t, z):
                        ins = act.activation(Z[:, j, :], Z[:, j, :], ACT.Identity, scale=rstd[:, n, j - t:j - t + 1],
                                             bias=shift[:, n, j - t:j - t + 1])
                    ins.then_inc(ctx_normed, 1)
                act.wait_ge(gb_loaded, 32)
                scale(0)
                scale(1)
                root(1)
                for n in range(2, C_TURNS):
                    scale(n)
                    high(n - 2)
                high(C_TURNS - 2)
                high(C_TURNS - 1)
                root(2)
                scale(C_TURNS)
                for n in range(C_TURNS + 1, len(turns)):
                    scale(n)
                    high(n - 1)
                high(len(turns) - 1)

            @block.vector
            def _(dve):
                dve.memset(Z[:, KT - 1, :], 0.0).then_inc(tail_clear, 1)
                dve.memset(mv[:], 1.0).then_inc(len_made, 1)
                dve.memset(eps_col[:], EPS).then_inc(consts_made, 1)
                dve.wait_ge(len_made, 1)

                def moments_of(r):
                    mine = [(n, t, z) for n, (rr, t, z) in enumerate(groups) if rr == r]
                    for n, t, z in mine:
                        if r == 2:
                            dve.wait_ge(x_normed, n - C_GROUPS - len(mine) + 1)
                        for j in range(t, z):
                            ins = dve.bn_stats(stats[:, n, j - t, :], Z[:, j, :])
                    ins.then_inc(stats_made, 1)
                    dve.wait_ge(stats_made, r + 1)
                    for n, t, z in mine:
                        for j in range(t, z):
                            ins = dve.bn_aggr(mv[:, n, j - t, :], stats[:, n, j - t, :])
                    ins.then_inc(moments, 1)

                def reciprocals(r):
                    gs = [n for n, group in enumerate(groups) if group[0] == r]
                    dve.wait_ge(std_made, r + 1)
                    dve.reciprocal(rstd[:, gs[0]:gs[-1] + 1, :], std[:, gs[0]:gs[-1] + 1, :]).then_inc(rstd_made, 1)
                    dve.wait_ge(rstd_made, r + 1)

                def normalise(r):
                    for n, (rr, t, z) in enumerate(groups):
                        if rr == r:
                            for j in range(t, z):
                                ins = dve.tensor_scalar(Z[:, j, :], Z[:, j, :], mv[:, n, j - t, 0:1], rstd[:, n, j - t:j - t + 1],
                                                        ALU.subtract, ALU.mult)
                            ins.then_inc(x_normed, 1)

                def mask(n):
                    hi, lo, d, t, k, at = turns[n]
                    dve.wait_ge(scaled, n + 1)
                    dve.tensor_tensor(T32[:, n % NS, 0:k * P], T32[:, n % NS, 0:k * P], valid[:, t * P:(t + k) * P],
                                      ALU.mult).then_inc(masked, 1)

                def low(n):
                    hi, lo, d, t, k, at = turns[n]
                    dve.wait_ge(hi_made, n + 1)
                    dve.tensor_tensor(lo[:, d, t * P:(t + k) * P], T32[:, n % NS, 0:k * P],
                                      hi[:, d, t * P:(t + k) * P], ALU.subtract).then_inc(lo_made, 1)

                dve.wait_ge(ctx_loaded, 32)
                moments_of(0)
                dve.wait_ge(small_loaded, 32)
                dve.tensor_copy(ident_b[:], ident)
                dve.tensor_copy(len_f[:], len_i[:]).then_inc(len_made, 1)
                reciprocals(0)
                dve.scalar_tensor_tensor(out=shift[:], in0=mv[:, 0:C_GROUPS, :, 0], scalar=-1.0, in1=rstd[:, 0:C_GROUPS, :],
                                         op0=ALU.mult, op1=ALU.mult).then_inc(shift_made, 1)
                dve.wait_ge(x_loaded, 16)
                moments_of(1)
                reciprocals(1)
                normalise(1)
                dve.wait_ge(valid_made, 1)
                mask(0)
                mask(1)
                moments_of(2)
                for n in range(2, C_TURNS):
                    mask(n)
                    low(n - 2)
                low(C_TURNS - 2)
                low(C_TURNS - 1)
                reciprocals(2)
                normalise(2)
                for n in range(C_TURNS, len(turns)):
                    low(n)
                dve.wait_ge(bias_ready, 1)
                dve.tensor_tensor(bob[:], bias_bank[:, 0:D], bo_b[:], ALU.add)

            @block.gpsimd
            def _(pool):
                pool.memset(zeros[:], 0.0).then_inc(zeros_made, 1)
                pool.wait_ge(keys_loaded, 16)
                pool.wait_ge(len_made, 2)
                pool.tensor_scalar(valid[:], keyb[:], len_f[:, 0:1], None, ALU.is_lt).then_inc(valid_made, 1)
                pool.tensor_scalar(invalid[:], keyb[:], len_f[:, 0:1], None, ALU.is_ge)
                pool.tensor_scalar(validc[:], cst[:, P:P + KT], len_f[:, 0:1], None, ALU.is_lt)
                pool.wait_ge(w_loaded, 32)
                pool.tensor_copy(w_hi[:], w32[:]).then_inc(w_hi_made, 1)
                pool.wait_ge(w_hi_made, 1)
                pool.tensor_tensor(w_lo[:], w32[:], w_hi[:], ALU.subtract).then_inc(w_lo_made, 1)
                pool.wait_ge(valid_made, 1)
                pool.wait_ge(rope_loaded, 16)
                for c in range(2):
                    pool.tensor_tensor(ropek[:, c, :], ropeq[:, c, 0:LP], valid[:], ALU.mult)
                pool.wait_ge(wo_loaded, 48)
                pool.tensor_copy(wo_hi[:], wo32[:]).then_inc(wo_hi_made, 1)
                pool.wait_ge(wo_hi_made, 1)
                pool.tensor_tensor(wo_lo[:], wo32[:], wo_hi[:], ALU.subtract)

            @block.tensor
            def _(pe):
                pe.wait_ge(small_loaded, 32)
                for n, (hi, lo, d, t, k, at) in enumerate(turns):
                    if n == C_TURNS:
                        pe.wait_ge(wo_loaded, 48)
                        J = H * HD // P
                        for j in range(J):
                            ins = pe.matmul(bias_bank[:, 0:D], bv[:, j:j + 1].to_broadcast([P, P]), wo32[:, j, :],
                                            start=j == 0, stop=j == J - 1)
                        ins.then_inc(bias_ready, 1)
                    if at == 0:
                        pe.wait_ge(ctx_normed, t // 4 + 1)
                    else:
                        pe.wait_ge(x_normed, NG - C_GROUPS - ST // 4 + t // 4 + 1)
                    if n >= NB:
                        pe.wait_ge(scaled, n - NB + 1)
                    for j in range(k):
                        ins = pe.transpose(tp[n % NB][:, j, :], Z[:, at + t + j, d * P:(d + 1) * P], ident)
                    ins.then_inc(turned, 1)


def attend(nc, sem, maker, have):
    XH, XL, CHI, CLO, ropeq, ropek, invalid, validc, ident_b = (have[k] for k in (
        "XH", "XL", "CHI", "CLO", "ropeq", "ropek", "invalid", "validc", "ident_b"))
    w_pairs, b_pairs, o_dram = (have[k] for k in ("w_pairs", "b_pairs", "o_dram"))
    w32, w_hi, w_lo, bqk, w_loaded, w_hi_made, w_lo_made = (have[k] for k in (
        "w32", "w_hi", "w_lo", "bqk", "w_loaded", "w_hi_made", "w_lo_made"))
    length = have["length"].unsqueeze(0)
    with ExitStack() as ctx:
        sb, pb = maker(ctx)
        Q1 = [sb(f"Q1_{a}", [P, S], BF16) for a in range(2)]
        Q2 = [sb(f"Q2_{a}", [HD + 1, S], BF16) for a in range(2)]
        K1 = [sb(f"K1_{a}", [P, LP], BF16) for a in range(2)]
        K2 = [sb(f"K2_{a}", [HD + 1, LP], BF16) for a in range(2)]
        VV = [sb(f"VV_{a}", [P, KT, VW], BF16) for a in range(2)]
        next_hi = [sb("next_q_hi", [P, S], BF16), sb("next_k_hi", [P, LP], BF16)]
        next_lo = [sb("next_q_lo", [P, S], BF16), sb("next_k_lo", [P, LP], BF16)]
        next_v = sb("next_v", [P, 2, KT, VW], BF16)
        q32 = sb("q32", [P, 4, QC])
        q32s = sb("q32s", [P, 4, QC])
        by_cos = sb("by_cos", [P, QC])
        by_sin = sb("by_sin", [P, QC])
        turned_raw = sb("turned_raw", [P, QC])
        turned = sb("turned", [P, 2, QC])
        key0 = sb("key0", [P, 1])
        prob = sb("prob", [P, PRING, 2, QC])
        prob_lo = sb("prob_lo", [P, PRING, 2, QC], BF16)
        part_max = sb("part_max", [P, 2, QT, 3])
        max_col = sb("max_col", [P, QT], BF16)
        o_raw = sb("o_raw", [P, 2, QT, VW])
        rden = sb("rden", [P, 2, QT])
        o_sum = sb("o_sum", [P, QT, HD])
        o_out = sb("o_out", [P, 2, QT, HD])

        sc = [pb(f"sc{i}", [P, QC]) for i in range(2)]
        pv = pb("pv", [P, 2, 512])
        mx = pb("mx", [P, 3, 512])
        pj = pb("pj", [P, 512])

        pj_ready = sem("pj_ready")
        pj_read_act = sem("pj_read_act")
        swapped = [sem(f"swapped{i}") for i in range(4)]
        cos_done, sin_done, raw_done, turn_done = sem("cos_done"), sem("sin_done"), sem("raw_done"), sem("turn_done")
        key0_made = sem("key0_made")
        qk_hi_made, qk_lo_made = sem("qk_hi_made"), sem("qk_lo_made")
        v_hi_made, v_lo_made = sem("v_hi_made"), sem("v_lo_made")
        q_loaded = [sem("q_loaded0"), sem("q_loaded1")]
        k_loaded = [sem("k_loaded0"), sem("k_loaded1")]
        v_loaded = [sem("v_loaded0"), sem("v_loaded1")]
        ones_made = sem("ones_made")
        scores_ready = sem("scores_ready")
        exp_done = sem("exp_done")
        lo_dve, lo_pool = sem("lo_dve"), sem("lo_pool")
        pv_done = sem("pv_done")
        part_ready = sem("part_ready")
        part_read = sem("part_read")
        col_made, row_ready, row_made = sem("col_made"), sem("row_ready"), sem("row_made")
        o_copied = sem("o_copied")
        rden_made = sem("rden_made")
        o_summed = sem("o_summed")
        o_made = sem("o_made")
        o_stored = [sem("o_stored0"), sem("o_stored1")]

        def set_of(block_):
            return block_ // CH % 2, block_ % CH

        def body(program, loop_engine):
            with loop_engine.Fori(0, PAIRS - 1) as p:
                program(p, False)
            program(PAIRS - 1, True)

        with nc.Block() as block:
            @block.tensor
            def _(pe):
                def program(pl):
                    def project(pair, u, least=0):
                        if u == 0:
                            need(pe, w_hi_made, pair, 1, 1, least)
                            need(pe, w_lo_made, pair, 1, 1, least)
                            need(pe, v_lo_made, pair, pl.v_units, 0, least)
                        elif u <= QK_UNITS:
                            need(pe, pj_read_act, pair, QK_UNITS, u, least)
                        else:
                            need(pe, v_lo_made, pair, pl.v_units, u - QK_UNITS, least)
                        if u < QK_UNITS:
                            kind, cols, n = pl.unit_block(u)
                            hi, lo = ((XH, XL), (CHI, CLO))[kind]
                            steps = [(w, z, d) for d in range(DT) for w, z in ((w_hi, hi), (w_hi, lo), (w_lo, hi))]
                            for j, (w, z, d) in enumerate(steps):
                                ins = pe.matmul(pj[:, 0:n], w[:, kind, d, :], z[:, d, cols], start=j == 0, stop=j == len(steps) - 1)
                        else:
                            for k, t in enumerate(pl.v_tiles(u - QK_UNITS)):
                                steps = [(z, w, d) for d in range(DT) for z, w in ((CHI, w_hi), (CHI, w_lo), (CLO, w_hi))]
                                for j, (z, w, d) in enumerate(steps):
                                    ins = pe.matmul(pj[:, k * P:(k + 1) * P], z[:, d, t * P:(t + 1) * P], w[:, 2, d, :],
                                                    start=j == 0, stop=j == len(steps) - 1)
                        ins.then_inc(pj_ready, 1)

                    def scores(p, s):
                        i, m = divmod(s, pl.groups)
                        a, c = set_of(i)
                        q = slice(c * QC, (c + 1) * QC)
                        if m == 0:
                            need(pe, row_made, p, BLOCKS, i + 1)
                        for n, t in pl.tiles_of(s):
                            k = slice(t * P, (t + 1) * P)
                            need(pe, exp_done, p, BLOCKS * pl.kt, n + 1)
                            pe.matmul(sc[n % 2][:], K1[a][:, k], Q1[a][:, q], start=True, stop=False)
                            pe.matmul(sc[n % 2][:], K2[a][:, k], Q2[a][:, q], start=False, stop=True).then_inc(scores_ready, 1)

                    def part(p, b_, qt, h):
                        a, c = set_of(b_)
                        if c == 0 and qt == 0 and h == 0:
                            need(pe, q_loaded[a], p, 48, 48 * (1 + b_ // BLOCKS))
                            need(pe, k_loaded[a], p, 48, 48 * (1 + b_ // BLOCKS))
                        if qt == 0 and h == 0:
                            need(pe, row_made, p, BLOCKS, b_)
                        need(pe, part_read, p, BLOCKS * pl.block_parts, pl.block_parts * b_ + len(pl.parts) * qt + h + 1)
                        for bank, k0 in zip(pl.part_banks(qt, h), pl.parts[h]):
                            ins = pe.matmul(mx[:, bank, 0:pl.width], Q1[a][:, c * QC + qt * P:c * QC + (qt + 1) * P],
                                            K1[a][:, k0:k0 + pl.width], start=True, stop=True)
                        ins.then_inc(part_ready, 1)

                    def max_row(p, b_):
                        need(pe, col_made, p, BLOCKS, b_ + 1)
                        for qt in range(QT):
                            ins = pe.matmul(mx[0:1, 0, qt * P:(qt + 1) * P], max_col[:, qt:qt + 1], ident_b[:], start=True, stop=True)
                        ins.then_inc(row_ready, 1)

                    def times_v(p, s):
                        i, m = divmod(s, pl.groups)
                        a, _ = set_of(i)
                        if s in (0, pl.groups * CH):
                            need(pe, v_loaded[a], p, 16, 16)
                        if m == 0:
                            need(pe, o_copied, p, BLOCKS, i + 1)
                        if m in pl.dve_groups:
                            need(pe, lo_dve, p, BLOCKS * len(pl.dve_groups), i * len(pl.dve_groups) + pl.dve_groups.index(m) + 1)
                        else:
                            need(pe, lo_pool, p, BLOCKS * len(pl.pool_groups), i * len(pl.pool_groups) + pl.pool_groups.index(m) + 1)
                        for j, (n, t) in enumerate(pl.tiles_of(s)):
                            hi = hi_half(prob[:, s % PRING, j, :])
                            for qt in range(QT):
                                at = (qt % 2) * VW
                                pe.matmul(pv[:, qt // 2, at:at + VW], hi[:, 2 * qt * P + 1:2 * (qt + 1) * P:2], VV[a][:, t, :],
                                          start=t == 0 and qt % 2 == 0, stop=False, skip_group_check=True)
                                ins = pe.matmul(pv[:, qt // 2, at + HD:at + VW], prob_lo[:, s % PRING, j, qt * P:(qt + 1) * P],
                                                VV[a][:, t, HD:VW], start=False, stop=t == pl.kt - 1, skip_group_check=True)
                        ins.then_inc(pv_done, 1)

                    def slot_scores(p, s, last):
                        if not (last and s >= BLOCKS * pl.groups):
                            scores(p, s)

                    def slot(p, s, last):
                        if pl.row_block(s) is not None and not (last and pl.row_block(s) >= BLOCKS):
                            max_row(p, pl.row_block(s))
                        behind = pl.row_block(s) is not None
                        if behind:
                            slot_scores(p, s, last)
                        for n, (b_, qt, h) in enumerate(pl.parts_of(s)):
                            if not (last and b_ >= BLOCKS):
                                part(p, b_, qt, h)
                            if n == 0 and not behind:
                                slot_scores(p, s, last)
                        if s >= LAG:
                            times_v(p, s - LAG)

                    def pair(p, last):
                        for s in range(LAG, BLOCKS * pl.groups + LAG):
                            slot(p, s, last)
                            for u in range(pl.units):
                                if not last and s == pl.hook_slot(u):
                                    project(p + 1, u, 1)

                    pe.sem_inc(pv_done, PRING)
                    for u in range(pl.units):
                        project(0, u)
                    pe.wait_ge(ones_made, 2)
                    for n in range(pl.block_parts):
                        part(0, 0, n // len(pl.parts), n % len(pl.parts))
                    max_row(0, 0)
                    for b_, qt, h in pl.parts_of(-2) + pl.parts_of(-1):
                        part(0, b_, qt, h)
                    for s in range(LAG):
                        slot(0, s, False)
                    body(pair, pe)

                for_key_count(pe, length, program)

            @block.scalar
            def _(act):
                def program(pl):
                    def load_weights(pair, least=0):
                        need(act, w_lo_made, pair, 1, 0, least)
                        act.dma_start(w32[:], w_pairs[bass.ds(pair, 1)].rearrange("a p k c n -> p (a k) c n")).then_inc(w_loaded, 16)
                        need(act, pj_read_act, pair, QK_UNITS, 0, least)
                        act.dma_start(bqk[:], b_pairs[bass.ds(pair, 1)].rearrange("a p k -> p (a k)")).then_inc(w_loaded, 16)

                    def split_weights(pair, least=0):
                        need(act, w_loaded, pair, 32, 32, least)
                        need(act, pj_ready, pair, pl.units, 0, least)
                        act.activation(w_hi[:], w32[:], ACT.Copy).then_inc(w_hi_made, 1)

                    def evacuate(pair, u, least=0):
                        kind, cols, n = pl.unit_block(u)
                        need(act, pj_ready, pair, pl.units, u + 1, least)
                        need(act, swapped[u % 4], pair, 64 * 2, 64 * (u // 4), least)
                        need(act, turn_done, pair, QK_UNITS, u - 3, least)
                        act.activation(q32[:, u % 4, 0:n], pj[:, 0:n], ACT.Identity,
                                       bias=bqk[:, kind:kind + 1]).then_inc(pj_read_act, 1)

                    def qk_hi(pair, u, least=0):
                        kind, cols, n = pl.unit_block(u)
                        need(act, turn_done, pair, QK_UNITS, u + 1, least)
                        if u in (0, 4):
                            for a in range(2):
                                need(act, (q_loaded, k_loaded)[kind][a], pair, 48, 0, least)
                        act.activation(next_hi[kind][:, cols], turned[:, u % 2, 0:n], ACT.Copy).then_inc(qk_hi_made, 1)

                    def v_hi(pair, v, least=0):
                        ts = pl.v_tiles(v)
                        need(act, pj_ready, pair, pl.units, QK_UNITS + v + 1, least)
                        if v == 0:
                            for a in range(2):
                                need(act, v_loaded[a], pair, 16, 0, least)
                        for a in range(2):
                            ins = act.activation(next_v[:, a, ts[0]:ts[-1] + 1, HD:2 * HD],
                                                 pj[:, 0:len(ts) * P].rearrange("p (t c) -> p t c", c=P)[:, :, a * HD:(a + 1) * HD], ACT.Copy)
                        ins.then_inc(v_hi_made, 1)

                    def hooks(pair, k, least=0):
                        if 0 <= k - 2 < QK_UNITS:
                            qk_hi(pair, k - 2, least)
                        if 0 <= k - QK_UNITS < pl.v_units:
                            v_hi(pair, k - QK_UNITS, least)
                        if k < QK_UNITS:
                            evacuate(pair, k, least)

                    def exps(p, s):
                        need(act, pv_done, p, BLOCKS * pl.groups, s + 1)
                        for j, (n, t) in enumerate(pl.tiles_of(s)):
                            need(act, scores_ready, p, BLOCKS * pl.kt, n + 1)
                            act.activation(prob[:, s % PRING, j, :], sc[n % 2][:], ACT.Exp, scale=HD ** -0.5).then_inc(exp_done, 1)

                    def copy_out(p, i):
                        need(act, pv_done, p, BLOCKS * pl.groups, pl.groups * (i + 1) + PRING)
                        need(act, o_made, p, BLOCKS, i + 1)
                        act.activation(o_raw[:, i % 2, :, :].rearrange("p (b t) v -> p b t v", b=2),
                                       pv[:, :, 0:2 * VW].rearrange("p b (t v) -> p b t v", t=2), ACT.Copy).then_inc(o_copied, 1)

                    def max_row(p, b_):
                        a, c = set_of(b_)
                        need(act, row_ready, p, BLOCKS, b_ + 1)
                        act.activation(Q2[a][HD:HD + 1, c * QC:(c + 1) * QC], mx[0:1, 0, :], ACT.Copy, scale=-1.0).then_inc(row_made, 1)

                    def slot(p, s, last):
                        i, m = divmod(s, pl.groups)
                        if pl.row_block(s) is not None and not (last and pl.row_block(s) >= BLOCKS):
                            max_row(p, pl.row_block(s))
                        if not (last and s >= BLOCKS * pl.groups):
                            exps(p, s)
                        if m == 1 and s > pl.groups:
                            copy_out(p, i - 1)

                    def pair(p, last):
                        for s in range(LAG, BLOCKS * pl.groups + LAG):
                            slot(p, s, last)
                            if not last:
                                if s == LAG:
                                    load_weights(p + 1, 1)
                                if s == pl.groups - 1:
                                    split_weights(p + 1, 1)
                                for k in range(pl.units + 2):
                                    if s == pl.hook_slot(k):
                                        hooks(p + 1, k, 1)

                    act.sem_inc(exp_done, 2)
                    act.sem_inc(o_copied, 1)
                    for k in range(pl.units + 1):
                        if k < QK_UNITS:
                            evacuate(0, k)
                        if 0 <= k - QK_UNITS < pl.v_units:
                            v_hi(0, k - QK_UNITS)
                        if 0 <= k - 3 < QK_UNITS:
                            qk_hi(0, k - 3)
                    max_row(0, 0)
                    for s in range(LAG):
                        slot(0, s, False)
                    body(pair, act)

                for_key_count(act, length, program)

            @block.vector
            def _(dve):
                def program(pl):
                    def cosines(pair, u, least=0):
                        kind, cols, n = pl.unit_block(u)
                        need(dve, pj_read_act, pair, QK_UNITS, u + 1, least)
                        need(dve, turn_done, pair, QK_UNITS, u, least)
                        dve.tensor_tensor(by_cos[:, 0:n], q32[:, u % 4, 0:n], (ropeq, ropek)[kind][:, 0, cols], ALU.mult).then_inc(cos_done, 1)

                    def turn(pair, u, least=0):
                        kind, cols, n = pl.unit_block(u)
                        need(dve, cos_done, pair, QK_UNITS, u + 1, least)
                        need(dve, sin_done, pair, QK_UNITS, u + 1, least)
                        need(dve, qk_lo_made, pair, QK_UNITS, u - 1, least)
                        if kind == 0:
                            dve.tensor_tensor(turned[:, u % 2, 0:n], by_cos[:, 0:n], by_sin[:, 0:n], ALU.add).then_inc(turn_done, 1)
                            return
                        dve.tensor_tensor(turned_raw[:, 0:n], by_cos[:, 0:n], by_sin[:, 0:n], ALU.add).then_inc(raw_done, 1)
                        need(dve, raw_done, pair, 4, u - 4 + 1, least)
                        if u == 4:
                            dve.tensor_copy(key0[:], turned_raw[:, 0:1]).then_inc(key0_made, 1)
                            need(dve, key0_made, pair, 1, 1, least)
                        dve.scalar_tensor_tensor(out=turned[:, u % 2, 0:n], in0=invalid[:, cols], scalar=key0[:, 0:1],
                                                 in1=turned_raw[:, 0:n], op0=ALU.mult, op1=ALU.add).then_inc(turn_done, 1)

                    def v_lo(pair, v, least=0):
                        ts = pl.v_tiles(v)
                        need(dve, v_hi_made, pair, pl.v_units, v + 1, least)
                        for a in range(2):
                            ins = dve.tensor_tensor(next_v[:, a, ts[0]:ts[-1] + 1, 0:HD],
                                                    pj[:, 0:len(ts) * P].rearrange("p (t c) -> p t c", c=P)[:, :, a * HD:(a + 1) * HD],
                                                    next_v[:, a, ts[0]:ts[-1] + 1, HD:2 * HD], ALU.subtract)
                        ins.then_inc(v_lo_made, 1)

                    def hooks(pair, k, least=0):
                        if 0 <= k - 1 < QK_UNITS:
                            cosines(pair, k - 1, least)

                    def part(p, b_, qt, h):
                        need(dve, part_ready, p, BLOCKS * pl.block_parts, pl.block_parts * b_ + len(pl.parts) * qt + h + 1)
                        dve.tensor_reduce(part_max[:, b_ % 2, qt, h:h + 1], mx[:, pl.part_banks(qt, h)[0]:pl.part_banks(qt, h)[-1] + 1, 0:pl.width],
                                          mybir.AxisListType.XY, ALU.max).then_inc(part_read, 1)

                    def max_column(p, b_):
                        need(dve, part_read, p, BLOCKS * pl.block_parts, pl.block_parts * (b_ + 1) + pl.part_slots)
                        need(dve, row_ready, p, BLOCKS, b_)
                        dve.tensor_reduce(max_col[:], part_max[:, b_ % 2, :, 0:len(pl.parts)], AX_X, ALU.max).then_inc(col_made, 1)

                    def low(p, s):
                        g = pl.gsize[s % pl.groups]
                        need(dve, exp_done, p, BLOCKS * pl.kt, pl.tiles_of(s)[-1][0] + 1 + 2)
                        dve.tensor_tensor(prob_lo[:, s % PRING, 0:g, :], prob[:, s % PRING, 0:g, :],
                                          hi_half(prob[:, s % PRING, 0:g, :])[:, :, 1::2], ALU.subtract).then_inc(lo_dve, 1)

                    def inverse(p, i):
                        need(dve, o_copied, p, BLOCKS, i + 1 + 1)
                        dve.reciprocal(rden[:, i % 2, :], o_raw[:, i % 2, :, 2 * HD]).then_inc(rden_made, 1)

                    def slot(p, s, last):
                        i, m = divmod(s, pl.groups)
                        for b_, qt, h in pl.parts_of(s):
                            if not (last and b_ >= BLOCKS):
                                part(p, b_, qt, h)
                        if pl.column_block(s) is not None and not (last and pl.column_block(s) >= BLOCKS):
                            max_column(p, pl.column_block(s))
                        if m in pl.dve_groups and not (last and s >= BLOCKS * pl.groups):
                            low(p, s)
                        if m == 1 and s > pl.groups:
                            inverse(p, i - 1)

                    def pair(p, last):
                        for s in range(LAG, BLOCKS * pl.groups + LAG):
                            slot(p, s, last)
                            if not last:
                                for k in range(pl.units + 2):
                                    if s == pl.hook_slot(k):
                                        hooks(p + 1, k, 1)
                                    if s == pl.hook_slot(k) + 1 and 0 <= k - 1 < QK_UNITS:
                                        turn(p + 1, k - 1, 1)
                                    if s == pl.hook_slot(k) + 1 and 0 <= k - QK_UNITS < pl.v_units:
                                        v_lo(p + 1, k - QK_UNITS, 1)

                    dve.sem_inc(part_read, pl.part_slots)
                    for a in range(2):
                        dve.memset(K2[a][HD:HD + 1, :], 1.0).then_inc(ones_made, 1)
                        dve.tensor_copy(next_v[:, a, :, 2 * HD], validc[:])
                    for k in range(pl.units + 2):
                        if 0 <= k - QK_UNITS < pl.v_units:
                            v_lo(0, k - QK_UNITS)
                        if 0 <= k - 2 < QK_UNITS:
                            turn(0, k - 2)
                        if 0 <= k - 1 < QK_UNITS:
                            cosines(0, k - 1)
                    for n in range(pl.block_parts):
                        part(0, 0, n // len(pl.parts), n % len(pl.parts))
                    max_column(0, 0)
                    for b_, qt, h in pl.parts_of(-2) + pl.parts_of(-1):
                        part(0, b_, qt, h)
                    for s in range(LAG):
                        slot(0, s, False)
                    body(pair, dve)

                for_key_count(dve, length, program)

            @block.gpsimd
            def _(pool):
                def program(pl):
                    def split_weights(pair, least=0):
                        need(pool, w_hi_made, pair, 1, 1, least)
                        pool.tensor_tensor(w_lo[:], w32[:], w_hi[:], ALU.subtract).then_inc(w_lo_made, 1)

                    def sines(pair, u, least=0):
                        kind, cols, n = pl.unit_block(u)
                        need(pool, swapped[u % 4], pair, 64 * 2, 64 * (u // 4 + 1), least)
                        need(pool, turn_done, pair, QK_UNITS, u, least)
                        pool.tensor_tensor(by_sin[:, 0:n], q32s[:, u % 4, 0:n], (ropeq, ropek)[kind][:, 1, cols], ALU.mult).then_inc(sin_done, 1)

                    def qk_lo(pair, u, least=0):
                        kind, cols, n = pl.unit_block(u)
                        need(pool, qk_hi_made, pair, QK_UNITS, u + 1, least)
                        pool.tensor_tensor(next_lo[kind][:, cols], turned[:, u % 2, 0:n], next_hi[kind][:, cols],
                                          ALU.subtract).then_inc(qk_lo_made, 1)

                    def low(p, s):
                        g = pl.gsize[s % pl.groups]
                        need(pool, exp_done, p, BLOCKS * pl.kt, pl.tiles_of(s)[-1][0] + 1 + 2)
                        pool.tensor_tensor(prob_lo[:, s % PRING, 0:g, :], prob[:, s % PRING, 0:g, :],
                                           hi_half(prob[:, s % PRING, 0:g, :])[:, :, 1::2], ALU.subtract).then_inc(lo_pool, 1)

                    def hooks(pair, k, least=0):
                        if 0 <= k - 2 < QK_UNITS:
                            qk_lo(pair, k - 2, least)
                        if 0 <= k - 1 < QK_UNITS:
                            sines(pair, k - 1, least)

                    def output(p, i):
                        need(pool, rden_made, p, BLOCKS, i + 1)
                        pool.tensor_tensor(o_sum[:], o_raw[:, i % 2, :, 0:HD], o_raw[:, i % 2, :, HD:2 * HD], ALU.add).then_inc(o_summed, 1)
                        need(pool, o_summed, p, BLOCKS, i + 1)
                        need(pool, o_stored[i % 2], p, 16 * BLOCKS // 2, 16 * (i // 2 + 1))
                        pool.tensor_tensor(o_out[:, i % 2, :, :], o_sum[:], rden[:, i % 2, :].unsqueeze(2).to_broadcast([P, QT, HD]),
                                           ALU.mult).then_inc(o_made, 1)

                    def slot(p, s, last):
                        i, m = divmod(s, pl.groups)
                        if m in pl.pool_groups and not (last and s >= BLOCKS * pl.groups):
                            low(p, s)
                        if m == 1 and s > pl.groups:
                            output(p, i - 1)

                    def pair(p, last):
                        for s in range(LAG, BLOCKS * pl.groups + LAG):
                            slot(p, s, last)
                            if not last:
                                if s == pl.groups - 1:
                                    split_weights(p + 1, 1)
                                for k in range(pl.units + 2):
                                    if s == pl.hook_slot(k):
                                        hooks(p + 1, k, 1)

                    pool.sem_inc(o_made, 2)
                    for k in range(QK_UNITS + 3):
                        if 0 <= k - 1 < QK_UNITS:
                            sines(0, k - 1)
                        if 0 <= k - 3 < QK_UNITS:
                            qk_lo(0, k - 3)
                    for s in range(LAG):
                        slot(0, s, False)
                    body(pair, pool)

                for_key_count(pool, length, program)

            @block.sync
            def _(sp):
                def program(pl):
                    def swap(pair, u, least=0):
                        kind, cols, n = pl.unit_block(u)
                        need(sp, pj_read_act, pair, QK_UNITS, u + 1, least)
                        for h in range(2):
                            for k in range(2):
                                a, z = HD * h + 32 * k, HD * h + 32 * (1 - k)
                                sp.dma_start(q32s[a:a + 32, u % 4, 0:n], q32[z:z + 32, u % 4, 0:n]).then_inc(swapped[u % 4], 16)

                    def load_q(pair, a):
                        need(sp, qk_lo_made, pair, QK_UNITS, 4, 0 if isinstance(pair, int) else 1)
                        r = slice(a * HD, (a + 1) * HD)
                        sp.dma_start(Q1[a][0:HD, :], next_hi[0][r, :]).then_inc(q_loaded[a], 16)
                        sp.dma_start(Q1[a][HD:P, :], next_hi[0][r, :]).then_inc(q_loaded[a], 16)
                        sp.dma_start(Q2[a][0:HD, :], next_lo[0][r, :]).then_inc(q_loaded[a], 16)

                    def load_k(pair, a):
                        need(sp, qk_lo_made, pair, QK_UNITS, 8, 0 if isinstance(pair, int) else 1)
                        n = pl.kt * P
                        r = slice(a * HD, (a + 1) * HD)
                        sp.dma_start(K1[a][0:HD, 0:n], next_hi[1][r, 0:n]).then_inc(k_loaded[a], 16)
                        sp.dma_start(K1[a][HD:P, 0:n], next_lo[1][r, 0:n]).then_inc(k_loaded[a], 16)
                        sp.dma_start(K2[a][0:HD, 0:n], next_hi[1][r, 0:n]).then_inc(k_loaded[a], 16)

                    def load_v(pair, a):
                        need(sp, v_lo_made, pair, pl.v_units, pl.v_units, 0 if isinstance(pair, int) else 1)
                        sp.dma_start(VV[a][:, 0:pl.kt, :], next_v[:, a, 0:pl.kt, :]).then_inc(v_loaded[a], 16)

                    def store(p, i):
                        a, c = set_of(i)
                        need(sp, o_made, p, BLOCKS, i + 1 + 2)
                        rows = o_dram[c * QC:(c + 1) * QC, :].rearrange("(t p) d -> p t d", p=P)
                        sp.dma_start(rows[:, :, bass.ds(p * P + a * HD, HD)], o_out[:, i % 2, :, :]).then_inc(o_stored[i % 2], 16)

                    def pair(p, last):
                        for s in range(LAG, BLOCKS * pl.groups + LAG):
                            if s % pl.groups == 1 and s > pl.groups:
                                store(p, s // pl.groups - 1)
                            if last:
                                continue
                            for u in range(QK_UNITS):
                                if s == pl.hook_slot(u):
                                    swap(p + 1, u, 1)
                            if s == pl.hook_slot(6) + 1:
                                load_q(p + 1, 0)
                            if s == pl.hook_slot(9) + 1:
                                load_k(p + 1, 0)
                            if s == pl.hook_slot(12) + 1:
                                load_v(p + 1, 0)
                        if not last:
                            load_q(p + 1, 1)
                            load_k(p + 1, 1)
                            load_v(p + 1, 1)

                    for i in range(2):
                        sp.sem_inc(o_stored[i], 16)
                    for u in range(QK_UNITS):
                        swap(0, u)
                    for a in range(2):
                        load_q(0, a)
                        load_k(0, a)
                    for a in range(2):
                        load_v(0, a)
                    body(pair, sp)
                    for i in range(2):
                        sp.wait_ge(o_stored[i], 16 + 16 * PAIRS * BLOCKS // 2)

                for_key_count(sp, length, program)


def experts(nc, sem, maker, have):
    x, gate, w_exp, o_dram, out, wo_hi, wo_lo, bob = (have[k] for k in (
        "x", "gate", "w_exp", "o_dram", "out", "wo_hi", "wo_lo", "bob"))
    ident, ident_b, eps_col, rank8, cst, x_slots, y_slots, zeroed = (have[k] for k in (
        "ident", "ident_b", "eps_col", "rank8", "cst", "x_slots", "y_slots", "zeroed"))
    with ExitStack() as both:
        sb, _ = maker(both)
        x1 = sb("x1", [P, ST, D])
        yrows = sb("yrows", [P, ST, 2 * D], BF16)
        we_hi = sb("we_hi", [P, E, WC], BF16)
        we_lo = sb("we_lo", [P, E, WC], BF16)
        logits = sb("logits", [P, ST, E])
        project_out(nc, sem, maker, locals())
        mixture(nc, sem, maker, locals())


def project_out(nc, sem, maker, have):
    x, gate, o_dram, ident, eps_col, x1, yrows, logits = (have[k] for k in (
        "x", "gate", "o_dram", "ident", "eps_col", "x1", "yrows", "logits"))
    w_exp, we_hi, we_lo = (have[k] for k in ("w_exp", "we_hi", "we_lo"))
    HALF = WC // 2
    wo_hi, wo_lo, bob = (have[k] for k in ("wo_hi", "wo_lo", "bob"))
    J = H * HD // P
    with ExitStack() as ctx:
        sb, pb = maker(ctx)
        o_in = sb("o_in", [P, 2, J * P])
        OH = sb("OH", [P, 2, J, P], BF16)
        OL = sb("OL", [P, 2, J, P], BF16)
        gate_sb = sb("gate_sb", [P, DT, E])
        stats = sb("stats2", [P, 2, 6])
        mv = sb("mv2", [P, 2, 2])
        std = sb("std2", [P, 2])
        rstd = sb("rstd2", [P, 2])
        normed = sb("normed2", [P, 2, D])
        WS = 3
        we32 = sb("we32", [P, WS, HALF])
        YF = sb("YF", [P, 2, DT, P])
        ot = [pb(f"ot{i}", [P, 2, 4, P]) for i in range(2)]
        wp = [pb(f"wp{i}", [P, 512]) for i in range(2)]
        yt = pb("yt", [P, 4, P])
        gp = pb("gp", [P, 512])

        o_loaded = [sem("o_loaded0"), sem("o_loaded1")]
        in_loaded = sem("in_loaded")
        bias_added = sem("bias_added")
        ot_ready, oh_made, ol_made = sem("ot_ready"), sem("oh_made"), sem("ol_made")
        wp_ready, x1_made, st_made, mv_made, sd_made, rs_made, nm_made = (sem(n) for n in (
            "wp_ready", "x1_made", "st_made", "mv_made", "sd_made", "rs_made", "nm_made"))
        yt_ready, yf_made, y_hi_made, y_lo_made, gp_ready, gp_read = (sem(n) for n in (
            "yt_ready", "yf_made", "y_hi_made", "y_lo_made", "gp_ready", "gp_read"))
        we_loaded = [sem(f"we_loaded{i}") for i in range(WS)]
        we_hi_made, we_lo_made = sem("we_hi_made"), sem("we_lo_made")

        def half(w, n):
            return w[:, n // 2, (n % 2) * HALF:(n % 2 + 1) * HALF]

        STEPS = ST + 5

        with nc.Block() as block:
            @block.sync
            def _(sp):
                for t in range(ST):
                    if t >= 2:
                        sp.wait_ge(ot_ready, t - 1)
                    sp.dma_start(o_in[:, t % 2, :], o_dram[t * P:(t + 1) * P, :]).then_inc(o_loaded[t % 2], 16)

            @block.scalar
            def _(act):
                act.dma_start(x1[:], x[0].rearrange("(t p) d -> p t d", p=P)).then_inc(in_loaded, 16)
                act.dma_start(gate_sb[:], gate).then_inc(in_loaded, 16)

                def load_half(n):
                    act.dma_start(we32[:, n % WS, :], w_exp[n // 2, :, (n % 2) * HALF:(n % 2 + 1) * HALF]).then_inc(we_loaded[n % WS], 16)

                load_half(0)
                load_half(1)
                for step in range(STEPS):
                    t = step
                    if t < ST:
                        act.wait_ge(ot_ready, t + 1)
                        if t >= 2:
                            act.wait_ge(wp_ready, t - 1)
                        act.activation(OH[:, t % 2, :, :], ot[t % 2][:].rearrange("p b k c -> p (b k) c"), ACT.Copy).then_inc(oh_made, 1)
                    t = step - 2
                    if 0 <= t < ST:
                        act.wait_ge(mv_made, t + 1)
                        act.activation(std[:, t % 2:t % 2 + 1], mv[:, t % 2, 1:2], ACT.Sqrt, bias=eps_col[:]).then_inc(sd_made, 1)
                    t = step - 4
                    if 0 <= t < ST:
                        act.wait_ge(yt_ready, t + 1)
                        if t >= 2:
                            act.wait_ge(gp_ready, t - 1)
                        act.activation(YF[:, t % 2, :, :], yt[:, 0:DT, :], ACT.Copy).then_inc(yf_made, 1)
                        act.activation(yrows[:, t, 0:D], normed[:, t % 2, :], ACT.Copy).then_inc(y_hi_made, 1)
                    n = step
                    if n < 2 * E:
                        act.wait_ge(we_loaded[n % WS], 16 * (n // WS + 1))
                        act.activation(half(we_hi, n), we32[:, n % WS, :], ACT.Copy).then_inc(we_hi_made, 1)
                        if n + 2 < 2 * E:
                            if n + 2 >= WS:
                                act.wait_ge(we_lo_made, n + 3 - WS)
                            load_half(n + 2)

            @block.gpsimd
            def _(pool):
                for step in range(STEPS):
                    n = step
                    if n < 2 * E:
                        pool.wait_ge(we_hi_made, n + 1)
                        pool.tensor_tensor(half(we_lo, n), we32[:, n % WS, :], half(we_hi, n), ALU.subtract).then_inc(we_lo_made, 1)
                    t = step - 4
                    if 0 <= t < ST:
                        pool.wait_ge(y_hi_made, t + 1)
                        pool.tensor_tensor(yrows[:, t, D:2 * D], normed[:, t % 2, :], yrows[:, t, 0:D], ALU.subtract).then_inc(y_lo_made, 1)

            @block.vector
            def _(dve):
                dve.wait_ge(in_loaded, 32)
                for step in range(STEPS):
                    t = step
                    if t < ST:
                        dve.tensor_tensor(x1[:, t, :], x1[:, t, :], bob[:], ALU.add).then_inc(bias_added, 1)
                    t = step - 2
                    if 0 <= t < ST:
                        dve.wait_ge(bias_added, t + 1)
                        dve.wait_ge(wp_ready, t + 1)
                        dve.tensor_tensor(x1[:, t, :], wp[t % 2][:, 0:D], x1[:, t, :], ALU.add).then_inc(x1_made, 1)
                        dve.wait_ge(x1_made, t + 1)
                        dve.bn_stats(stats[:, t % 2, :], x1[:, t, :]).then_inc(st_made, 1)
                        dve.wait_ge(st_made, t + 1)
                        dve.bn_aggr(mv[:, t % 2, :], stats[:, t % 2, :]).then_inc(mv_made, 1)
                    t = step
                    if t < ST:
                        dve.wait_ge(oh_made, t + 1)
                        dve.tensor_tensor(OL[:, t % 2, :, :], ot[t % 2][:].rearrange("p b k c -> p (b k) c"), OH[:, t % 2, :, :],
                                          ALU.subtract).then_inc(ol_made, 1)
                    t = step - 3
                    if 0 <= t < ST:
                        dve.wait_ge(sd_made, t + 1)
                        dve.reciprocal(rstd[:, t % 2:t % 2 + 1], std[:, t % 2:t % 2 + 1]).then_inc(rs_made, 1)
                        dve.wait_ge(rs_made, t + 1)
                        if t >= 2:
                            dve.wait_ge(yt_ready, t - 1)
                            dve.wait_ge(y_lo_made, t - 1)
                        dve.tensor_scalar(normed[:, t % 2, :], x1[:, t, :], mv[:, t % 2, 0:1], rstd[:, t % 2:t % 2 + 1],
                                          ALU.subtract, ALU.mult).then_inc(nm_made, 1)
                    t = step - 5
                    if 0 <= t < ST:
                        dve.wait_ge(gp_ready, t + 1)
                        dve.tensor_copy(logits[:, t, :], gp[:, 0:E]).then_inc(gp_read, 1)

            @block.tensor
            def _(pe):
                for step in range(STEPS):
                    t = step
                    if t < ST:
                        pe.wait_ge(o_loaded[t % 2], 16 * (t // 2 + 1))
                        if t >= 2:
                            pe.wait_ge(ol_made, t - 1)
                        for j in range(J):
                            ins = pe.transpose(ot[t % 2][:, j // 4, j % 4, :], o_in[:, t % 2, j * P:(j + 1) * P], ident)
                        ins.then_inc(ot_ready, 1)
                    t = step - 1
                    if 0 <= t < ST:
                        pe.wait_ge(ol_made, t + 1)
                        if t >= 2:
                            pe.wait_ge(x1_made, t - 1)
                        steps = [(z, w, j) for j in range(J) for z, w in ((OH, wo_hi), (OH, wo_lo), (OL, wo_hi))]
                        for n, (z, w, j) in enumerate(steps):
                            ins = pe.matmul(wp[t % 2][:, 0:D], z[:, t % 2, j, :], w[:, j, :], start=n == 0, stop=n == len(steps) - 1)
                        ins.then_inc(wp_ready, 1)
                    t = step - 4
                    if 0 <= t < ST:
                        pe.wait_ge(nm_made, t + 1)
                        if t >= 1:
                            pe.wait_ge(yf_made, t)
                        for d in range(DT):
                            ins = pe.transpose(yt[:, d, :], normed[:, t % 2, d * P:(d + 1) * P], ident)
                        ins.then_inc(yt_ready, 1)
                    t = step - 5
                    if 0 <= t < ST:
                        pe.wait_ge(yf_made, t + 1)
                        if t >= 1:
                            pe.wait_ge(gp_read, t)
                        for d in range(DT):
                            ins = pe.matmul(gp[:, 0:E], YF[:, t % 2, d, :], gate_sb[:, d, :], start=d == 0, stop=d == DT - 1)
                        ins.then_inc(gp_ready, 1)


def mixture(nc, sem, maker, have):
    out, x1, yrows, we_hi, we_lo, logits = (have[k] for k in ("out", "x1", "yrows", "we_hi", "we_lo", "logits"))
    cst, rank8, ident_b, x_slots, y_slots, zeroed = (have[k] for k in ("cst", "rank8", "ident_b", "x_slots", "y_slots", "zeroed"))
    at = P + KT + E
    rows_before = cst[:, at:at + P]
    experts_before = cst[:, at + P:at + P + E * E]
    multiples = cst[:, at + P + E * E:at + P + E * E + ST]
    tile_numbers = cst[:, at + P + E * E + ST:at + P + E * E + ST + MT]
    W3, W2 = DT * FF, 2 * DT * FF
    TURN = 6
    TURNS = (MT - 2) // TURN
    with ExitStack() as ctx:
        sb, pb = maker(ctx)
        g8 = [sb(f"g8_{i}", [P, ST, E]) for i in range(3)]
        pick = [sb(f"pick{i}", [P, ST, E]) for i in range(2)]
        top = sb("top", [P, 4, ST])
        ew = sb("ew", [P, 4, ST])
        chosen = sb("chosen", [P, ST, E], BF16)
        before_b = sb("before_b", [P, P], BF16)
        ones_b = sb("ones_b", [P, P], BF16)
        count = sb("count", [P, E])
        filled = sb("filled", [P, E, ST])
        tiles = sb("tiles", [P, 4, E])
        tri = sb("tri", [P, E, E])
        slot_of = sb("slot_of", [P, ST, E])
        slot_f = sb("slot_f", [P, 4, ST])
        slot = sb("slot", [P, 2, ST], U32)
        first_low = sb("first_low", [P, 2, ST])
        ew_part = sb("ew_part", [P, 4, ST])
        ew_by = sb("ew_by", [P, 2, ST])
        ended = sb("ended", [1, MT, E])
        owner_f = sb("owner_f", [1, 2, MT])
        owner = sb("owner", [1, MT], I32)
        scatter_f = sb("scatter_f", [1, 2, MT])
        scatters = sb("scatters", [1, MT], I32)
        below_f = sb("below_f", [1, 2, MT])
        stores_f = sb("stores_f", [1, 2, 4])
        stores = sb("stores", [1, 4], I32)
        x_in = sb("x_in", [P, 2, 2 * D], BF16)
        xT = sb("xT", [P, 2, 2, DT, P], BF16)
        act_s = sb("act_s", [P, 2, FF])
        hid = sb("hid", [P, 2, FF])
        hid_lo = sb("hid_lo", [P, 2, FF], BF16)
        hT = sb("hT", [P, 2, 2, FT, P], BF16)
        y_out = sb("y_out", [P, 2, D])
        y_low = yrows[:].rearrange("p t c -> p (t c)").bitcast(F32).rearrange("p (t d) -> p t d", d=D)
        y_high = sb("y_high", [P, ST, D])
        p1 = pb("p1", [P, FF])
        p3 = pb("p3", [P, FF])
        pxt = pb("pxt", [P, 2, DT, P], BF16)
        pht = [pb(f"pht{i}", [P, 2, FT, P], BF16) for i in range(2)]
        py = [pb(f"py{i}", [P, 512]) for i in range(2)]
        pc = pb("pc", [P, 512])

        routed, picked, exp_made, chosen_made, counted, slots_made, owner_made = (sem(n) for n in (
            "routed", "picked", "exp_made", "chosen_made", "counted", "slots_made", "owner_made"))
        scattered_low, scattered_high = sem("scattered_low"), sem("scattered_high")
        rows_placed = sem("rows_placed")
        load_turn = sem("load_turn")
        x_tile = [sem("x_tile0"), sem("x_tile1")]
        xt_ready, xt_made = sem("xt_ready"), sem("xt_made")
        up1_ready, up3_ready = sem("up1_ready"), sem("up3_ready")
        silu_made = sem("silu_made")
        hid_made = sem("hid_made")
        hid_lo_made = sem("hid_lo_made")
        ht_ready = sem("ht_ready")
        ht_hi_made, ht_lo_made = sem("ht_hi_made"), sem("ht_lo_made")
        down_ready = sem("down_ready")
        y_made = sem("y_made")
        y_stored = [sem("y_stored0"), sem("y_stored1")]
        low_gathered = sem("low_gathered")
        high_gathered = [sem(f"high_gathered{c}") for c in range(CH)]
        stores_seen = sem("stores_seen")
        weighted = sem("weighted")
        stored = sem("stored")

        def body(program, engine):
            with engine.Fori(0, TURNS) as q:
                program(q, range(1, TURN + 1), False)
            program(TURNS, range(1, MT - TURNS * TURN), True)

        with nc.Block() as block:
            @block.sync
            def _(sp):
                def load(i, q=0):
                    if not isinstance(q, int) or i >= 2:
                        need(sp, xt_ready, q, TURN, i - 1)
                    sp.sem_inc(load_turn, 1)
                    sp.wait_ge(rows_placed, sp.value_load(scatters[0:1, bass.ds(q * TURN + i, 1)], min_val=1, max_val=2))
                    sp.dma_start(x_in[:, i % 2, :], x_slots[bass.ds((q * TURN + i) * P, P), :]).then_inc(x_tile[i % 2], 16)

                def store(i, q=0):
                    need(sp, y_made, q, TURN, i + 1 + 2)
                    sp.dma_start(y_slots[bass.ds((q * TURN + i) * P, P), :], y_out[:, i % 2, :]).then_inc(y_stored[i % 2], 16)

                def turn(q, tiles_, last):
                    for j in tiles_:
                        if not last or j + 2 < tiles_.stop:
                            load(j + 2, q)
                        store(j - 1, q)

                for i in range(2):
                    sp.sem_inc(y_stored[i], 16)
                sp.wait_ge(owner_made, 1)
                sp.wait_ge(scattered_low, 16 * ST)
                load(0)
                load(1)
                load(2)
                body(turn, sp)
                store(MT - 1)
                for c in range(CH):
                    sp.wait_ge(weighted, ST + QT * (c + 1))
                    sp.dma_start(out[0, c * QC:(c + 1) * QC, :].rearrange("(t p) d -> p t d", p=P),
                                 x1[:, c * QT:(c + 1) * QT, :]).then_inc(stored, 16)
                sp.wait_ge(stored, 16 * CH)

            @block.scalar
            def _(act):
                def silu(i, q=0):
                    need(act, up1_ready, q, TURN, i + 1)
                    need(act, hid_made, q, TURN, i)
                    act.activation(act_s[:, i % 2, :], p1[:], ACT.Silu).then_inc(silu_made, 1)

                def results(i, q=0):
                    need(act, ht_ready, q, TURN, i + 1)
                    need(act, down_ready, q, TURN, i + 1)
                    act.activation(hT[:, i % 2, 0, :, :], pht[0][:, 0, :, :], ACT.Copy).then_inc(ht_hi_made, 1)
                    need(act, down_ready, q, TURN, i + 1 + 2)
                    need(act, y_stored[i % 2], q, 8 * TURN, 16 * (i // 2) + 16)
                    act.activation(y_out[:, i % 2, :], py[i % 2][:, 0:D], ACT.Copy).then_inc(y_made, 1)

                def turn(q, tiles_, last):
                    for j in tiles_:
                        silu(j, q)
                        results(j - 1, q)

                act.sem_inc(y_made, 2)
                act.sem_inc(ht_hi_made, 1)
                act.wait_ge(routed, 1)
                act.activation(ew[:, 0, :], top[:, 2, :], ACT.Exp).then_inc(exp_made, 1)
                silu(0)
                body(turn, act)
                results(MT - 1)

            @block.gpsimd
            def _(pool):
                def gather(into, k, t, done):
                    pool.indirect_dma_start(into[:, t, :], None, y_slots,
                                            bass.IndirectOffsetOnAxis(slot[:, k, t:t + 1], 0)).then_inc(done, 16)

                def wait_stores(k):
                    for i in range(2):
                        at = 2 * k + i
                        count = pool.value_load(stores[0:1, at:at + 1], min_val=16, max_val=16 * MT)
                        pool.wait_ge(y_stored[i], count)
                        pool.sem_inc(stores_seen, 1)

                pool.sem_inc(rows_placed, 1)
                pool.wait_ge(zeroed, 32)
                pool.wait_ge(slots_made, 1)
                for k in range(2):
                    for t in range(ST):
                        pool.indirect_dma_start(x_slots, bass.IndirectOffsetOnAxis(slot[:, k, t:t + 1], 0),
                                                yrows[:, t, :], None).then_inc((scattered_low, scattered_high)[k], 16)
                pool.wait_ge(scattered_high, 16 * ST)
                pool.sem_inc(rows_placed, 1)
                pool.wait_ge(owner_made, 1)
                pool.wait_ge(scattered_low, 16 * ST)
                wait_stores(0)
                for t in range(ST):
                    gather(y_low, 0, t, low_gathered)
                wait_stores(1)
                for t in range(ST):
                    gather(y_high, 1, t, high_gathered[t // QT])

            @block.vector
            def _(dve):
                chain = [0]

                def then(ins):
                    chain[0] += 1
                    ins.then_inc(picked, 1)
                    dve.wait_ge(picked, chain[0])

                def choose():
                    ranks = rank8.unsqueeze(1).to_broadcast([P, ST, E])
                    left = logits
                    for k in range(2):
                        def wide(row):
                            return top[:, row, :].unsqueeze(2).to_broadcast([P, ST, E])
                        then(dve.tensor_reduce(top[:, k, :], left[:], AX_X, ALU.max))
                        then(dve.tensor_tensor(g8[0][:], left[:], wide(k), ALU.is_ge))
                        then(dve.tensor_tensor(g8[1][:], g8[0][:], ranks, ALU.mult))
                        then(dve.tensor_reduce(top[:, 3, :], g8[1][:], AX_X, ALU.max))
                        then(dve.tensor_tensor(pick[k][:], g8[1][:], wide(3), ALU.is_equal))
                        if k == 0:
                            then(dve.scalar_tensor_tensor(out=g8[2][:], in0=pick[0][:], scalar=-3e38, in1=logits[:],
                                                          op0=ALU.mult, op1=ALU.add))
                            left = g8[2]
                    dve.tensor_tensor(chosen[:], pick[0][:], pick[1][:], ALU.add).then_inc(chosen_made, 1)
                    dve.tensor_tensor(top[:, 2, :], top[:, 1, :], top[:, 0, :], ALU.subtract).then_inc(routed, 1)

                def place():
                    dve.wait_ge(counted, 1)
                    then(dve.tensor_copy(count[:], py[0][:, 0:E]))
                    then(dve.tensor_tensor(filled[:], count[:].unsqueeze(2).to_broadcast([P, E, ST]),
                                           multiples.unsqueeze(1).to_broadcast([P, E, ST]), ALU.is_gt))
                    then(dve.tensor_reduce(tiles[:, 0, :], filled[:], AX_X, ALU.add))
                    then(dve.tensor_tensor(tri[:], tiles[:, 0, :].unsqueeze(1).to_broadcast([P, E, E]),
                                           experts_before.rearrange("p (a b) -> p a b", b=E), ALU.mult))
                    then(dve.tensor_reduce(tiles[:, 1, :], tri[:], AX_X, ALU.add))
                    then(dve.tensor_scalar(tiles[:, 3, :], tiles[:, 1, :], float(P), None, ALU.mult))
                    then(dve.tensor_tensor(slot_of[:], pc[:, 0:ST * E].rearrange("p (t e) -> p t e", e=E),
                                           tiles[:, 3, :].unsqueeze(1).to_broadcast([P, ST, E]), ALU.add))
                    for k in range(2):
                        then(dve.tensor_tensor(g8[k][:], slot_of[:], pick[k][:], ALU.mult))
                        then(dve.tensor_reduce(slot_f[:, k, :], g8[k][:], AX_X, ALU.add))
                    then(dve.tensor_tensor(slot_f[:, 2, :], slot_f[:, 0, :], slot_f[:, 1, :], ALU.min))
                    then(dve.tensor_tensor(slot_f[:, 3, :], slot_f[:, 0, :], slot_f[:, 1, :], ALU.max))
                    dve.tensor_copy(slot[:], slot_f[:, 2:4, :]).then_inc(slots_made, 1)
                    then(dve.tensor_tensor(tiles[:, 2, :], tiles[:, 1, :], tiles[:, 0, :], ALU.add))
                    then(dve.tensor_tensor(ended[:], tile_numbers[0:1, :].unsqueeze(2).to_broadcast([1, MT, E]),
                                           tiles[0:1, 2, :].unsqueeze(1).to_broadcast([1, MT, E]), ALU.is_ge))
                    then(dve.tensor_reduce(owner_f[:, 0, :], ended[:], AX_X, ALU.add))
                    then(dve.tensor_scalar(owner_f[:, 1, :], owner_f[:, 0, :], float(E - 1), None, ALU.min))
                    then(dve.tensor_copy(owner[:], owner_f[:, 1, :]))
                    then(dve.tensor_scalar(scatter_f[:, 0, :], tile_numbers[0:1, :], tiles[0:1, 2, 0:1], None, ALU.is_ge))
                    then(dve.tensor_scalar(scatter_f[:, 1, :], scatter_f[:, 0, :], 1.0, None, ALU.add))
                    then(dve.tensor_copy(scatters[:], scatter_f[:, 1, :]))
                    for k in range(2):
                        then(dve.tensor_scalar(below_f[:, k, :], tile_numbers[0:1, :], tiles[0:1, 2, E - 2 + k:E - 1 + k], None,
                                               ALU.is_lt))
                        for i in range(2):
                            at = 2 * k + i
                            then(dve.tensor_reduce(stores_f[:, 0, at:at + 1], below_f[:, k, i::2], AX_X, ALU.add))
                    then(dve.tensor_scalar(stores_f[:, 1, :], stores_f[:, 0, :], 16.0, 16.0, ALU.mult, ALU.add))
                    dve.tensor_copy(stores[:], stores_f[:, 1, :]).then_inc(owner_made, 1)

                def weights():
                    dve.wait_ge(exp_made, 1)
                    then(dve.tensor_scalar(ew[:, 1, :], ew[:, 0, :], 1.0, None, ALU.add))
                    then(dve.reciprocal(ew[:, 2, :], ew[:, 1, :]))
                    then(dve.tensor_tensor(ew[:, 3, :], ew[:, 0, :], ew[:, 2, :], ALU.mult))
                    then(dve.tensor_tensor(first_low[:, 0, :], slot_f[:, 0, :], slot_f[:, 1, :], ALU.is_lt))
                    then(dve.tensor_tensor(first_low[:, 1, :], slot_f[:, 0, :], slot_f[:, 1, :], ALU.is_gt))
                    for k in range(2):
                        for m in range(2):
                            then(dve.tensor_tensor(ew_part[:, 2 * k + m, :], ew[:, 2 + m, :], first_low[:, (k + m) % 2, :], ALU.mult))
                        then(dve.tensor_tensor(ew_by[:, k, :], ew_part[:, 2 * k, :], ew_part[:, 2 * k + 1, :], ALU.add))

                def turn_x(i, q=0):
                    need(dve, xt_ready, q, TURN, i + 1)
                    dve.tensor_copy(xT[:, i % 2, :, :, :], pxt[:]).then_inc(xt_made, 1)

                def hidden(i, q=0):
                    need(dve, silu_made, q, TURN, i + 1)
                    need(dve, up3_ready, q, TURN, i + 1)
                    dve.tensor_tensor(hid[:, i % 2, :], act_s[:, i % 2, :], p3[:], ALU.mult).then_inc(hid_made, 1)

                def low(i, q=0):
                    need(dve, hid_made, q, TURN, i + 1 + 1)
                    dve.tensor_tensor(hid_lo[:, i % 2, :], hid[:, i % 2, :], hi_half(hid[:, i % 2, :])[:, 1::2],
                                      ALU.subtract).then_inc(hid_lo_made, 1)

                def turn_low(i, q=0):
                    need(dve, ht_ready, q, TURN, i + 1)
                    need(dve, down_ready, q, TURN, i + 1)
                    dve.tensor_copy(hT[:, i % 2, 1, :, :], pht[1][:, 0, :, :]).then_inc(ht_lo_made, 1)

                def turn(q, tiles_, last):
                    for j in tiles_:
                        turn_low(j - 1, q)
                        hidden(j, q)
                        if not last or j + 1 < tiles_.stop:
                            turn_x(j + 1, q)
                        low(j, q)

                dve.sem_inc(hid_made, 1)
                dve.sem_inc(ht_lo_made, 1)
                dve.tensor_copy(before_b[:], rows_before)
                dve.memset(ones_b[:], 1.0)
                choose()
                place()
                weights()
                turn_x(0)
                hidden(0)
                turn_x(1)
                low(0)
                body(turn, dve)
                turn_low(MT - 1)
                dve.wait_ge(low_gathered, 16 * ST)
                for k, y in enumerate((y_low, y_high)):
                    for t in range(ST):
                        if k == 1:
                            dve.wait_ge(weighted, t + 1)
                            if t % QT == 0:
                                dve.wait_ge(high_gathered[t // QT], 16 * QT)
                        dve.scalar_tensor_tensor(out=x1[:, t, :], in0=y[:, t, :], scalar=ew_by[:, k, t:t + 1],
                                                 in1=x1[:, t, :], op0=ALU.mult, op1=ALU.add).then_inc(weighted, 1)

            @block.tensor
            def _(pe):
                def turn_x(i, q=0):
                    need(pe, x_tile[i % 2], q, 8 * TURN, 16 * (i // 2 + 1))
                    need(pe, xt_made, q, TURN, i)
                    for h in range(2):
                        for d in range(DT):
                            ins = pe.transpose(pxt[:, h, d, :], x_in[:, i % 2, (h * DT + d) * P:(h * DT + d + 1) * P], ident_b[:])
                    ins.then_inc(xt_ready, 1)

                def up(expert, which, i, q=0):
                    need(pe, xt_made, q, TURN, i + 1)
                    if which == 0:
                        need(pe, silu_made, q, TURN, i)
                    else:
                        need(pe, hid_made, q, TURN, i + 1)
                    steps = [(h, w, d) for d in range(DT) for h, w in ((0, we_hi), (0, we_lo), (1, we_hi))]
                    for n, (h, w, d) in enumerate(steps):
                        at = which * W3 + d * FF
                        ins = pe.matmul((p1, p3)[which][:], xT[:, i % 2, h, d, :],
                                        w[:, bass.ds(expert, 1), at:at + FF].rearrange("p a c -> p (a c)"),
                                        start=n == 0, stop=n == len(steps) - 1)
                    ins.then_inc((up1_ready, up3_ready)[which], 1)

                def turn_hidden(i, q=0):
                    need(pe, hid_lo_made, q, TURN, i + 1)
                    need(pe, ht_hi_made, q, TURN, i + 1)
                    need(pe, ht_lo_made, q, TURN, i + 1)
                    for f in range(FT):
                        pe.transpose(pht[0][:, 0, f, :], hi_half(hid[:, i % 2, :])[:, 2 * f * P + 1:2 * (f + 1) * P:2], ident_b[:])
                    for f in range(FT):
                        ins = pe.transpose(pht[1][:, 0, f, :], hid_lo[:, i % 2, f * P:(f + 1) * P], ident_b[:])
                    ins.then_inc(ht_ready, 1)

                def down(expert, i, q=0):
                    need(pe, ht_hi_made, q, TURN, i + 1 + 1)
                    need(pe, ht_lo_made, q, TURN, i + 1 + 1)
                    need(pe, y_made, q, TURN, i + 1)
                    for f in range(FT):
                        for n, (h, w) in enumerate(((0, we_hi), (0, we_lo), (1, we_hi))):
                            at = W2 + f * D
                            ins = pe.matmul(py[i % 2][:, 0:D], hT[:, i % 2, h, f, :],
                                            w[:, bass.ds(expert, 1), at:at + D].rearrange("p a c -> p (a c)"),
                                            start=f == 0 and n == 0, stop=f == FT - 1 and n == 2)
                    ins.then_inc(down_ready, 1)

                def turn(q, tiles_, last):
                    def owner_of(j):
                        return pe.value_load(owner[0:1, bass.ds(q * TURN + j, 1)], min_val=0, max_val=E - 1)

                    before, mine = owner_of(0), owner_of(1)
                    for j in tiles_:
                        up(mine, 0, j, q)
                        turn_hidden(j - 1, q)
                        up(mine, 1, j, q)
                        if not last or j + 1 < tiles_.stop:
                            turn_x(j + 1, q)
                        down(before, j - 1, q)
                        if j + 1 < tiles_.stop:
                            before, mine = mine, owner_of(j + 1)

                pe.sem_inc(down_ready, 2)
                pe.wait_ge(chosen_made, 1)
                pe.matmul(pc[:, 0:ST * E], before_b[:], chosen[:].rearrange("p t e -> p (t e)"), start=True, stop=False)
                for t in range(ST - 1):
                    pe.matmul(pc[:, (t + 1) * E:ST * E], ones_b[:], chosen[:, t:t + 1, :].to_broadcast([P, ST - 1 - t, E]),
                              start=False, stop=t == ST - 2)
                for t in range(ST):
                    ins = pe.matmul(py[0][:, 0:E], ones_b[:], chosen[:, t, :], start=t == 0, stop=t == ST - 1)
                ins.then_inc(counted, 1)
                pe.wait_ge(owner_made, 1)
                first = pe.value_load(owner[0:1, 0:1], min_val=0, max_val=E - 1)
                turn_x(0)
                up(first, 0, 0)
                up(first, 1, 0)
                turn_x(1)
                body(turn, pe)
                turn_hidden(MT - 1)
                down(pe.value_load(owner[0:1, MT - 1:MT], min_val=0, max_val=E - 1), MT - 1)


_INS = ["x", "ctx_1024", "_lenS2", "L0_xattn_ln_g", "L0_xattn_ln_b", "w_pairs", "b_pairs", "bv_cols", "L0_xattn_Wo",
        "L0_xattn_bo", "gate", "w_exp", "rope", "keypos", "consts"]


def kernel(**inputs):
    import numpy as np
    import concourse.bacc as bacc
    from concourse.bass_utils import run_bass_kernel_spmd

    a = {k: np.asarray(v) for k, v in inputs.items()}
    order = np.concatenate([np.arange(0, HD, 2), np.arange(1, HD, 2)])
    cols = (np.arange(H)[:, None] * HD + order[None, :]).reshape(-1)

    def by_pair(w):
        return w.reshape(DT, P, PAIRS, P).transpose(2, 1, 0, 3)

    a["w_pairs"] = np.stack([by_pair(a["L0_xattn_Wq"][:, cols]), by_pair(a["L0_xattn_Wk"][:, cols]),
                             by_pair(a["L0_xattn_Wv"])], axis=2)
    a["b_pairs"] = np.stack([a["L0_xattn_bq"][cols].reshape(PAIRS, P), a["L0_xattn_bk"][cols].reshape(PAIRS, P)], axis=2)
    a["bv_cols"] = a["L0_xattn_bv"].reshape(PAIRS, P).T
    a["gate"] = a["L0_ffn_gate_w"].T.reshape(DT, P, E).transpose(1, 0, 2)

    def by_rows(w):
        return w.reshape(E, -1, P, w.shape[2]).transpose(0, 2, 1, 3).reshape(E, P, -1)

    a["w_exp"] = np.concatenate([by_rows(a["L0_ffn_w1"].transpose(0, 2, 1)), by_rows(a["L0_ffn_w3"].transpose(0, 2, 1)),
                                 by_rows(a["L0_ffn_w2"].transpose(0, 2, 1))], axis=2)
    inv = (np.float32(1) / np.power(10000.0, np.arange(0, HD, 2) / HD)).astype(np.float32)
    angle = (np.arange(S, dtype=np.float32)[None, :] * inv[:, None]).astype(np.float64)
    a["rope"] = np.stack([np.tile(np.cos(angle), (4, 1)),
                          np.tile(np.concatenate([-np.sin(angle), np.sin(angle)]), (2, 1))]).astype(np.float32)
    key = np.arange(LP, dtype=np.float32)
    key[L:] = 1e9
    a["keypos"] = key
    a["consts"] = np.concatenate([np.eye(P, dtype=np.float32), key.reshape(KT, P).T,
                                  np.tile(np.arange(E, 0, -1, dtype=np.float32), (P, 1)),
                                  np.triu(np.ones((P, P), np.float32), 1),
                                  np.tile(np.tril(np.ones((E, E), np.float32), -1).reshape(-1), (P, 1)),
                                  np.tile(P * np.arange(ST, dtype=np.float32), (P, 1)),
                                  np.tile(np.arange(MT, dtype=np.float32), (P, 1))], axis=1)

    nc = bacc.Bacc("TRN2", target_bir_lowering=False, num_devices=1)
    arrays, args = {}, []
    for name in _INS:
        v = np.ascontiguousarray(a[name])
        arrays[f"in_{name}"] = v
        args.append(nc.dram_tensor(f"in_{name}", v.shape, mybir.dt.from_np(v.dtype), kind="ExternalInput").ap())
    out = nc.dram_tensor("out", [1, S, D], F32, kind="ExternalOutput").ap()
    build(nc, *args, out)
    r = run_bass_kernel_spmd(nc, [arrays], core_ids=[0])
    return r.results[0]["out"]
```
